# Optimizing a Trainium2 kernel written in Bass

```python
import numpy as np
import jax
import jax.numpy as jnp

def _softmax(x, axis=-1):
    return jax.nn.softmax(x, axis=axis)

def _gelu(x):
    return jax.nn.gelu(x, approximate=True)

def _silu(x):
    return jax.nn.silu(x)

def _sigmoid(x):
    return jax.nn.sigmoid(x)

def _layernorm(x, axis=-1, eps=1e-05):
    m = jnp.mean(x, axis=axis, keepdims=True)
    v = jnp.var(x, axis=axis, keepdims=True)
    return (x - m) / jnp.sqrt(v + eps)

def _scatter_add(tgt, idx, src, axis=0):
    return tgt.at[idx].add(src)

def _segment_sum(src, seg, n):
    return jax.ops.segment_sum(src, seg, n)
kernel_name = 'mk_gnn_preln_d4_gnn_r32_b2fad2'

def setup_inputs(seed: int=0):
    np.random.seed(seed)
    _w = jnp.asarray

    def _rec_inputs():
        import jax
        import jax.numpy as jnp
        _gk = jax.random.key(seed)
        x = -0.000202 + 1 * jax.random.normal(jax.random.fold_in(_gk, 1), (3125, 128), jnp.float32)
        src = jax.random.randint(jax.random.fold_in(_gk, 2), (50000,), 0, 3125, jnp.int32)
        dst = jax.random.randint(jax.random.fold_in(_gk, 3), (50000,), 0, 3125, jnp.int32)
        _o = jnp.argsort(dst, stable=True)
        src = src[_o]
        dst = dst[_o]
        edge_attr_16 = 0.000254156 + 0.999948 * jax.random.normal(jax.random.fold_in(_gk, 13), (50000, 16), jnp.float32)
        edge_type_500 = jax.random.randint(jax.random.fold_in(_gk, 15), (50000,), 0, 500, jnp.int32)
        return (x, src, dst, edge_attr_16, edge_type_500)
    x, src, dst, edge_attr_16, edge_type_500 = _rec_inputs()

    def _L0_gnn_setup():
        import jax, jax.numpy as jnp
        import numpy as np
        N, E, D_IN, D_H, D_E, L = (50000, 25000, 128, 128, 16, 3)
        LN_EPS = 1e-05
        key = jax.random.key(seed)
        ks = jax.random.split(key, 8)
        x = jax.random.normal(ks[0], (N, D_IN), jnp.float32)
        edge_index = jax.random.randint(ks[1], (2, E), 0, N, jnp.int32)
        edge_attr = jax.random.normal(ks[2], (E, D_E), jnp.float32)
        s = lambda d: 1.0 / np.sqrt(d)
        lin_w = jax.random.normal(ks[3], (L, D_IN, D_H), jnp.float32) * s(D_IN)
        edge_w1 = jax.random.normal(ks[4], (L, D_E, D_H), jnp.float32) * s(D_E)
        edge_b1 = jnp.zeros((L, D_H), jnp.float32)
        edge_w2 = jax.random.normal(ks[5], (L, D_H, D_H), jnp.float32) * s(D_H)
        edge_b2 = jnp.zeros((L, D_H), jnp.float32)
        bias = jnp.zeros((L, D_H), jnp.float32)
        ln_w = jnp.ones((L, D_H), jnp.float32)
        ln_b = jnp.zeros((L, D_H), jnp.float32)
        return dict(x=x, edge_attr=edge_attr, lin_w=lin_w, edge_w1=edge_w1, edge_b1=edge_b1, edge_w2=edge_w2, edge_b2=edge_b2, bias=bias, ln_w=ln_w, ln_b=ln_b, edge_index=edge_index)
    _L0_gnn_all = _L0_gnn_setup()
    _L0_gnn_in = {k: v for k, v in _L0_gnn_all.items() if k in ('lin_w', 'edge_w1', 'edge_b1', 'edge_w2', 'edge_b2', 'bias', 'ln_w', 'ln_b')}
    del _L0_gnn_all

    def _L1_gnn_setup():
        import jax, jax.numpy as jnp
        import numpy as np
        N_NODES = 50000
        N_EDGES = 18750
        D = 128
        D_OUT = 128
        key = jax.random.key(seed)
        ks = jax.random.split(key, 6)
        features = jax.random.normal(ks[0], (N_NODES, D), dtype=jnp.float32)
        edge_index = jax.random.randint(ks[1], (2, N_EDGES), 0, N_NODES, dtype=jnp.int64)

        def xavier(k, shape):
            gain = float(np.sqrt(2.0))
            fan_out, fan_in = shape
            bound = gain * float(np.sqrt(6.0 / (fan_in + fan_out)))
            return jax.random.uniform(k, shape, jnp.float32, -bound, bound)
        W_neigh = xavier(ks[2], (D, D))
        b_neigh = jnp.zeros((D,), jnp.float32)
        W_edge = xavier(ks[3], (D, 2 * D))
        b_edge = jnp.zeros((D,), jnp.float32)
        W_lin = xavier(ks[4], (D_OUT, 2 * D))
        b_lin = jnp.zeros((D_OUT,), jnp.float32)
        return {'features': features, 'edge_index': edge_index, 'W_neigh': W_neigh, 'b_neigh': b_neigh, 'W_edge': W_edge, 'b_edge': b_edge, 'W_lin': W_lin, 'b_lin': b_lin}
    _L1_gnn_all = _L1_gnn_setup()
    _L1_gnn_in = {k: v for k, v in _L1_gnn_all.items() if k in ('W_neigh', 'b_neigh', 'W_edge', 'b_edge', 'W_lin', 'b_lin')}
    del _L1_gnn_all

    def _L2_gnn_setup():
        import jax, jax.numpy as jnp
        import numpy as np
        N_NODES = 3125
        N_EDGES = 18750
        D = 128
        EPS = 1e-05

        def _linear_params(key, d_in, d_out):
            kw, kb = jax.random.split(key)
            bound = 1.0 / np.sqrt(d_in)
            w = jax.random.uniform(kw, (d_in, d_out), minval=-bound, maxval=bound, dtype=jnp.float32)
            b = jax.random.uniform(kb, (d_out,), minval=-bound, maxval=bound, dtype=jnp.float32)
            return (w, b)

        def _layernorm(h, gamma, beta):
            mu = jnp.mean(h, axis=-1, keepdims=True)
            var = jnp.mean(jnp.square(h - mu), axis=-1, keepdims=True)
            return (h - mu) * jax.lax.rsqrt(var + EPS) * gamma + beta
        key = jax.random.key(seed)
        ks = jax.random.split(key, 6)
        x = jax.random.normal(ks[0], (N_NODES, D), dtype=jnp.float32)
        edge_index = jax.random.randint(ks[1], (2, N_EDGES), 0, N_NODES, dtype=jnp.int32)
        w_m1, b_m1 = _linear_params(ks[2], 2 * D, D)
        w_m2, b_m2 = _linear_params(ks[3], D, D)
        w_u1, b_u1 = _linear_params(ks[4], 2 * D, D)
        w_u2, b_u2 = _linear_params(ks[5], D, D)
        gamma = jnp.ones((D,), dtype=jnp.float32)
        beta = jnp.zeros((D,), dtype=jnp.float32)
        return {'x': x, 'edge_index': edge_index, 'w_m1': w_m1, 'b_m1': b_m1, 'w_m2': w_m2, 'b_m2': b_m2, 'w_u1': w_u1, 'b_u1': b_u1, 'w_u2': w_u2, 'b_u2': b_u2, 'gamma': gamma, 'beta': beta}
    _L2_gnn_all = _L2_gnn_setup()
    _L2_gnn_in = {k: v for k, v in _L2_gnn_all.items() if k in ('w_m1', 'b_m1', 'w_m2', 'b_m2', 'w_u1', 'b_u1', 'w_u2', 'b_u2', 'gamma', 'beta')}
    del _L2_gnn_all

    def _L3_gnn_setup():
        import jax, jax.numpy as jnp
        import numpy as np
        N_NODES = 50000
        N_EDGES = 18750
        N_RELS = 500
        D = 128
        key = jax.random.key(seed)
        ks = jax.random.split(key, 8)
        h = jax.random.normal(ks[0], (N_NODES, D), dtype=jnp.float32)
        norm = jax.random.uniform(ks[1], (N_NODES, 1), dtype=jnp.float32)
        rel_emb = jax.random.normal(ks[2], (N_RELS, D), dtype=jnp.float32)
        lim = np.sqrt(6.0 / (D + D)) * np.sqrt(2.0)
        W_neighbor = jax.random.uniform(ks[3], (D, D), dtype=jnp.float32, minval=-lim, maxval=lim)
        loop_weight = jax.random.uniform(ks[4], (D, D), dtype=jnp.float32, minval=-lim, maxval=lim)
        edge_src = jax.random.randint(ks[5], (N_EDGES,), 0, N_NODES, dtype=jnp.int64 if jax.config.jax_enable_x64 else jnp.int32)
        edge_dst = jax.random.randint(ks[6], (N_EDGES,), 0, N_NODES, dtype=edge_src.dtype)
        edge_type = jax.random.randint(ks[7], (N_EDGES,), 0, N_RELS, dtype=edge_src.dtype)
        return {'h': h, 'norm': norm, 'rel_emb': rel_emb, 'W_neighbor': W_neighbor, 'loop_weight': loop_weight, 'edge_src': edge_src, 'edge_dst': edge_dst, 'edge_type': edge_type}
    _L3_gnn_all = _L3_gnn_setup()
    _L3_gnn_in = {k: v for k, v in _L3_gnn_all.items() if k in ('rel_emb', 'W_neighbor', 'loop_weight')}
    del _L3_gnn_all
    return {'x': x, 'src': src, 'dst': dst, 'edge_attr_16': edge_attr_16, 'edge_type_500': edge_type_500, 'L0_gnn_lin_w': _L0_gnn_in['lin_w'], 'L0_gnn_edge_w1': _L0_gnn_in['edge_w1'], 'L0_gnn_edge_b1': _L0_gnn_in['edge_b1'], 'L0_gnn_edge_w2': _L0_gnn_in['edge_w2'], 'L0_gnn_edge_b2': _L0_gnn_in['edge_b2'], 'L0_gnn_bias': _L0_gnn_in['bias'], 'L0_gnn_ln_w': _L0_gnn_in['ln_w'], 'L0_gnn_ln_b': _L0_gnn_in['ln_b'], 'L1_gnn_W_neigh': _L1_gnn_in['W_neigh'], 'L1_gnn_b_neigh': _L1_gnn_in['b_neigh'], 'L1_gnn_W_edge': _L1_gnn_in['W_edge'], 'L1_gnn_b_edge': _L1_gnn_in['b_edge'], 'L1_gnn_W_lin': _L1_gnn_in['W_lin'], 'L1_gnn_b_lin': _L1_gnn_in['b_lin'], 'L2_gnn_w_m1': _L2_gnn_in['w_m1'], 'L2_gnn_b_m1': _L2_gnn_in['b_m1'], 'L2_gnn_w_m2': _L2_gnn_in['w_m2'], 'L2_gnn_b_m2': _L2_gnn_in['b_m2'], 'L2_gnn_w_u1': _L2_gnn_in['w_u1'], 'L2_gnn_b_u1': _L2_gnn_in['b_u1'], 'L2_gnn_w_u2': _L2_gnn_in['w_u2'], 'L2_gnn_b_u2': _L2_gnn_in['b_u2'], 'L2_gnn_gamma': _L2_gnn_in['gamma'], 'L2_gnn_beta': _L2_gnn_in['beta'], 'L3_gnn_rel_emb': _L3_gnn_in['rel_emb'], 'L3_gnn_W_neighbor': _L3_gnn_in['W_neighbor'], 'L3_gnn_loop_weight': _L3_gnn_in['loop_weight']}

def reference(x, src, dst, edge_attr_16, edge_type_500, L0_gnn_lin_w, L0_gnn_edge_w1, L0_gnn_edge_b1, L0_gnn_edge_w2, L0_gnn_edge_b2, L0_gnn_bias, L0_gnn_ln_w, L0_gnn_ln_b, L1_gnn_W_neigh, L1_gnn_b_neigh, L1_gnn_W_edge, L1_gnn_b_edge, L1_gnn_W_lin, L1_gnn_b_lin, L2_gnn_w_m1, L2_gnn_b_m1, L2_gnn_w_m2, L2_gnn_b_m2, L2_gnn_w_u1, L2_gnn_b_u1, L2_gnn_w_u2, L2_gnn_b_u2, L2_gnn_gamma, L2_gnn_beta, L3_gnn_rel_emb, L3_gnn_W_neighbor, L3_gnn_loop_weight):
    import jax
    import jax.numpy as jnp

    def _L0_gnn_ref(x, edge_attr, lin_w, edge_w1, edge_b1, edge_w2, edge_b2, bias, ln_w, ln_b, edge_index):
        import jax, jax.numpy as jnp
        import numpy as np
        N, E, D_IN, D_H, D_E, L = (50000, 25000, 128, 128, 16, 3)
        LN_EPS = 1e-05
        row, col = (edge_index[0], edge_index[1])
        n = x.shape[0]
        deg = jax.ops.segment_sum(jnp.ones(row.shape, x.dtype), col, num_segments=n)
        dis = jnp.where(deg > 0, jax.lax.rsqrt(jnp.maximum(deg, 1e-30)), 0.0)
        w = dis[row] * dis[col]
        h = x
        for l in range(L):
            hx = h @ lin_w[l]
            ea = jax.nn.relu(edge_attr @ edge_w1[l] + edge_b1[l]) @ edge_w2[l] + edge_b2[l]
            msg = hx[row] * w[:, None] + ea
            out = jax.ops.segment_sum(msg, col, num_segments=n) + bias[l]
            mu = out.mean(-1, keepdims=True)
            var = ((out - mu) ** 2).mean(-1, keepdims=True)
            h = jax.nn.relu((out - mu) * jax.lax.rsqrt(var + LN_EPS) * ln_w[l] + ln_b[l])
        return h

    def _L1_gnn_ref(features, edge_index, W_neigh, b_neigh, W_edge, b_edge, W_lin, b_lin):
        import jax, jax.numpy as jnp
        import numpy as np
        N_NODES = 50000
        N_EDGES = 18750
        D = 128
        D_OUT = 128
        n = features.shape[0]
        dst = edge_index[0]
        src = edge_index[1]
        h = features @ W_neigh.T + b_neigh
        h_src = h[src]
        edge_feats = jnp.abs(h[dst] - h_src)
        new_h = jnp.concatenate([h_src, edge_feats], axis=-1) @ W_edge.T + b_edge
        seg_sum = jax.ops.segment_sum(new_h, dst, num_segments=n)
        cnt = jax.ops.segment_sum(jnp.ones((dst.shape[0],), jnp.float32), dst, num_segments=n)[:, None]
        s = (h + seg_sum) / jnp.maximum(cnt, 1.0)
        z = jnp.concatenate([features, s], axis=-1) @ W_lin.T + b_lin
        return z

    def _L2_gnn_ref(x, edge_index, w_m1, b_m1, w_m2, b_m2, w_u1, b_u1, w_u2, b_u2, gamma, beta):
        import jax, jax.numpy as jnp
        import numpy as np
        N_NODES = 3125
        N_EDGES = 18750
        D = 128
        EPS = 1e-05

        def _linear_params(key, d_in, d_out):
            kw, kb = jax.random.split(key)
            bound = 1.0 / np.sqrt(d_in)
            w = jax.random.uniform(kw, (d_in, d_out), minval=-bound, maxval=bound, dtype=jnp.float32)
            b = jax.random.uniform(kb, (d_out,), minval=-bound, maxval=bound, dtype=jnp.float32)
            return (w, b)

        def _layernorm(h, gamma, beta):
            mu = jnp.mean(h, axis=-1, keepdims=True)
            var = jnp.mean(jnp.square(h - mu), axis=-1, keepdims=True)
            return (h - mu) * jax.lax.rsqrt(var + EPS) * gamma + beta
        row, col = (edge_index[0], edge_index[1])
        m_in = jnp.concatenate([x[row], x[col]], axis=-1)
        m = jax.nn.relu(m_in @ w_m1 + b_m1) @ w_m2 + b_m2
        agg = jax.ops.segment_sum(m, col, num_segments=x.shape[0])
        u_in = jnp.concatenate([x, agg], axis=-1)
        h = jax.nn.relu(u_in @ w_u1 + b_u1) @ w_u2 + b_u2
        return _layernorm(h, gamma, beta) + x

    def _L3_gnn_ref(h, norm, rel_emb, W_neighbor, loop_weight, edge_src, edge_dst, edge_type):
        import jax, jax.numpy as jnp
        import numpy as np
        N_NODES = 50000
        N_EDGES = 18750
        N_RELS = 500
        D = 128
        loop_message = h @ loop_weight
        relation = rel_emb[edge_type]
        node = h[edge_src]
        msg = (node + relation) @ W_neighbor
        agg = jax.ops.segment_sum(msg, edge_dst, num_segments=h.shape[0])
        node_repr = agg * norm
        node_repr = jax.nn.relu(node_repr + loop_message)
        return node_repr
    edge_index = jnp.stack([src, dst])
    deg = jnp.maximum(jax.ops.segment_sum(jnp.ones(dst.shape, jnp.float32), dst, num_segments=3125), 1.0)
    deg_isqrt = deg ** (-0.5)
    h = jnp.maximum(_layernorm(x, axis=-1), 0.0)
    x = x + _L0_gnn_ref(h, edge_attr_16, L0_gnn_lin_w, L0_gnn_edge_w1, L0_gnn_edge_b1, L0_gnn_edge_w2, L0_gnn_edge_b2, L0_gnn_bias, L0_gnn_ln_w, L0_gnn_ln_b, edge_index)
    h = jnp.maximum(_layernorm(x, axis=-1), 0.0)
    x = x + _L1_gnn_ref(h, edge_index, L1_gnn_W_neigh, L1_gnn_b_neigh, L1_gnn_W_edge, L1_gnn_b_edge, L1_gnn_W_lin, L1_gnn_b_lin)
    h = jnp.maximum(_layernorm(x, axis=-1), 0.0)
    x = x + _L2_gnn_ref(h, edge_index, L2_gnn_w_m1, L2_gnn_b_m1, L2_gnn_w_m2, L2_gnn_b_m2, L2_gnn_w_u1, L2_gnn_b_u1, L2_gnn_w_u2, L2_gnn_b_u2, L2_gnn_gamma, L2_gnn_beta)
    h = jnp.maximum(_layernorm(x, axis=-1), 0.0)
    x = x + _L3_gnn_ref(h, deg_isqrt[:, None], L3_gnn_rel_emb, L3_gnn_W_neighbor, L3_gnn_loop_weight, src, dst, edge_type_500)
    return x

_drawn_inputs = setup_inputs


def setup_inputs(seed=0):
    import zlib

    import numpy as np

    out = dict(_drawn_inputs(seed))
    spreads = {'L0_gnn_edge_b1': (0.0, 0.1),
     'L0_gnn_edge_b2': (0.0, 0.1),
     'L0_gnn_bias': (0.0, 0.8),
     'L0_gnn_ln_w': (1.0, 0.2),
     'L0_gnn_ln_b': (0.0, 0.1),
     'L1_gnn_b_neigh': (0.0, 0.1),
     'L1_gnn_b_edge': (0.0, 0.1),
     'L1_gnn_b_lin': (0.0, 0.1),
     'L2_gnn_gamma': (1.0, 0.2),
     'L2_gnn_beta': (0.0, 0.1)}
    factors = {'L2_gnn_b_u1': 5.495}
    for name, (base, spread) in spreads.items():
        noise = np.random.default_rng([zlib.crc32(name.encode()), seed]).standard_normal(out[name].shape)
        drawn = base * np.exp(spread * noise) if base else spread * noise
        out[name] = jnp.asarray(drawn.astype(out[name].dtype))
    for name, factor in factors.items():
        out[name] = (out[name] * factor).astype(out[name].dtype)
    return out
```

```python
from contextlib import ExitStack

import numpy as np
import concourse.bass as bass
from concourse import mybir

F32 = mybir.dt.float32
I32 = mybir.dt.int32
BF16 = mybir.dt.bfloat16
ALU = mybir.AluOpType
ACT = mybir.ActivationFunctionType
AX = mybir.AxisListType

D = 128
N = 3125
E = 50000
DE = 16
NRELS = 500
LAYERS = 3
EPS = 1e-5

NB = -(-N // 128)
NP = NB * 128
CB = 5
CH = NB // CB
CW = CB * 128
U = 8
H = U // 2
ITERS = -(-E // (128 * U))
TILES = ITERS * U
SLACK = 128
MS = 2 * D + 1
NACC = 4
DUMP = NP

WEIGHTS = ["lin0", "lin1", "lin2", "ew0", "ew1", "ew2", "neigh", "edge_a", "edge_b", "l1_a", "l1_b",
           "m1_a", "m1_b", "m2", "u1_a", "u1_b", "u2", "neighbor", "loop"]
ROWS = ["lnw0", "lnw1", "lnw2", "lnb0", "lnb1", "lnb2", "bias0", "bias1", "bias2", "eb0", "eb1", "eb2",
        "b_neigh", "b_edge", "b_lin", "b_m1", "b_m2", "b_u1", "b_u2", "gamma", "beta"]


class Count:

    def __init__(self, by=1, start=1):
        self.by, self.start, self.n, self.var = by, start, 0, None

    def enter(self, var, per, first=0):
        self.var, self.per, self.first, self.n0 = var, per, first, self.n

    def leave(self, trips):
        assert self.n - self.n0 == self.per, (self.n, self.n0, self.per)
        self.n, self.var = self.n0 + self.per * trips, None

    def next(self, back=0):
        self.n += 1
        return self.now(back)

    def now(self, back=0):
        k = self.start + self.by * (self.n - back)
        if self.var is None:
            return k
        per = self.by * self.per
        return self.var * per + (k - self.first * per)


def build(nc, x_in, src_in, dst_in, typ_in, srcrow_in, dstgrp_in, ea_in, w_in, w1_in, rows_in, cols_in, rel_in, out):
    ctx = ExitStack()
    with ctx:
        def sb(name, shape, dt=F32):
            return ctx.enter_context(nc.sbuf_tensor(name, shape, dt))

        def sem(name):
            return ctx.enter_context(nc.semaphore(name))

        def dram(name, shape, dt=F32):
            return nc.dram_tensor(name, shape, dt, kind="Internal").ap()

        tab_a, tab_b = dram("tab_a", (NP, D)), dram("tab_b", (NP, D))
        acc_d = [dram(f"acc_d{k}", (NP + 128, MS)) for k in range(NACC)]
        deg_d = dram("deg_d", (NB, 128))

        x = sb("x", [128, NB, D])
        keep = sb("keep", [128, NB, D])
        side = sb("side", [128, NB, D])
        acc = sb("acc", [128, 2, NP + SLACK])
        wts = sb("wts", [128, len(WEIGHTS), D])
        w1 = sb("w1", [128, LAYERS, D])
        rows = sb("rows", [128, len(ROWS), D])
        bu1_col = sb("bu1_col", [128, 1])
        src_i, dst_i, typ_i = (sb(n, [128, TILES], I32) for n in ("src_i", "dst_i", "typ_i"))
        lo_i, hi_i = sb("lo_i", [128, TILES], I32), sb("hi_i", [128, TILES], I32)
        src_f, dst_f = sb("src_f", [128, TILES]), sb("dst_f", [128, TILES])
        lo_f, hi_f = sb("lo_f", [128, TILES]), sb("hi_f", [128, TILES])
        iota = sb("iota", [128, NP])
        ident = sb("ident", [128, 128])
        lower = sb("lower", [128, 128])
        dump = sb("dump", [128, 1])
        zeros = sb("zeros", [128, 512])
        deg, dis, norm = sb("deg", [128, NB]), sb("dis", [128, NB]), sb("norm", [128, NB])
        rcnt = sb("rcnt", [128, 2, CB])
        small = sb("small", [128, 6, NB])
        deg_row = sb("deg_row", [1, NP])
        s_a, s_b, hT = sb("s_a", [128, CW]), sb("s_b", [128, CW]), sb("hT", [128, CW])
        o, hh, ta, tb = (sb(n, [128, CB, D]) for n in ("o", "hh", "ta", "tb"))
        stats, mv = sb("stats", [128, CB, 6]), sb("mv", [128, CB, 2])
        lns = sb("lns", [128, 6, CB])
        sm = sb("sm", [128, NACC, CB, MS])
        col = sb("col", [128, 2, 2, H], I32)
        g_a = sb("g_a", [128, U, D])
        msg = sb("msg", [128, U, MS])
        sums = sb("sums", [128, U, MS])
        big = sb("big", [128, NP])
        iota_i = big[:, :].bitcast(I32)
        halves = big[:, 0:3072].rearrange("p (w h j k) -> p w h j k", w=3, h=2, j=H)
        eq = halves[:, 0]
        junk = halves[:, 1]
        srow = big[:, 2048:3072].bitcast(I32).rearrange("p (h k) -> p h k", h=2)
        diff = sb("diff", [128, 2, H, D])
        where_i = sb("where_i", [128, 2, H], I32)
        before = sb("before", [128, 2, H])
        bsel = sb("bsel", [128, 2, 3, H])
        oh_lo, oh_hi = sb("oh_lo", [128, U, 128], BF16), sb("oh_hi", [128, U, NB], BF16)
        ea_t = sb("ea_t", [128, 128])
        zf = sb("zf", [128, 128])
        zcol = sb("zcol", [128, 1])

        ps = ctx.enter_context(nc.psum_tensor("ps", [128, 4096], F32))
        ps_t, ps_m, ps_h, ps_o = (ps[:, 1024 * k:1024 * k + CW] for k in range(4))

        in_small, in_x, in_w, zeroed = sem("in_small"), sem("in_x"), sem("in_w"), sem("zeroed")
        deg_out, deg_back, out_done = sem("deg_out"), sem("deg_back"), sem("out_done")
        store, sm_in = sem("store"), sem("sm_in")
        ga_in = [sem(f"ga_in{r}") for r in range(U)]
        gb_in = [sem(f"gb_in{r}") for r in range(U)]
        added = [sem(f"added{k}") for k in range(NACC)]
        srow_in = [sem(f"srow_in{k}") for k in range(2)]
        ea_in_s = sem("ea_in_s")
        passed = sem("passed")
        stored = sem("stored")
        consts = sem("consts")
        dve_c = sem("dve_c")
        act_c = sem("act_c")
        pool_c = sem("pool_c")
        hot = sem("hot")
        deg_mm = sem("deg_mm")
        seg = sem("seg")
        ps_full = sem("ps_full")
        zmm = sem("zmm")
        relu = sem("relu")
        msg_s = sem("msg_s")
        full = sem("full")
        pe_n = sem("pe_n")
        act_n = sem("act_n")
        dve_n = sem("dve_n")
        eq_s, diff_s, abs_s, mrg, summed, where = (sem(n) for n in ("eq_s", "diff_s", "abs_s", "mrg", "summed", "where"))

        W = {n: wts[:, k, :] for k, n in enumerate(WEIGHTS)}

        def row(name, blocks=CB):
            k = ROWS.index(name)
            return rows[:, k:k + 1, :].to_broadcast([128, blocks, D])

        def row1(name):
            return rows[:, ROWS.index(name), :]

        def blk(c):
            return bass.ds(c * CB, CB)

        def nodes(c):
            return bass.ds(c * CW, CW)


        side_fm = side[:, :, :].rearrange("p b f -> p (b f)")
        tab_rows = {t: d.rearrange("(b p) f -> p b f", p=128) for t, d in (("a", tab_a), ("b", tab_b))}
        out_rows = out.rearrange("(b p) f -> p b f", p=128)
        ps_z = ps[:, 3584:3712]
        BANKS = [(k, min(512, NP - k)) for k in range(0, NP, 512)]

        def ln_dve(t):
            return [t + "." + k for k in ("st", "mv", "ve", "r0", "r1", "r2", "r3", "r4", "co")]

        def ln_act(t):
            return [t + ".sd", t + ".out"]

        def gcn(last):
            return {
                "pe": ["ta", "mb", "tr"] + (["mm", "mz"] if last else ["mm"]),
                "act": ["sa", "sb"] + ln_act("n") + (ln_act("m") + ["hT"] if last else ["hT", "tab"]),
                "dve": ["c0", "c1", "c2", "c3", "c4"] + ln_dve("n") + ["w", "b"]
                + (["xn", "xw"] + ln_dve("m") + ["hn", "kp", "zs"] if last else ["hd"]),
            }

        STEPS = {
            "start": {"pe": ["tr", "mm"], "act": ln_act("m") + ["hT", "tab"], "dve": ["xc"] + ln_dve("m") + ["hd"]},
            "gcn0": gcn(False), "gcn1": gcn(False), "gcn2": gcn(True),
            "sage": {
                "pe": ["ta", "tb", "me", "tr", "mz", "tr2", "mp", "mq", "mu"],
                "act": ["sa", "sb", "hT"] + ln_act("m") + ["hT2", "tp", "us"],
                "dve": ["s0", "s1", "s2", "cn", "rc", "c0", "c1", "c2", "c3", "z0", "xn", "xw"] + ln_dve("m")
                + ["kp", "tq"],
            },
            "mlp": {
                "pe": ["ag", "mu", "my", "tr", "ml"],
                "act": ["sa", "ur"] + ln_act("n") + ln_act("m") + ["hT", "zs"],
                "dve": ["ua", "y"] + ln_dve("n") + ["w", "b", "hb", "xn", "xw"] + ln_dve("m"),
            },
            "rel": {"pe": ["mn"], "act": ["sa"], "dve": ["c0", "c1", "c2"]},
        }
        PHASES = list(STEPS)
        STEP0 = 32
        done_in = {e: [] for e in ("pe", "act", "dve")}

        def at(e, ph, c, name, back=0):
            names = STEPS[ph][e]
            before = sum(CH * len(STEPS[p][e]) for p in PHASES[:PHASES.index(ph)])
            return c * len(names) + (STEP0 + before + names.index(name) + 1 - back * len(names))

        def end(e, ph):
            return at(e, ph, CH - 1, STEPS[ph][e][-1])

        step_sem = {"pe": pe_n, "act": act_n, "dve": dve_n}

        def tick(e, ph, name, ins):
            assert name == STEPS[ph][e][len(done_in[e]) % len(STEPS[ph][e])], (e, ph, name)
            done_in[e].append(name)
            ins.then_inc(step_sem[e], 1)

        def phase_over(e, ph):
            assert done_in[e] == STEPS[ph][e], (e, ph)
            done_in[e].clear()

        STORES = {"start": 1, "gcn0": 1, "gcn1": 1, "gcn2": 1, "sage": 2, "mlp": 1, "rel": 1}

        def stored_at(ph, c, k=0, back=0):
            before = sum(CH * STORES[p] for p in PHASES[:PHASES.index(ph)])
            return c * STORES[ph] + (1 + before + k + 1 - back * STORES[ph])

        def all_stored(ph):
            return stored_at(ph, CH - 1, STORES[ph] - 1)

        DEG_CHAIN = 12
        DEG_READY = DEG_CHAIN

        block = ctx.enter_context(nc.Block())

        @block.sync
        def _(sp):
            sp.sem_inc(stored, 1)
            for k, (dst, src) in enumerate(((src_i, src_in), (dst_i, dst_in), (typ_i, typ_in))):
                sp.dma_start(dst[:, :], src).then_inc(in_small, 16)
            sp.dma_start(x[:, :, :], x_in).then_inc(in_x, 16)
            sp.dma_start(wts[:, :, :], w_in).then_inc(in_w, 16)
            sp.wait_ge(dve_c, 2)
            sp.dma_start(w1[0:DE + 1, :, :], w1_in).then_inc(in_w, 16)
            sp.dma_start(rows[:, :, :], rows_in.unsqueeze(0).to_broadcast([128, len(ROWS), D])).then_inc(in_w, 16)
            sp.dma_start(bu1_col[:, :], cols_in).then_inc(in_w, 16)
            for k in range(NACC):
                flat = acc_d[k].rearrange("(b p) f -> p b f", p=128)
                for b in range(NB + 1):
                    sp.dma_start(flat[:, b, :], zeros[:, 0:MS]).then_inc(zeroed, 16)
            sp.wait_ge(dve_c, DEG_READY)
            sp.dma_start(deg_d.rearrange("b p -> p b"), deg[:, :], allow_slow_non_contiguous=True).then_inc(deg_out, 16)
            sp.wait_ge(deg_out, 16)
            sp.dma_start(deg_row[:, :], deg_d.rearrange("(a b) p -> a (b p)", a=1)).then_inc(deg_back, 16)

            def store_table(ph, dst, src, e, name):
                with sp.Fori(0, CH) as c:
                    sp.wait_ge(step_sem[e], at(e, ph, c, name))
                    sp.dma_start(dst[:, blk(c), :], src[:, :, :]).then_inc(store, 16)
                    sp.wait_ge(store, (stored_at(ph, c) - 1) * 16)
                    sp.sem_inc(stored, 1)

            zc = Count()

            def load_ea(layer):
                with sp.Fori(0, TILES) as t:
                    zc.enter(t, 1)
                    sp.wait_ge(zmm, zc.next(back=1))
                    sp.dma_start(ea_t[0:DE + 1, :], ea_in[:, bass.ds(t * 128, 128)]).then_inc(ea_in_s, 16)
                zc.leave(TILES)

            store_table("start", tab_rows["a"], tb, "act", "tab")
            load_ea(0)
            store_table("gcn0", tab_rows["a"], tb, "act", "tab")
            load_ea(1)
            store_table("gcn1", tab_rows["a"], tb, "act", "tab")
            load_ea(2)
            store_table("gcn2", tab_rows["a"], ta, "dve", "hn")

            def load_srow(i, hf):
                tile = i * U + hf * H
                sp.wait_ge(eq_s, i * 2 + (hf + 1))
                sp.dma_start(srow[:, hf, :], srcrow_in[:, bass.ds(tile * 128, H * 128)]
                             .to_broadcast([128, H * 128])).then_inc(srow_in[hf], 16)

            with sp.Fori(0, ITERS) as i:
                for hf in range(2):
                    load_srow(i, hf)

            for k in range(NACC):
                sp.wait_ge(added[k], 32 * ITERS)
            with sp.Fori(0, CH) as c:
                sp.wait_ge(pe_n, at("pe", "sage", c, "tb", back=1))
                sp.wait_ge(dve_n, at("dve", "sage", c, "c0", back=1))
                for k in range(NACC):
                    sp.dma_start(sm[:, k, :, :], acc_d[k].rearrange("(b p) f -> p b f", p=128)[:, blk(c), :]).then_inc(sm_in, 16)
                for k, (e, name, dst, src) in enumerate((("act", "tp", "a", tb), ("dve", "tq", "b", ta))):
                    sp.wait_ge(step_sem[e], at(e, "sage", c, name))
                    sp.dma_start(tab_rows[dst][:, blk(c), :], src[:, :, :]).then_inc(store, 16)
                    sp.wait_ge(store, (stored_at("sage", c, k) - 1) * 16)
                    sp.sem_inc(stored, 1)

            store_table("mlp", tab_rows["a"], hh, "act", "m.out")
            store_table("rel", out_rows, tb, "dve", "c2")
            sp.wait_ge(store, (all_stored("rel") - 1) * 16)


        @block.gpsimd
        def _(pool):
            pool.sem_inc(pool_c, 1)
            pool.iota(iota_i[:, :], pattern=[[1, NP]], base=0, channel_multiplier=0).then_inc(consts, 1)
            pool.memset(ident[:, :], 0.0).then_inc(consts, 1)
            pool.memset(lower[:, :], 1.0).then_inc(consts, 1)
            pool.wait_ge(consts, 3)
            pool.tensor_copy(iota[:, :], iota_i[:, :]).then_inc(consts, 1)
            pool.affine_select(out=ident[:, :], in_=ident[:, :], compare_op=ALU.not_equal, fill=1.0, base=0,
                               pattern=[[-1, 128]], channel_multiplier=1).then_inc(consts, 1)
            pool.affine_select(out=lower[:, :], in_=lower[:, :], compare_op=ALU.is_gt, fill=0.0, base=0,
                               pattern=[[-1, 128]], channel_multiplier=1).then_inc(consts, 1)
            pool.wait_ge(consts, 4)
            pool.iota(iota_i[:, 0:1], pattern=[[1, 1]], base=DUMP, channel_multiplier=1).then_inc(consts, 1)
            pool.wait_ge(consts, 7)
            pool.tensor_copy(dump[:, :], iota_i[:, 0:1]).then_inc(consts, 1)
            pool.wait_ge(in_small, 48)

            copies, segs = Count(), Count()

            def gather(g, table, index, signal):
                pool.indirect_dma_start(g, None, table, bass.IndirectOffsetOnAxis(ap=index, axis=0)).then_inc(signal, 16)

            def gather_pass(ph, second):
                pool.wait_ge(stored, all_stored(ph))
                with pool.Fori(0, TILES) as t:
                    copies.enter(t, 2)
                    segs.enter(t, 1)
                    pool.wait_ge(seg, segs.next(back=1))
                    pool.tensor_copy(col[:, 0, 0, 0:1], src_i[:, bass.ds(t, 1)]).then_inc(pool_c, 1)
                    other = src_i if second is None else second[1]
                    copies.next()
                    pool.tensor_copy(col[:, 0, 1, 0:1], other[:, bass.ds(t, 1)]).then_inc(pool_c, 1)
                    pool.wait_ge(pool_c, copies.next())
                    pool.sem_inc(passed, 1)
                    gather(g_a[:, 0, :], tab_a, col[:, 0, 0, 0:1], ga_in[0])
                    if second is not None:
                        gather(msg[:, 0, 0:D], second[0], col[:, 0, 1, 0:1], gb_in[0])
                copies.leave(TILES)
                segs.leave(TILES)

            for layer in range(LAYERS):
                gather_pass(("start", "gcn0", "gcn1")[layer], None)
                segs.n += TILES

            pool.wait_ge(stored, all_stored("gcn2"))

            def gathers(i, hf, first):
                r0, tile = hf * H, i * U + hf * H
                if not first:
                    pool.wait_ge(mrg, i * 2 + hf - 1 + 1)
                pool.tensor_copy(col[:, hf, 0, :], src_i[:, bass.ds(tile, H)]).then_inc(pool_c, 1)
                copies.next()
                pool.tensor_copy(col[:, hf, 1, :], dst_i[:, bass.ds(tile, H)]).then_inc(pool_c, 1)
                pool.wait_ge(pool_c, copies.next())
                pool.sem_inc(passed, 1)
                for j in range(H):
                    gather(g_a[:, r0 + j, :], tab_a, col[:, hf, 0, j:j + 1], ga_in[r0 + j])
                    gather(msg[:, r0 + j, 0:D], tab_a, col[:, hf, 1, j:j + 1], gb_in[r0 + j])

            def scatters(i, hf, first=False):
                pool.wait_ge(where, i * 2 + hf + 2)
                pool.wait_ge(summed, i * 2 + hf + 2)
                for j in range(H):
                    if not first:
                        pool.wait_ge(added[j], i * 32 + 16 * hf)
                    pool.sem_inc(passed, 1)
                    pool.indirect_dma_start(acc_d[j], bass.IndirectOffsetOnAxis(ap=where_i[:, hf, j:j + 1], axis=0),
                                            sums[:, hf * H + j, :], None, compute_op=ALU.add).then_inc(added[j], 16)

            gathers(0, 0, True)
            gathers(0, 1, True)
            pool.wait_ge(zeroed, 16 * NACC * (NB + 1))
            scatters(0, 0, True)
            with pool.Fori(1, ITERS) as i:
                copies.enter(i, 4, 1)
                gathers(i, 0, False)
                scatters(i - 1, 1)
                gathers(i, 1, False)
                scatters(i, 0)
            copies.leave(ITERS - 1)
            scatters(ITERS - 1, 1)

            gather_pass("sage", (tab_b, dst_i))
            gather_pass("mlp", (rel_in, typ_i))

        @block.vector
        def _(dve):
            dve.sem_inc(hot, 1)
            dve.sem_inc(eq_s, 2)
            dve.sem_inc(dve_n, STEP0)
            dve.sem_inc(msg_s, 1)
            for q in (diff_s, where):
                dve.sem_inc(q, 1)
            chain = Count(start=0)

            def link(ins):
                ins.then_inc(dve_c, 1)
                dve.wait_ge(dve_c, chain.next())

            link(dve.memset(zeros[:, :], 0.0))
            link(dve.memset(w1[:, :, :], 0.0))
            link(dve.memset(ea_t[:, :], 0.0))
            link(dve.memset(acc[:, :, NP:], 0.0))
            link(dve.memset(msg[:, :, 2 * D:], 1.0))
            dve.wait_ge(in_small, 48)
            dve.wait_ge(consts, 8)
            link(dve.tensor_copy(src_f[:, :], src_i[:, :]))
            link(dve.tensor_copy(dst_f[:, :], dst_i[:, :]))
            link(dve.tensor_scalar(lo_i[:, :], dst_i[:, :], 127, None, ALU.bitwise_and))
            link(dve.tensor_scalar(hi_i[:, :], dst_i[:, :], 7, None, ALU.logical_shift_right))
            link(dve.tensor_copy(lo_f[:, :], lo_i[:, :]))
            link(dve.tensor_copy(hi_f[:, :], hi_i[:, :]))

            hots = Count()
            with dve.Fori(0, ITERS) as i:
                dve.wait_ge(deg_mm, i + 1)
                for oh, part, width in ((oh_lo, lo_f, 128), (oh_hi, hi_f, NB)):
                    dve.tensor_tensor(oh[:, :, :], iota[:, 0:width].unsqueeze(1).to_broadcast([128, U, width]),
                                      part[:, bass.ds(i * U, U)].unsqueeze(2).to_broadcast([128, U, width]),
                                      ALU.is_equal).then_inc(hot, 1)
            hots.n += 2 * ITERS
            dve.wait_ge(deg_mm, ITERS + 2)
            link(dve.tensor_copy(deg[:, :], ps[:, 0:NB]))
            link(dve.tensor_scalar(small[:, 0, :], deg[:, :], 1.0, None, ALU.max))
            chain_sq = chain.n
            dve.wait_ge(act_c, 1)
            link(dve.reciprocal(small[:, 2, :], small[:, 1, :]))
            link(dve.tensor_tensor(small[:, 3, :], small[:, 2, :], small[:, 2, :], ALU.mult))
            link(dve.tensor_tensor(small[:, 3, :], small[:, 3, :], small[:, 0, :], ALU.mult))
            link(dve.tensor_scalar(small[:, 3, :], small[:, 3, :], -0.5, 1.5, ALU.mult, ALU.add))
            link(dve.tensor_tensor(norm[:, :], small[:, 2, :], small[:, 3, :], ALU.mult))
            link(dve.tensor_scalar(small[:, 4, :], deg[:, :], 0.0, None, ALU.is_gt))
            link(dve.tensor_tensor(dis[:, :], norm[:, :], small[:, 4, :], ALU.mult))
            assert chain.n == DEG_CHAIN + 8 and chain_sq == DEG_CHAIN + 1, (chain.n, chain_sq)

            dve.wait_ge(in_x, 16)
            dve.wait_ge(in_w, 64)

            def step(ph, name, ins):
                tick("dve", ph, name, ins)

            def after(ph, c, name):
                dve.wait_ge(dve_n, at("dve", ph, c, name))

            def ln(ph, c, t, src):
                for k in range(CB):
                    last = dve.bn_stats(stats[:, k, :], src[:, k, :])
                step(ph, t + ".st", last)
                after(ph, c, t + ".st")
                dve.sem_inc(passed, 1)
                for k in range(CB):
                    last = dve.bn_aggr(mv[:, k, :], stats[:, k, :])
                step(ph, t + ".mv", last)
                after(ph, c, t + ".mv")
                step(ph, t + ".ve", dve.tensor_scalar(lns[:, 0, :], mv[:, :, 1], EPS, None, ALU.add))
                dve.wait_ge(act_n, at("act", ph, c, t + ".sd"))
                step(ph, t + ".r0", dve.reciprocal(lns[:, 2, :], lns[:, 1, :]))
                after(ph, c, t + ".r0")
                step(ph, t + ".r1", dve.tensor_tensor(lns[:, 3, :], lns[:, 2, :], lns[:, 2, :], ALU.mult))
                after(ph, c, t + ".r1")
                step(ph, t + ".r2", dve.tensor_tensor(lns[:, 3, :], lns[:, 3, :], lns[:, 0, :], ALU.mult))
                after(ph, c, t + ".r2")
                step(ph, t + ".r3", dve.tensor_scalar(lns[:, 3, :], lns[:, 3, :], -0.5, 1.5, ALU.mult, ALU.add))
                after(ph, c, t + ".r3")
                step(ph, t + ".r4", dve.tensor_tensor(lns[:, 4, :], lns[:, 2, :], lns[:, 3, :], ALU.mult))
                after(ph, c, t + ".r4")
                step(ph, t + ".co", dve.scalar_tensor_tensor(out=lns[:, 5, :], in0=mv[:, :, 0], scalar=-1.0,
                                                             in1=lns[:, 4, :], op0=ALU.mult, op1=ALU.mult))

            def per_node(v, c):
                return v[:, blk(c)].unsqueeze(2).to_broadcast([128, CB, D])

            def psv(p):
                return p.rearrange("p (b f) -> p b f", f=D)

            def affine(ph, c, w, b):
                dve.wait_ge(act_n, at("act", ph, c, "n.out"))
                step(ph, "w", dve.tensor_tensor(hh[:, :, :], hh[:, :, :], row(w), ALU.mult))
                after(ph, c, "w")
                step(ph, "b", dve.tensor_tensor(hh[:, :, :], hh[:, :, :], row(b), ALU.add))
                after(ph, c, "b")

            def add_to_x(ph, c, src):
                after(ph, c, "xn")
                step(ph, "xw", dve.tensor_scalar(x[:, blk(c), :], src[:, :, :], 1.0, None, ALU.mult))

            ph = "start"
            with dve.Fori(0, CH) as c:
                dve.wait_ge(act_n, at("act", ph, c, "m.out", back=1))
                step(ph, "xc", dve.tensor_scalar(ta[:, :, :], x[:, blk(c), :], 1.0, None, ALU.mult))
                after(ph, c, "xc")
                ln(ph, c, "m", ta)
                dve.wait_ge(act_n, at("act", ph, c, "m.out"))
                dve.wait_ge(pe_n, at("pe", ph, c, "tr", back=1))
                step(ph, "hd", dve.tensor_tensor(o[:, :, :], hh[:, :, :], per_node(dis, c), ALU.mult))
            phase_over("dve", ph)

            def one_hot_pass(mix=None):
                with dve.Fori(0, TILES) as t:
                    hots.enter(t, 1)
                    segs.enter(t, 1)
                    dve.wait_ge(seg, segs.next(back=1))
                    dve.tensor_scalar(big[:, :], iota[:, :], dst_f[:, bass.ds(t, 1)], None, ALU.is_equal).then_inc(hot, 1)
                    hots.next()
                    if mix is not None:
                        mixes.enter(t, 1)
                        loads.enter(t, 1)
                        dve.wait_ge(ga_in[0], loads.next())
                        dve.wait_ge(gb_in[0], 16 * t + 16 * mix[1])
                        dve.tensor_tensor(mix[0], g_a[:, 0, :], msg[:, 0, 0:D], ALU.add).then_inc(msg_s, 1)
                        mixes.next()
                hots.leave(TILES)
                segs.leave(TILES)
                if mix is not None:
                    mixes.leave(TILES)
                    loads.leave(TILES)

            segs, mixes, loads = Count(), Count(), Count(by=16, start=0)

            for layer in range(LAYERS):
                ph = f"gcn{layer}"
                loads.n += TILES
                one_hot_pass()
                one_hot_pass()
                with dve.Fori(0, CH) as c:
                    dve.wait_ge(pe_n, at("pe", ph, c, "ta"))
                    dve.wait_ge(pe_n, at("pe", ph, c, "tr", back=1))
                    step(ph, "c0", dve.tensor_tensor(o[:, :, :], psv(ps_t), per_node(dis, c), ALU.mult))
                    if layer == LAYERS - 1:
                        dve.wait_ge(stored, stored_at(ph, c, back=1))
                        dve.wait_ge(dve_n, at("dve", ph, c, "kp", back=1))
                    step(ph, "c1", dve.tensor_tensor(ta[:, :, :], row(f"eb{layer}"), per_node(deg, c), ALU.mult))
                    after(ph, c, "c1")
                    step(ph, "c2", dve.tensor_tensor(ta[:, :, :], ta[:, :, :], row(f"bias{layer}"), ALU.add))
                    after(ph, c, "c2")
                    step(ph, "c3", dve.tensor_tensor(o[:, :, :], o[:, :, :], ta[:, :, :], ALU.add))
                    after(ph, c, "c3")
                    dve.wait_ge(pe_n, at("pe", ph, c, "mb"))
                    step(ph, "c4", dve.tensor_tensor(o[:, :, :], o[:, :, :], psv(ps_m), ALU.add))
                    after(ph, c, "c4")
                    ln(ph, c, "n", o)
                    affine(ph, c, f"lnw{layer}", f"lnb{layer}")
                    if layer < LAYERS - 1:
                        step(ph, "hd", dve.scalar_tensor_tensor(out=o[:, :, :], in0=hh[:, :, :], scalar=0.0,
                                                                in1=per_node(dis, c), op0=ALU.max, op1=ALU.mult))
                    else:
                        step(ph, "xn", dve.scalar_tensor_tensor(out=ta[:, :, :], in0=hh[:, :, :], scalar=0.0,
                                                                in1=x[:, blk(c), :], op0=ALU.max, op1=ALU.add))
                        add_to_x(ph, c, ta)
                        ln(ph, c, "m", ta)
                        dve.wait_ge(act_n, at("act", ph, c, "m.out"))
                        dve.wait_ge(pe_n, at("pe", ph, c, "mm"))
                        step(ph, "hn", dve.tensor_tensor(ta[:, :, :], psv(ps_o), row("b_neigh"), ALU.add))
                        after(ph, c, "hn")
                        step(ph, "kp", dve.tensor_scalar(keep[:, blk(c), :], ta[:, :, :], 1.0, None, ALU.mult))
                        dve.wait_ge(pe_n, at("pe", ph, c, "mz"))
                        step(ph, "zs", dve.tensor_tensor(side[:, blk(c), :], psv(ps_m), row("b_lin"), ALU.add))
                phase_over("dve", ph)

            def edge_half(i, hf, prior):
                r, tile = slice(hf * H, hf * H + H), i * U + hf * H
                here = src_f[:, bass.ds(tile, H)]
                dve.wait_ge(srow_in[hf], i * 16 + 16)
                dve.wait_ge(mrg, i * 2 + hf + 0 if prior else 1)
                dve.tensor_tensor(eq[:, hf, :, :], srow[:, hf, :].rearrange("p (j k) -> p j k", j=H),
                                  here.unsqueeze(2).to_broadcast([128, H, 128]), ALU.is_equal).then_inc(eq_s, 1)
                dve.wait_ge(eq_s, i * 2 + hf + 3)
                lchain(i, dve.tensor_tensor(junk[:, hf, :, :], eq[:, hf, :, :],
                                            lower[:, :].unsqueeze(1).to_broadcast([128, H, 128]), ALU.mult))
                lchain(i, dve.tensor_reduce(before[:, hf, :], junk[:, hf, :, :], AX.X, ALU.add))
                lchain(i, dve.tensor_scalar(bsel[:, hf, 0, :], before[:, hf, :], 0.0, None, ALU.is_gt))
                lchain(i, dve.tensor_tensor(bsel[:, hf, 1, :], dump[:, 0:1].to_broadcast([128, H]), here, ALU.subtract))
                lchain(i, dve.tensor_tensor(bsel[:, hf, 2, :], bsel[:, hf, 0, :], bsel[:, hf, 1, :], ALU.mult))
                for j in range(H if prior else 0):
                    dve.wait_ge(added[j], i * 32 + 16 * (hf - 1))
                dve.tensor_tensor(where_i[:, hf, :], bsel[:, hf, 2, :], here, ALU.add).then_inc(where, 1)
                for j in range(H):
                    dve.wait_ge(ga_in[hf * H + j], (LAYERS * TILES * 16 if hf * H + j == 0 else 0) + 16 + i * 16)
                    dve.wait_ge(gb_in[hf * H + j], i * 16 + 16)
                dve.wait_ge(abs_s, i * 2 + hf + 0 if prior else 1)
                dve.tensor_tensor(diff[:, hf, :, :], g_a[:, r, :], msg[:, r, 0:D], ALU.subtract).then_inc(diff_s, 1)

            def lchain(i, ins):
                ins.then_inc(dve_c, 1)
                dve.wait_ge(dve_c, chain.next())

            edge_half(0, 0, False)
            edge_half(0, 1, False)
            with dve.Fori(1, ITERS) as i:
                chain.enter(i, 10, 1)
                edge_half(i, 0, True)
                edge_half(i, 1, True)
            chain.leave(ITERS - 1)

            ph = "sage"
            with dve.Fori(0, CH) as c:
                dve.wait_ge(sm_in, c * (16 * NACC) + 16 * NACC)
                step(ph, "s0", dve.tensor_tensor(sm[:, 0, :, :], sm[:, 0, :, :], sm[:, 1, :, :], ALU.add))
                step(ph, "s1", dve.tensor_tensor(sm[:, 2, :, :], sm[:, 2, :, :], sm[:, 3, :, :], ALU.add))
                after(ph, c, "s1")
                step(ph, "s2", dve.tensor_tensor(sm[:, 0, :, :], sm[:, 0, :, :], sm[:, 2, :, :], ALU.add))
                after(ph, c, "s2")
                step(ph, "cn", dve.tensor_scalar(rcnt[:, 0, :], sm[:, 0, :, 2 * D], 1.0, None, ALU.max))
                after(ph, c, "cn")
                step(ph, "rc", dve.reciprocal(rcnt[:, 1, :], rcnt[:, 0, :]))
                dve.wait_ge(stored, stored_at(ph, c, 1, back=1))
                step(ph, "c0", dve.tensor_tensor(ta[:, :, :], row("b_edge"),
                                                 sm[:, 0, :, 2 * D:].to_broadcast([128, CB, D]), ALU.mult))
                after(ph, c, "c0")
                dve.wait_ge(pe_n, at("pe", ph, c, "me"))
                step(ph, "c1", dve.tensor_tensor(ta[:, :, :], ta[:, :, :], psv(ps_o), ALU.add))
                after(ph, c, "c1")
                step(ph, "c2", dve.tensor_tensor(ta[:, :, :], ta[:, :, :], keep[:, blk(c), :], ALU.add))
                after(ph, c, "c2")
                dve.wait_ge(pe_n, at("pe", ph, c, "tr", back=1))
                step(ph, "c3", dve.tensor_tensor(o[:, :, :], ta[:, :, :],
                                                 rcnt[:, 1, :].unsqueeze(2).to_broadcast([128, CB, D]), ALU.mult))
                dve.wait_ge(pe_n, at("pe", ph, c, "mz"))
                dve.wait_ge(stored, stored_at(ph, c, 0, back=1))
                step(ph, "z0", dve.tensor_tensor(tb[:, :, :], side[:, blk(c), :], psv(ps_t), ALU.add))
                after(ph, c, "z0")
                step(ph, "xn", dve.tensor_tensor(ta[:, :, :], tb[:, :, :], x[:, blk(c), :], ALU.add))
                add_to_x(ph, c, ta)
                ln(ph, c, "m", ta)
                dve.wait_ge(act_n, at("act", ph, c, "m.out"))
                step(ph, "kp", dve.tensor_scalar(keep[:, blk(c), :], hh[:, :, :], 1.0, None, ALU.mult))
                dve.wait_ge(pe_n, at("pe", ph, c, "mq"))
                step(ph, "tq", dve.tensor_tensor(ta[:, :, :], psv(ps_m), row("b_m1"), ALU.add))
            phase_over("dve", ph)

            loads.n += ITERS
            gb0 = ITERS + 1
            one_hot_pass((diff[:, 0, 0, :], gb0))
            ph = "mlp"
            with dve.Fori(0, CH) as c:
                dve.wait_ge(pe_n, at("pe", ph, c, "mu"))
                dve.wait_ge(pe_n, at("pe", ph, c, "ml", back=1))
                step(ph, "ua", dve.tensor_tensor(hT[:, :], side_fm[:, nodes(c)], ps_m, ALU.add))
                dve.wait_ge(pe_n, at("pe", ph, c, "my"))
                step(ph, "y", dve.tensor_tensor(o[:, :, :], row("b_u2"), psv(ps_o), ALU.add))
                after(ph, c, "y")
                ln(ph, c, "n", o)
                affine(ph, c, "gamma", "beta")
                step(ph, "hb", dve.tensor_tensor(ta[:, :, :], hh[:, :, :], keep[:, blk(c), :], ALU.add))
                after(ph, c, "hb")
                step(ph, "xn", dve.tensor_tensor(tb[:, :, :], ta[:, :, :], x[:, blk(c), :], ALU.add))
                add_to_x(ph, c, tb)
                ln(ph, c, "m", tb)
            phase_over("dve", ph)

            one_hot_pass((zf[:, :], gb0 + TILES))
            ph = "rel"
            with dve.Fori(0, CH) as c:
                dve.wait_ge(pe_n, at("pe", ph, c, "mn"))
                step(ph, "c0", dve.tensor_tensor(o[:, :, :], psv(ps_o), per_node(norm, c), ALU.mult))
                after(ph, c, "c0")
                step(ph, "c1", dve.tensor_tensor(ta[:, :, :], o[:, :, :], side[:, blk(c), :], ALU.add))
                after(ph, c, "c1")
                dve.wait_ge(stored, stored_at(ph, c, back=1))
                step(ph, "c2", dve.scalar_tensor_tensor(out=tb[:, :, :], in0=ta[:, :, :], scalar=0.0,
                                                        in1=x[:, blk(c), :], op0=ALU.max, op1=ALU.add))
            phase_over("dve", ph)

        @block.scalar
        def _(act):
            for q in (abs_s, summed, relu, full):
                act.sem_inc(q, 1)
            act.sem_inc(act_n, STEP0)

            def step(ph, name, ins):
                tick("act", ph, name, ins)

            def copy(ph, name, dst, src):
                step(ph, name, act.activation(dst, src, ACT.Copy))

            def ln(ph, c, t, src, func, again=None):
                act.wait_ge(dve_n, at("dve", ph, c, t + ".ve"))
                step(ph, t + ".sd", act.activation(lns[:, 1, :], lns[:, 0, :], ACT.Sqrt))
                act.wait_ge(dve_n, at("dve", ph, c, t + ".co"))
                if again is not None:
                    again(c)
                for k in range(CB):
                    last = act.activation(hh[:, k, :], src[:, k, :], func, scale=lns[:, 4, k:k + 1],
                                          bias=lns[:, 5, k:k + 1])
                step(ph, t + ".out", last)

            def turned(ph, c, name, pe_name, free):
                act.wait_ge(pe_n, at("pe", ph, c, pe_name))
                act.wait_ge(pe_n, free)
                copy(ph, name, hT[:, :], ps_h)

            act.wait_ge(dve_c, DEG_CHAIN + 1)
            act.activation(small[:, 1, :], small[:, 0, :], ACT.Sqrt).then_inc(act_c, 1)

            ph = "start"
            with act.Fori(0, CH) as c:
                ln(ph, c, "m", ta, ACT.Relu, lambda c: act.wait_ge(dve_n, at("dve", "start", c, "hd", back=1)))
                turned(ph, c, "hT", "tr", at("pe", ph, c, "mm", back=1))
                act.wait_ge(pe_n, at("pe", ph, c, "mm"))
                act.wait_ge(stored, stored_at(ph, c, back=1))
                copy(ph, "tab", tb[:, :, :].rearrange("p b f -> p (b f)"), ps_o)
            phase_over("act", ph)

            relus, mixes, fulls, zs = Count(), Count(), Count(start=0), Count()

            def sums_out(k):
                act.wait_ge(ps_full, fulls.next())
                act.activation(acc[:, k, 0:NP], ps[:, 0:NP], ACT.Copy).then_inc(full, 1)

            for layer in range(LAYERS):
                ph = f"gcn{layer}"
                sums_out(0)
                with act.Fori(0, TILES) as t:
                    relus.enter(t, 1)
                    zs.enter(t, 1)
                    act.wait_ge(seg, t + (1 + TILES * (2 * layer + 1)))
                    act.wait_ge(zmm, zs.next())
                    act.activation(zf[:, :], ps_z, ACT.Relu).then_inc(relu, 1)
                    relus.next()
                relus.leave(TILES)
                zs.leave(TILES)
                sums_out(1)
                with act.Fori(0, CH) as c:
                    act.wait_ge(full, 1 + fulls.n)
                    act.wait_ge(pe_n, at("pe", ph, c, "ta", back=1))
                    copy(ph, "sa", s_a[:, :], acc[:, 0, nodes(c)])
                    act.wait_ge(pe_n, at("pe", ph, c, "mb", back=1))
                    copy(ph, "sb", s_b[:, :], acc[:, 1, nodes(c)])
                    if layer < LAYERS - 1:
                        ln(ph, c, "n", o, ACT.Identity, lambda c: act.wait_ge(dve_n, at("dve", ph, c, "hd", back=1)))
                        turned(ph, c, "hT", "tr", at("pe", ph, c, "mm", back=1))
                        act.wait_ge(pe_n, at("pe", ph, c, "mm"))
                        act.wait_ge(stored, stored_at(ph, c, back=1))
                        copy(ph, "tab", tb[:, :, :].rearrange("p b f -> p (b f)"), ps_o)
                    else:
                        ln(ph, c, "n", o, ACT.Identity, lambda c: act.wait_ge(pe_n, at("pe", ph, c, "tr", back=1)))
                        ln(ph, c, "m", ta, ACT.Relu)
                        turned(ph, c, "hT", "tr", at("pe", ph, c, "mz", back=1))
                phase_over("act", ph)

            def edge_half(i, hf, prior):
                r = slice(hf * H, hf * H + H)
                act.wait_ge(diff_s, i * 2 + hf + 2)
                act.sem_inc(passed, 1)
                act.activation(msg[:, r, D:2 * D], diff[:, hf, :, :], ACT.Abs).then_inc(abs_s, 1)
                act.wait_ge(mrg, i * 2 + hf + 2)
                for j in range(H if prior else 0):
                    act.wait_ge(added[j], i * 32 + 16 * (hf - 1))
                act.activation(sums[:, r, :], ps[:, 2048 * hf:2048 * hf + 2048].rearrange("p (j f) -> p j f", j=H)[:, :, 0:MS],
                               ACT.Copy).then_inc(summed, 1)

            edge_half(0, 0, False)
            edge_half(0, 1, False)
            with act.Fori(1, ITERS) as i:
                edge_half(i, 0, True)
                edge_half(i, 1, True)

            ph = "sage"
            with act.Fori(0, CH) as c:
                act.wait_ge(pe_n, at("pe", ph, c, "ta"))
                act.wait_ge(pe_n, at("pe", ph, c, "me", back=1))
                copy(ph, "sa", s_a[:, :], ps_t)
                act.wait_ge(pe_n, at("pe", ph, c, "tb"))
                copy(ph, "sb", s_b[:, :], ps_m)
                turned(ph, c, "hT", "tr", at("pe", ph, c, "mu", back=1))
                ln(ph, c, "m", ta, ACT.Relu, lambda c: act.wait_ge(pe_n, at("pe", "sage", c, "tr2", back=1)))
                turned(ph, c, "hT2", "tr2", at("pe", ph, c, "mz"))
                act.wait_ge(pe_n, at("pe", ph, c, "mp"))
                act.wait_ge(dve_n, at("dve", ph, c, "xn"))
                copy(ph, "tp", tb[:, :, :].rearrange("p b f -> p (b f)"), ps_o)
                act.wait_ge(pe_n, at("pe", ph, c, "mu"))
                step(ph, "us", act.activation(side_fm[:, nodes(c)], ps_t, ACT.Identity, bias=bu1_col[:, 0:1]))
            phase_over("act", ph)

            with act.Fori(0, TILES) as t:
                relus.enter(t, 1)
                mixes.enter(t, 1)
                act.wait_ge(msg_s, mixes.next())
                act.wait_ge(seg, t + (1 + TILES * 2 * LAYERS))
                act.activation(zf[:, :], diff[:, 0, 0, :], ACT.Relu).then_inc(relu, 1)
                relus.next()
            relus.leave(TILES)
            mixes.leave(TILES)
            sums_out(0)
            ph = "mlp"
            with act.Fori(0, CH) as c:
                act.wait_ge(pe_n, at("pe", ph, c, "ag"))
                act.wait_ge(pe_n, at("pe", ph, c, "mu", back=1))
                copy(ph, "sa", s_a[:, :], ps_t)
                act.wait_ge(dve_n, at("dve", ph, c, "ua"))
                act.wait_ge(pe_n, at("pe", ph, c, "my", back=1))
                step(ph, "ur", act.activation(s_b[:, :], hT[:, :], ACT.Relu))

                def hh_free(c):
                    act.wait_ge(stored, stored_at("mlp", c, back=1))
                    act.wait_ge(pe_n, at("pe", "mlp", c, "tr", back=1))

                ln(ph, c, "n", o, ACT.Identity, hh_free)
                ln(ph, c, "m", tb, ACT.Relu)
                act.wait_ge(act_n, at("act", ph, c, "ur"))
                turned(ph, c, "hT", "tr", at("pe", ph, c, "ml", back=1))
                act.wait_ge(pe_n, at("pe", ph, c, "ml"))
                act.wait_ge(dve_n, at("dve", ph, c, "ua"))
                step(ph, "zs", act.activation(side_fm[:, nodes(c)], ps_m, ACT.Copy))
            phase_over("act", ph)
            sums_out(0)
            ph = "rel"
            with act.Fori(0, CH) as c:
                act.wait_ge(full, 1 + fulls.n)
                act.wait_ge(pe_n, at("pe", ph, c, "mn", back=1))
                copy(ph, "sa", s_a[:, :], acc[:, 0, nodes(c)])
            phase_over("act", ph)

        @block.tensor
        def _(pe):
            for q in (deg_mm, seg, zmm, mrg):
                pe.sem_inc(q, 1)
            pe.sem_inc(pe_n, STEP0)

            def step(ph, name, ins):
                tick("pe", ph, name, ins)

            def open_sums(banks):
                for k, width in banks:
                    pe.matmul(ps[:, k:k + width], zeros[:, 0:128], zeros[:, 0:width], start=True, stop=False,
                              skip_group_check=True)

            def close_sums(banks):
                for k, width in banks:
                    last = pe.matmul(ps[:, k:k + width], zeros[:, 0:128], zeros[:, 0:width], start=False, stop=True,
                                     skip_group_check=True)
                return last

            pe.wait_ge(dve_c, 1)
            open_sums([(0, NB)])
            with pe.Fori(0, ITERS) as i:
                pe.wait_ge(hot, i * 2 + 3)
                for j in range(U):
                    last = pe.matmul(ps[:, 0:NB], oh_lo[:, j, :], oh_hi[:, j, :], start=False, stop=False,
                                     skip_group_check=True)
                last.then_inc(deg_mm, 1)
            close_sums([(0, NB)]).then_inc(deg_mm, 1)

            pe.wait_ge(consts, 8)
            pe.wait_ge(in_w, 64)
            pe.wait_ge(dve_c, 5)
            hots, segs, relus, mixes, loads, zin = Count(), Count(), Count(), Count(), Count(by=16, start=0), Count(by=16, start=0)
            hots.n += 2 * ITERS

            def turn(ph, c, name, dst, src):
                for k in range(CB):
                    last = pe.transpose(dst[:, k * 128:k * 128 + 128], src(k), ident[:, :])
                step(ph, name, last)

            def by_rows(ph, name, dst, parts):
                for k in range(CB):
                    for n, (lhs, w) in enumerate(parts):
                        last = pe.matmul(dst[:, k * 128:k * 128 + 128], lhs[:, k * 128:k * 128 + 128], W[w],
                                         start=(n == 0), stop=(n == len(parts) - 1))
                step(ph, name, last)

            def hh_blk(k):
                return hh[:, k, :]

            def o_blk(k):
                return o[:, k, :]

            def add_tile(message):
                for k, width in BANKS:
                    last = pe.matmul(ps[:, k:k + width], message, big[:, k:k + width], start=False, stop=False,
                                     skip_group_check=True)
                last.then_inc(seg, 1)

            def sum_pass(message, came):
                open_sums(BANKS)
                with pe.Fori(0, TILES) as t:
                    hots.enter(t, 1)
                    pe.wait_ge(hot, hots.next())
                    came(t)
                    add_tile(message)
                hots.leave(TILES)
                close_sums(BANKS).then_inc(ps_full, 1)

            ph = "start"
            with pe.Fori(0, CH) as c:
                pe.wait_ge(dve_n, at("dve", ph, c, "hd"))
                pe.wait_ge(act_n, at("act", ph, c, "hT", back=1))
                turn(ph, c, "tr", ps_h, o_blk)
                pe.wait_ge(act_n, at("act", ph, c, "hT"))
                pe.wait_ge(act_n, at("act", ph, c, "tab", back=1))
                by_rows(ph, "mm", ps_o, [(hT, "lin0")])
            phase_over("pe", ph)

            full_n = 1
            for layer in range(LAYERS):
                pe.wait_ge(act_n, end("act", PHASES[layer]))
                pe.wait_ge(dve_n, end("dve", PHASES[layer]))
                if layer:
                    pe.wait_ge(full, full_n)

                def gathered(t):
                    loads.enter(t, 1)
                    pe.wait_ge(ga_in[0], loads.next())

                sum_pass(g_a[:, 0, :], gathered)
                loads.leave(TILES)
                full_n += 1
                pe.wait_ge(full, full_n)

                def through_mlp(t):
                    relus.enter(t, 1)
                    zin.enter(t, 1)
                    pe.wait_ge(ea_in_s, zin.next())
                    pe.matmul(ps_z, ea_t[:, :], w1[:, layer, :], start=True, stop=True).then_inc(zmm, 1)
                    pe.wait_ge(relu, relus.next())

                sum_pass(zf[:, :], through_mlp)
                relus.leave(TILES)
                zin.leave(TILES)
                full_n += 1
                pe.wait_ge(full, full_n)
                ph = f"gcn{layer}"
                with pe.Fori(0, CH) as c:
                    pe.wait_ge(act_n, at("act", ph, c, "sa"))
                    pe.wait_ge(dve_n, at("dve", ph, c, "c0", back=1))
                    turn(ph, c, "ta", ps_t, lambda k: s_a[:, k * 128:k * 128 + 128])
                    pe.wait_ge(act_n, at("act", ph, c, "sb"))
                    pe.wait_ge(dve_n, at("dve", ph, c, "zs" if layer == LAYERS - 1 else "c4", back=1))
                    by_rows(ph, "mb", ps_m, [(s_b, f"ew{layer}")])
                    if layer < LAYERS - 1:
                        pe.wait_ge(dve_n, at("dve", ph, c, "hd"))
                        pe.wait_ge(act_n, at("act", ph, c, "hT", back=1))
                        turn(ph, c, "tr", ps_h, o_blk)
                        pe.wait_ge(act_n, at("act", ph, c, "hT"))
                        pe.wait_ge(act_n, at("act", ph, c, "tab", back=1))
                        by_rows(ph, "mm", ps_o, [(hT, f"lin{layer + 1}")])
                    else:
                        pe.wait_ge(act_n, at("act", ph, c, "m.out"))
                        turn(ph, c, "tr", ps_h, hh_blk)
                        pe.wait_ge(act_n, at("act", ph, c, "hT"))
                        pe.wait_ge(dve_n, at("dve", ph, c, "hn", back=1))
                        by_rows(ph, "mm", ps_o, [(hT, "neigh")])
                        pe.wait_ge(dve_n, at("dve", ph, c, "c4"))
                        by_rows(ph, "mz", ps_m, [(hT, "l1_a")])
                phase_over("pe", ph)

            pe.wait_ge(act_n, end("act", "gcn2"))
            pe.wait_ge(dve_n, end("dve", "gcn2"))

            def edge_half(i, hf, prior):
                if prior:
                    pe.wait_ge(summed, i * 2 + hf)
                pe.wait_ge(eq_s, i * 2 + hf + 3)
                pe.wait_ge(abs_s, i * 2 + hf + 2)
                pe.sem_inc(passed, 1)
                for j in range(H):
                    k = 2048 * hf + 512 * j
                    last = pe.matmul(ps[:, k:k + MS], eq[:, hf, j, :], msg[:, hf * H + j, :], start=True, stop=True)
                last.then_inc(mrg, 1)

            edge_half(0, 0, False)
            edge_half(0, 1, False)
            with pe.Fori(1, ITERS) as i:
                edge_half(i, 0, True)
                edge_half(i, 1, True)

            ph = "sage"
            pe.wait_ge(summed, ITERS * 2 + 1)
            with pe.Fori(0, CH) as c:
                pe.wait_ge(dve_n, at("dve", ph, c, "s2"))
                pe.wait_ge(act_n, at("act", ph, c, "us", back=1))
                turn(ph, c, "ta", ps_t, lambda k: sm[:, 0, k, 0:D])
                pe.wait_ge(dve_n, at("dve", ph, c, "tq", back=1))
                turn(ph, c, "tb", ps_m, lambda k: sm[:, 0, k, D:2 * D])
                pe.wait_ge(act_n, at("act", ph, c, "sb"))
                pe.wait_ge(act_n, at("act", ph, c, "tp", back=1))
                by_rows(ph, "me", ps_o, [(s_a, "edge_a"), (s_b, "edge_b")])
                pe.wait_ge(dve_n, at("dve", ph, c, "c3"))
                turn(ph, c, "tr", ps_h, o_blk)
                pe.wait_ge(act_n, at("act", ph, c, "hT"))
                by_rows(ph, "mz", ps_t, [(hT, "l1_b")])
                pe.wait_ge(act_n, at("act", ph, c, "m.out"))
                turn(ph, c, "tr2", ps_h, hh_blk)
                pe.wait_ge(act_n, at("act", ph, c, "hT2"))
                pe.wait_ge(dve_n, at("dve", ph, c, "c1"))
                by_rows(ph, "mp", ps_o, [(hT, "m1_a")])
                by_rows(ph, "mq", ps_m, [(hT, "m1_b")])
                pe.wait_ge(dve_n, at("dve", ph, c, "z0"))
                for lo, hi in ((0, 512), (512, CW)):
                    last = pe.matmul(ps_t[:, lo:hi], W["u1_a"], hT[:, lo:hi], start=True, stop=True)
                step(ph, "mu", last)
            phase_over("pe", ph)

            pe.wait_ge(act_n, end("act", "sage"))
            pe.wait_ge(dve_n, end("dve", "sage"))

            def through_relu(t):
                relus.enter(t, 1)
                pe.wait_ge(relu, relus.next())

            sum_pass(zf[:, :], through_relu)
            relus.leave(TILES)
            full_n += 1
            pe.wait_ge(full, full_n)
            pe.wait_ge(deg_back, 16)
            ph = "mlp"
            eb = rows[0:1, ROWS.index("b_m2"), :]
            with pe.Fori(0, CH) as c:
                pe.wait_ge(act_n, at("act", ph, c, "sa", back=1))
                for lo, hi in ((0, 512), (512, CW)):
                    pe.matmul(ps_t[:, lo:hi], W["m2"], acc[:, 0, bass.ds(c * CW + lo, hi - lo)], start=True, stop=False)
                    last = pe.matmul(ps_t[:, lo:hi], eb, deg_row[0:1, bass.ds(c * CW + lo, hi - lo)], start=False, stop=True)
                step(ph, "ag", last)
                pe.wait_ge(act_n, at("act", ph, c, "sa"))
                pe.wait_ge(act_n, at("act", ph, c, "zs", back=1))
                for lo, hi in ((0, 512), (512, CW)):
                    last = pe.matmul(ps_m[:, lo:hi], W["u1_b"], s_a[:, lo:hi], start=True, stop=True)
                step(ph, "mu", last)
                pe.wait_ge(act_n, at("act", ph, c, "ur"))
                pe.wait_ge(dve_n, at("dve", ph, c, "y", back=1))
                by_rows(ph, "my", ps_o, [(s_b, "u2")])
                pe.wait_ge(act_n, at("act", ph, c, "m.out"))
                turn(ph, c, "tr", ps_h, hh_blk)
                pe.wait_ge(act_n, at("act", ph, c, "hT"))
                pe.wait_ge(dve_n, at("dve", ph, c, "ua"))
                by_rows(ph, "ml", ps_m, [(hT, "loop")])
            phase_over("pe", ph)

            pe.wait_ge(act_n, end("act", "mlp"))
            pe.wait_ge(dve_n, end("dve", "mlp"))

            def mixed(t):
                mixes.enter(t, 1)
                pe.wait_ge(msg_s, mixes.next())

            mixes.n += TILES
            sum_pass(zf[:, :], mixed)
            mixes.leave(TILES)
            full_n += 1
            pe.wait_ge(full, full_n)
            ph = "rel"
            with pe.Fori(0, CH) as c:
                pe.wait_ge(act_n, at("act", ph, c, "sa"))
                pe.wait_ge(dve_n, at("dve", ph, c, "c0", back=1))
                by_rows(ph, "mn", ps_o, [(s_a, "neighbor")])
            phase_over("pe", ph)


def kernel(**inputs):
    import concourse.bacc as bacc
    from concourse.bass_utils import run_bass_kernel_spmd

    g = {k: np.asarray(v) for k, v in inputs.items()}
    f32 = np.float32

    def edges(a):
        return np.concatenate([a, np.full(TILES * 128 - E, N, a.dtype)])

    x = np.concatenate([g["x"], np.zeros((NP - N, D), f32)]).reshape(NB, 128, D).transpose(1, 0, 2)
    src, dst = edges(g["src"]), edges(g["dst"])
    typ = np.concatenate([g["edge_type_500"], np.zeros(TILES * 128 - E, np.int32)])
    ea = np.concatenate([g["edge_attr_16"], np.zeros((TILES * 128 - E, DE), f32)]).T
    ea = np.concatenate([ea, np.ones((1, TILES * 128), f32)])
    n1, n2 = g["L1_gnn_W_edge"], g["L1_gnn_W_lin"]
    mats = {
        "lin0": g["L0_gnn_lin_w"][0], "lin1": g["L0_gnn_lin_w"][1], "lin2": g["L0_gnn_lin_w"][2],
        "ew0": g["L0_gnn_edge_w2"][0], "ew1": g["L0_gnn_edge_w2"][1], "ew2": g["L0_gnn_edge_w2"][2],
        "neigh": g["L1_gnn_W_neigh"].T, "edge_a": n1[:, :D].T, "edge_b": n1[:, D:].T,
        "l1_a": n2[:, :D].T, "l1_b": n2[:, D:].T,
        "m1_a": g["L2_gnn_w_m1"][:D], "m1_b": g["L2_gnn_w_m1"][D:], "m2": g["L2_gnn_w_m2"],
        "u1_a": g["L2_gnn_w_u1"][:D], "u1_b": g["L2_gnn_w_u1"][D:], "u2": g["L2_gnn_w_u2"],
        "neighbor": g["L3_gnn_W_neighbor"], "loop": g["L3_gnn_loop_weight"],
    }
    vecs = {"b_neigh": g["L1_gnn_b_neigh"], "b_edge": g["L1_gnn_b_edge"], "b_lin": g["L1_gnn_b_lin"],
            "b_m1": g["L2_gnn_b_m1"], "b_m2": g["L2_gnn_b_m2"], "b_u1": g["L2_gnn_b_u1"], "b_u2": g["L2_gnn_b_u2"],
            "gamma": g["L2_gnn_gamma"], "beta": g["L2_gnn_beta"]}
    for k in range(LAYERS):
        vecs |= {f"lnw{k}": g["L0_gnn_ln_w"][k], f"lnb{k}": g["L0_gnn_ln_b"][k], f"bias{k}": g["L0_gnn_bias"][k],
                 f"eb{k}": g["L0_gnn_edge_b2"][k]}
    w1 = np.concatenate([g["L0_gnn_edge_w1"], g["L0_gnn_edge_b1"][:, None, :]], axis=1).transpose(1, 0, 2)
    arrays = {
        "x_in": x, "src_in": src.reshape(TILES, 128).T, "dst_in": dst.reshape(TILES, 128).T,
        "typ_in": typ.reshape(TILES, 128).T, "srcrow_in": src.reshape(1, -1),
        "dstgrp_in": dst.reshape(TILES // H, H * 128), "ea_in": ea,
        "w_in": np.stack([mats[n] for n in WEIGHTS], axis=1), "w1_in": w1,
        "rows_in": np.stack([vecs[n] for n in ROWS]), "cols_in": g["L2_gnn_b_u1"].reshape(D, 1),
        "rel_in": g["L3_gnn_rel_emb"],
    }
    arrays = {k: np.ascontiguousarray(v) for k, v in arrays.items()}
    nc = bacc.Bacc("TRN2", target_bir_lowering=False, num_devices=1)
    args = {k: nc.dram_tensor(k, v.shape, mybir.dt.from_np(v.dtype), kind="ExternalInput").ap() for k, v in arrays.items()}
    out = nc.dram_tensor("out", (NP, D), F32, kind="ExternalOutput").ap()
    build(nc, **args, out=out)
    r = run_bass_kernel_spmd(nc, [arrays], core_ids=[0])
    return r.results[0]["out"][:N]
```

```python
from contextlib import ExitStack

import numpy as np
import concourse.bass as bass
from concourse import mybir

F32 = mybir.dt.float32
I32 = mybir.dt.int32
BF16 = mybir.dt.bfloat16
ALU = mybir.AluOpType
ACT = mybir.ActivationFunctionType
AX = mybir.AxisListType

D = 128
N = 3125
E = 50000
DE = 16
NRELS = 500
LAYERS = 3
EPS = 1e-5

NB = -(-N // 128)
NP = NB * 128
CB = 5
CH = NB // CB
CW = CB * 128
U = 8
H = U // 2
ITERS = -(-E // (128 * U))
TILES = ITERS * U
HALVES = 2 * ITERS
WIN = 128
TB = 4
TR = NRELS // TB
MS = 2 * D + 1
NACC = 4
DUMP = NP

WEIGHTS = ["lin0", "lin1", "lin2", "ew0", "ew1", "ew2", "neigh", "edge_a", "edge_b", "l1_a", "l1_b",
           "m1_a", "m1_b", "m2", "u1_a", "u1_b", "u2", "neighbor", "loop"]
ROWS = ["lnw0", "lnw1", "lnw2", "lnb0", "lnb1", "lnb2", "bias0", "bias1", "bias2", "eb0", "eb1", "eb2",
        "b_neigh", "b_edge", "b_lin", "b_m1", "b_m2", "b_u1", "b_u2", "gamma", "beta"]


class Count:

    def __init__(self, by=1, start=1):
        self.by, self.start, self.n, self.var = by, start, 0, None

    def enter(self, var, per, first=0):
        self.var, self.per, self.first, self.n0 = var, per, first, self.n

    def leave(self, trips):
        assert self.n - self.n0 == self.per, (self.n, self.n0, self.per)
        self.n, self.var = self.n0 + self.per * trips, None

    def next(self, back=0):
        self.n += 1
        return self.now(back)

    def now(self, back=0):
        k = self.start + self.by * (self.n - back)
        if self.var is None:
            return k
        per = self.by * self.per
        return self.var * per + (k - self.first * per)


def build(nc, x_in, src_in, dst_in, typ_in, srcrow_in, dstrow_in, dstgrp_in, ea_in, w_in, w1_in, rows_in, cols_in, rel_in, relblk_in, out):
    ctx = ExitStack()
    with ctx:
        def sb(name, shape, dt=F32):
            return ctx.enter_context(nc.sbuf_tensor(name, shape, dt))

        def sem(name):
            return ctx.enter_context(nc.semaphore(name))

        def dram(name, shape, dt=F32):
            return nc.dram_tensor(name, shape, dt, kind="Internal").ap()

        tab_a, tab_b = dram("tab_a", (NP, D)), dram("tab_b", (NP, D))
        acc_d = [dram(f"acc_d{k}", (NP + 128, MS)) for k in range(NACC)]
        deg_d = dram("deg_d", (NB, 128))
        grp_d = dram("grp_d", (HALVES, 2))

        x = sb("x", [128, NB, D])
        keep = sb("keep", [128, NB, D])
        side = sb("side", [128, NB, D])
        acc = sb("acc", [128, 2, NP])
        wts = sb("wts", [128, len(WEIGHTS), D])
        w1 = sb("w1", [128, LAYERS, D])
        rows = sb("rows", [128, len(ROWS), D])
        bu1_col = sb("bu1_col", [128, 1])
        src_i, dst_i, typ_i = (sb(n, [128, TILES], I32) for n in ("src_i", "dst_i", "typ_i"))
        src_f, dst_f, typ_f = (sb(n, [128, TILES]) for n in ("src_f", "dst_f", "typ_f"))
        iota = sb("iota", [128, NP])
        ident = sb("ident", [128, 128])
        lower = sb("lower", [128, 128])
        dump = sb("dump", [128, 1])
        zeros = sb("zeros", [128, 512])
        deg, dis, norm = sb("deg", [128, NB]), sb("dis", [128, NB]), sb("norm", [128, NB])
        rcnt = sb("rcnt", [128, 2, CB])
        small = sb("small", [128, 6, NB])
        deg_row = sb("deg_row", [1, NP])
        s_a, s_b, hT = sb("s_a", [128, CW]), sb("s_b", [128, CW]), sb("hT", [128, CW])
        o, hh, ta, tb = (sb(n, [128, CB, D]) for n in ("o", "hh", "ta", "tb"))
        stats, mv = sb("stats", [128, CB, 6]), sb("mv", [128, CB, 2])
        lns = sb("lns", [128, 6, CB])
        sm = sb("sm", [128, NACC, CB, MS])
        col = sb("col", [128, 2, 2, H], I32)
        g_a = sb("g_a", [128, U, D])
        msg = sb("msg", [128, U, MS])
        sums = sb("sums", [128, U, MS])
        big = sb("big", [128, NP])
        iota_i = big[:, :].bitcast(I32)
        halves = big[:, 0:3072].rearrange("p (w h j k) -> p w h j k", w=3, h=2, j=H)
        eq = halves[:, 0]
        junk = halves[:, 1]
        srow = big[:, 2048:3072].bitcast(I32).rearrange("p (h k) -> p h k", h=2)
        diff = sb("diff", [128, 2, H, D])
        where_i = sb("where_i", [128, 2, H], I32)
        before = sb("before", [128, 2, H])
        bsel = sb("bsel", [128, 2, 3, H])
        ea_t = sb("ea_t", [128, 128])
        zf = sb("zf", [128, 128])
        grp = sb("grp", [128, 6])
        grp_bc = sb("grp_bc", [128, HALVES, 2])
        base_row, unfit = sb("base_row", [1, HALVES], I32), sb("unfit", [1, 1])
        general = sb("general", [1, 1], I32)
        rel_dst = sb("rel_dst", [128, TILES])
        iota_p = sb("iota_p", [128, 1])
        first_p = sb("first_p", [128, HALVES])
        win = sb("win", [128, 2, D])
        rel_sb = sb("rel_sb", [TR, TB, D])
        oh16 = sb("oh16", [128, 2, H, WIN], BF16)
        oh, zr = halves[:, 0], halves[:, 1]
        ea_r = big[:, 2048:3072].rearrange("p (h k) -> p h k", h=2)
        smf = sm[:, :, :, :].rearrange("p a b c -> p (a b c)")
        lo_f, hi_f = smf[:, 0:TILES], smf[:, TILES:2 * TILES]
        lo_i, hi_i = smf[:, 2 * TILES:3 * TILES].bitcast(I32), smf[:, 3 * TILES:4 * TILES].bitcast(I32)
        oh_lo = smf[:, 1600:1600 + U * 64].bitcast(BF16).rearrange("p (u k) -> p u k", u=U)
        oh_hi = smf[:, 2112:2112 + U * NB // 2].bitcast(BF16).rearrange("p (u k) -> p u k", u=U)
        grp_i, grp_f = smf[0:HALVES, 2304:2816].bitcast(I32), smf[0:HALVES, 2816:3328]
        drow = smf[:, 0:1024].bitcast(I32).rearrange("p (h k) -> p h k", h=2)
        ohT = smf[:, 1024:2048].rearrange("p (h k) -> p h k", h=2)
        cnts = smf[0:TR, 2048:3072].rearrange("p (h b k) -> p h b k", h=2, b=TB)
        oh_typ = smf[:, 3072:3072 + H * NRELS].bitcast(BF16).rearrange("p (h j k) -> p h j k", h=2, j=H)

        ps = ctx.enter_context(nc.psum_tensor("ps", [128, 4096], F32))
        ps_t, ps_m, ps_h, ps_o = (ps[:, 1024 * k:1024 * k + CW] for k in range(4))

        in_small, in_x, in_w, zeroed = sem("in_small"), sem("in_x"), sem("in_w"), sem("zeroed")
        deg_out, deg_back, out_done = sem("deg_out"), sem("deg_back"), sem("out_done")
        store, sm_in = sem("store"), sem("sm_in")
        ga_in = [sem(f"ga_in{r}") for r in range(U)]
        gb_in = [sem(f"gb_in{r}") for r in range(U)]
        added = [sem(f"added{k}") for k in range(NACC)]
        srow_in = [sem(f"srow_in{k}") for k in range(2)]
        ea_in_s = sem("ea_in_s")
        grp_out, grp_back = sem("grp_out"), sem("grp_back")
        fa_in = [sem(f"fa_in{r}") for r in range(U)]
        ea_h = [sem(f"ea_h{k}") for k in range(2)]
        drow_in = [sem(f"drow_in{k}") for k in range(2)]
        win_in = [sem(f"win_in{k}") for k in range(2)]
        flag_made = sem("flag_made")
        passed = sem("passed")
        stored = sem("stored")
        consts = sem("consts")
        dve_c = sem("dve_c")
        act_c = sem("act_c")
        acc_clear = sem("acc_clear")
        pool_c = sem("pool_c")
        hot = sem("hot")
        deg_mm = sem("deg_mm")
        seg = sem("seg")
        ps_full = sem("ps_full")
        zmm = sem("zmm")
        relu = sem("relu")
        msg_s = sem("msg_s")
        full = sem("full")
        pe_n = sem("pe_n")
        act_n = sem("act_n")
        dve_n = sem("dve_n")
        eq_s, diff_s, abs_s, mrg, summed, where = (sem(n) for n in ("eq_s", "diff_s", "abs_s", "mrg", "summed", "where"))

        W = {n: wts[:, k, :] for k, n in enumerate(WEIGHTS)}

        def row(name, blocks=CB):
            k = ROWS.index(name)
            return rows[:, k:k + 1, :].to_broadcast([128, blocks, D])

        def row1(name):
            return rows[:, ROWS.index(name), :]

        def blk(c):
            return bass.ds(c * CB, CB)

        def nodes(c):
            return bass.ds(c * CW, CW)


        side_fm = side[:, :, :].rearrange("p b f -> p (b f)")
        tab_rows = {t: d.rearrange("(b p) f -> p b f", p=128) for t, d in (("a", tab_a), ("b", tab_b))}
        out_rows = out.rearrange("(b p) f -> p b f", p=128)
        ps_z = ps[:, 3584:3712]
        BANKS = [(k, min(512, NP - k)) for k in range(0, NP, 512)]

        def ln_dve(t):
            return [t + "." + k for k in ("st", "mv", "ve", "r0", "r1", "r2", "r3", "r4", "co")]

        def ln_act(t):
            return [t + ".sd", t + ".out"]

        def gcn(last):
            return {
                "pe": ["ta", "mb", "tr"] + (["mm", "mz"] if last else ["mm"]),
                "act": ["sa", "sb"] + ln_act("n") + (ln_act("m") + ["hT"] if last else ["hT", "tab"]),
                "dve": ["c0", "c1", "c2", "c3", "c4"] + ln_dve("n") + ["w", "b"]
                + (["xn", "xw"] + ln_dve("m") + ["hn", "kp", "zs"] if last else ["hd"]),
            }

        STEPS = {
            "start": {"pe": ["tr", "mm"], "act": ln_act("m") + ["hT", "tab"], "dve": ["xc"] + ln_dve("m") + ["hd"]},
            "gcn0": gcn(False), "gcn1": gcn(False), "gcn2": gcn(True),
            "sage": {
                "pe": ["ta", "tb", "me", "tr", "mz", "tr2", "mp", "mq", "mu"],
                "act": ["sa", "sb", "hT"] + ln_act("m") + ["hT2", "tp", "us"],
                "dve": ["s0", "s1", "s2", "cn", "rc", "c0", "c1", "c2", "c3", "z0", "xn", "xw"] + ln_dve("m")
                + ["kp", "tq"],
            },
            "mlp": {
                "pe": ["ag", "mu", "my", "tr", "ml"],
                "act": ["sa", "ur"] + ln_act("n") + ln_act("m") + ["hT", "zs"],
                "dve": ["ua", "y"] + ln_dve("n") + ["w", "b", "hb", "xn", "xw"] + ln_dve("m"),
            },
            "rel": {"pe": ["mn"], "act": ["sa"], "dve": ["c0", "c1", "c2"]},
        }
        PHASES = list(STEPS)
        STEP0 = 32
        done_in = {e: [] for e in ("pe", "act", "dve")}

        def at(e, ph, c, name, back=0):
            names = STEPS[ph][e]
            before = sum(CH * len(STEPS[p][e]) for p in PHASES[:PHASES.index(ph)])
            return c * len(names) + (STEP0 + before + names.index(name) + 1 - back * len(names))

        def end(e, ph):
            return at(e, ph, CH - 1, STEPS[ph][e][-1])

        step_sem = {"pe": pe_n, "act": act_n, "dve": dve_n}

        def tick(e, ph, name, ins):
            assert name == STEPS[ph][e][len(done_in[e]) % len(STEPS[ph][e])], (e, ph, name)
            done_in[e].append(name)
            ins.then_inc(step_sem[e], 1)

        def phase_over(e, ph):
            assert done_in[e] == STEPS[ph][e], (e, ph)
            done_in[e].clear()

        STORES = {"start": 1, "gcn0": 1, "gcn1": 1, "gcn2": 1, "sage": 2, "mlp": 1, "rel": 1}

        def stored_at(ph, c, k=0, back=0):
            before = sum(CH * STORES[p] for p in PHASES[:PHASES.index(ph)])
            return c * STORES[ph] + (1 + before + k + 1 - back * STORES[ph])

        def all_stored(ph):
            return stored_at(ph, CH - 1, STORES[ph] - 1)

        GRP_CHAIN = 10
        DEG_CHAIN = 23
        DEG_READY = DEG_CHAIN

        PASSES = ["gcn0", "gcn1", "gcn2", "sage", "mlp", "rel"]
        GCN = PASSES[0:3]
        PASSES_ADDING = [p for p in PASSES if p != "sage"]
        USED_IN = {
            "oh_made": GCN + ["mlp", "rel"],
            "z_made": GCN + ["sage", "mlp"],
            "relu_made": GCN + ["mlp"],
            "seg_made": GCN + ["mlp", "rel"],
            "win_added": GCN + ["mlp", "rel"],
            "ohT_made": ["sage", "mlp"],
            "mix_made": ["mlp"],
            "own_out": ["sage"],
            "typ_made": ["rel"],
            "cnt_made": ["rel"],
            "cnt_out": ["rel"],
        }
        half_sem = {n: sem(n) for n in USED_IN}

        def half(name, p, i, hf, back=0):
            return i * 2 + (hf + HALVES * USED_IN[name].index(p) + 3 - back)

        def dma_half(p, passes, i):
            return i * 16 + 16 * (ITERS * passes.index(p) + 1)

        def after_half(i, hf):
            return (i, 1) if hf == 0 else (i + 1, 0)

        ps_w = [ps[:, 1024 * k:1024 * k + 1024].rearrange("p (a k) -> p a k", a=2)[:, :, 0:WIN] for k in range(2)]
        ps_zh = [ps[:, 2048 + 512 * k:2560 + 512 * k] for k in range(2)]
        ps_c = [ps[0:TR, 3072 + 512 * k:3584 + 512 * k] for k in range(2)]

        def is_general(eng):
            eng.wait_ge(flag_made, 1)
            return eng.value_load(general[0:1, 0:1], min_val=0, max_val=1)

        def three_parts(eng, body):
            body(0, True, False)
            with eng.Fori(1, ITERS - 1) as i:
                body(i, False, False)
            body(ITERS - 1, False, True)

        def iterations(eng, body):
            with eng.Fori(0, ITERS - 1) as i:
                body(i, False)
            body(ITERS - 1, True)

        block = ctx.enter_context(nc.Block())

        @block.sync
        def _(sp):
            sp.sem_inc(stored, 1)
            sp.dma_start(grp_i, dstgrp_in).then_inc(in_small, 16)
            for k, (dst, src) in enumerate(((src_i, src_in), (dst_i, dst_in), (typ_i, typ_in))):
                sp.dma_start(dst[:, :], src).then_inc(in_small, 16)
            sp.dma_start(x[:, :, :], x_in).then_inc(in_x, 16)
            sp.dma_start(wts[:, :, :], w_in).then_inc(in_w, 16)
            sp.wait_ge(dve_c, 2)
            sp.dma_start(w1[0:DE + 1, :, :], w1_in).then_inc(in_w, 16)
            sp.dma_start(rows[:, :, :], rows_in.unsqueeze(0).to_broadcast([128, len(ROWS), D])).then_inc(in_w, 16)
            sp.dma_start(bu1_col[:, :], cols_in).then_inc(in_w, 16)
            sp.dma_start(rel_sb[:, :, :], relblk_in).then_inc(in_w, 16)
            sp.wait_ge(dve_c, GRP_CHAIN)
            sp.dma_start(grp_d, grp[0:HALVES, 2:4]).then_inc(grp_out, 16)
            sp.wait_ge(grp_out, 16)
            sp.dma_start(grp_bc[:, :, :], grp_d.unsqueeze(0).to_broadcast([128, HALVES, 2])).then_inc(grp_back, 16)
            for k in range(NACC):
                flat = acc_d[k].rearrange("(b p) f -> p b f", p=128)
                for b in range(NB + 1):
                    sp.dma_start(flat[:, b, :], zeros[:, 0:MS]).then_inc(zeroed, 16)
            sp.wait_ge(dve_c, DEG_READY)
            sp.dma_start(deg_d.rearrange("b p -> p b"), deg[:, :], allow_slow_non_contiguous=True).then_inc(deg_out, 16)
            sp.wait_ge(deg_out, 16)
            sp.dma_start(deg_row[:, :], deg_d.rearrange("(a b) p -> a (b p)", a=1)).then_inc(deg_back, 16)

            def store_table(ph, dst, src, e, name):
                with sp.Fori(0, CH) as c:
                    sp.wait_ge(step_sem[e], at(e, ph, c, name))
                    sp.dma_start(dst[:, blk(c), :], src[:, :, :]).then_inc(store, 16)
                    sp.wait_ge(store, (stored_at(ph, c) - 1) * 16)
                    sp.sem_inc(stored, 1)

            zc = Count()

            def load_ea(layer):
                with sp.Fori(0, TILES) as t:
                    zc.enter(t, 1)
                    sp.wait_ge(zmm, zc.next(back=1))
                    sp.dma_start(ea_t[0:DE + 1, :], ea_in[:, bass.ds(t * 128, 128)]).then_inc(ea_in_s, 16)
                zc.leave(TILES)

            def load_ea_halves(p):
                def body(i, last):
                    for hf in range(2):
                        sp.wait_ge(half_sem["z_made"], half("z_made", p, i, hf, back=2))
                        sp.dma_start(ea_r[0:DE + 1, hf, :], ea_in[:, bass.ds((i * U + hf * H) * 128, H * 128)])\
                          .then_inc(ea_h[hf], 16)
                iterations(sp, body)

            def load_windows(p):
                table = tab_a if p == "sage" else tab_b

                def body(i, last):
                    _, first = nc.values_load_multi_w_load_instructions(
                        base_row[0:1, bass.ds(i * 2, 2)], engines=[mybir.EngineType.SP], min_val=0, max_val=NP - WIN)
                    for hf in range(2):
                        tile = i * U + hf * H
                        sp.wait_ge(half_sem["ohT_made"], half("ohT_made", p, i, hf, back=2))
                        sp.dma_start(drow[:, hf, :], dstrow_in[:, bass.ds(tile * 128, H * 128)]
                                     .to_broadcast([128, H * 128])).then_inc(drow_in[hf], 16)
                        sp.wait_ge(half_sem["z_made"], half("z_made", p, i, hf, back=2))
                        sp.dma_start(win[:, hf, :], table[bass.ds(first[hf], WIN), :]).then_inc(win_in[hf], 16)
                        if p == "sage":
                            load_srow(i, hf)
                iterations(sp, body)

            def load_srow(i, hf):
                tile = i * U + hf * H
                sp.wait_ge(eq_s, i * 2 + (hf + 1))
                sp.dma_start(srow[:, hf, :], srcrow_in[:, bass.ds(tile * 128, H * 128)]
                             .to_broadcast([128, H * 128])).then_inc(srow_in[hf], 16)

            store_table("start", tab_rows["a"], tb, "act", "tab")
            unfitting = is_general(sp)
            for layer in range(LAYERS):
                with sp.If(unfitting == 0):
                    load_ea_halves(f"gcn{layer}")
                with sp.Else():
                    load_ea(layer)
                if layer < LAYERS - 1:
                    store_table(f"gcn{layer}", tab_rows["a"], tb, "act", "tab")
            store_table("gcn2", tab_rows["a"], ta, "dve", "hn")

            with sp.If(unfitting == 0):
                load_windows("sage")
            with sp.Else():
                with sp.Fori(0, ITERS) as i:
                    for hf in range(2):
                        load_srow(i, hf)

            for k in range(NACC):
                sp.wait_ge(added[k], 32 * ITERS)
            with sp.Fori(0, CH) as c:
                sp.wait_ge(pe_n, at("pe", "sage", c, "tb", back=1))
                sp.wait_ge(dve_n, at("dve", "sage", c, "c0", back=1))
                for k in range(NACC):
                    sp.dma_start(sm[:, k, :, :], acc_d[k].rearrange("(b p) f -> p b f", p=128)[:, blk(c), :]).then_inc(sm_in, 16)
                for k, (e, name, dst, src) in enumerate((("act", "tp", "a", tb), ("dve", "tq", "b", ta))):
                    sp.wait_ge(step_sem[e], at(e, "sage", c, name))
                    sp.dma_start(tab_rows[dst][:, blk(c), :], src[:, :, :]).then_inc(store, 16)
                    sp.wait_ge(store, (stored_at("sage", c, k) - 1) * 16)
                    sp.sem_inc(stored, 1)

            with sp.If(unfitting == 0):
                load_windows("mlp")
            with sp.Else():
                sp.sem_inc(passed, 1)
            store_table("mlp", tab_rows["a"], hh, "act", "m.out")
            store_table("rel", out_rows, tb, "dve", "c2")
            sp.wait_ge(store, (all_stored("rel") - 1) * 16)


        @block.gpsimd
        def _(pool):
            pool.sem_inc(pool_c, 1)
            pool.iota(iota_i[:, :], pattern=[[1, NP]], base=0, channel_multiplier=0).then_inc(consts, 1)
            pool.memset(ident[:, :], 0.0).then_inc(consts, 1)
            pool.memset(lower[:, :], 1.0).then_inc(consts, 1)
            pool.wait_ge(consts, 3)
            pool.tensor_copy(iota[:, :], iota_i[:, :]).then_inc(consts, 1)
            pool.affine_select(out=ident[:, :], in_=ident[:, :], compare_op=ALU.not_equal, fill=1.0, base=0,
                               pattern=[[-1, 128]], channel_multiplier=1).then_inc(consts, 1)
            pool.affine_select(out=lower[:, :], in_=lower[:, :], compare_op=ALU.is_gt, fill=0.0, base=0,
                               pattern=[[-1, 128]], channel_multiplier=1).then_inc(consts, 1)
            pool.wait_ge(consts, 4)
            pool.iota(iota_i[:, 0:1], pattern=[[1, 1]], base=DUMP, channel_multiplier=1).then_inc(consts, 1)
            pool.wait_ge(consts, 7)
            pool.tensor_copy(dump[:, :], iota_i[:, 0:1]).then_inc(consts, 1)
            pool.wait_ge(consts, 8)
            pool.iota(iota_i[:, 0:1], pattern=[[1, 1]], base=0, channel_multiplier=1).then_inc(consts, 1)
            pool.wait_ge(consts, 9)
            pool.tensor_copy(iota_p[:, :], iota_i[:, 0:1]).then_inc(consts, 1)
            pool.wait_ge(in_small, 64)

            copies, segs = Count(), Count()

            def gather(g, table, index, signal):
                pool.indirect_dma_start(g, None, table, bass.IndirectOffsetOnAxis(ap=index, axis=0)).then_inc(signal, 16)

            def gather_pass(ph, second):
                pool.wait_ge(stored, all_stored(ph))
                with pool.Fori(0, TILES) as t:
                    copies.enter(t, 2)
                    segs.enter(t, 1)
                    pool.wait_ge(seg, segs.next(back=1))
                    pool.tensor_copy(col[:, 0, 0, 0:1], src_i[:, bass.ds(t, 1)]).then_inc(pool_c, 1)
                    other = src_i if second is None else second[1]
                    copies.next()
                    pool.tensor_copy(col[:, 0, 1, 0:1], other[:, bass.ds(t, 1)]).then_inc(pool_c, 1)
                    pool.wait_ge(pool_c, copies.next())
                    pool.sem_inc(passed, 1)
                    gather(g_a[:, 0, :], tab_a, col[:, 0, 0, 0:1], ga_in[0])
                    if second is not None:
                        gather(msg[:, 0, 0:D], second[0], col[:, 0, 1, 0:1], gb_in[0])
                copies.leave(TILES)
                segs.leave(TILES)

            def gather_half(p, i, hf, free):
                free(i, hf)
                pool.tensor_copy(col[:, hf, 0, :], src_i[:, bass.ds(i * U + hf * H, H)]).then_inc(pool_c, 1)
                pool.wait_ge(pool_c, i * 2 + (hf + HALVES * PASSES.index(p) + 2))
                pool.sem_inc(passed, 1)
                for j in range(H):
                    gather(g_a[:, hf * H + j, :], tab_a, col[:, hf, 0, j:j + 1], fa_in[hf * H + j])

            def gather_windows(p, ph):
                pool.wait_ge(stored, all_stored(ph))
                reader = {"mlp": "mix_made"}.get(p, "seg_made")

                def free(i, hf):
                    pool.wait_ge(half_sem[reader], half(reader, p, i, hf, back=2))

                def body(i, last):
                    for hf in range(2):
                        gather_half(p, i, hf, free)
                iterations(pool, body)

            unfitting = is_general(pool)
            for layer in range(LAYERS):
                ph = ("start", "gcn0", "gcn1")[layer]
                with pool.If(unfitting == 0):
                    gather_windows(f"gcn{layer}", ph)
                with pool.Else():
                    gather_pass(ph, None)
                    segs.n += TILES

            pool.wait_ge(stored, all_stored("gcn2"))
            pool.wait_ge(zeroed, 16 * NACC * (NB + 1))

            def gathers(i, hf, first):
                r0, tile = hf * H, i * U + hf * H
                if not first:
                    pool.wait_ge(mrg, i * 2 + hf - 1 + 1)
                pool.tensor_copy(col[:, hf, 0, :], src_i[:, bass.ds(tile, H)]).then_inc(pool_c, 1)
                copies.next()
                pool.tensor_copy(col[:, hf, 1, :], dst_i[:, bass.ds(tile, H)]).then_inc(pool_c, 1)
                pool.wait_ge(pool_c, copies.next())
                pool.sem_inc(passed, 1)
                for j in range(H):
                    gather(g_a[:, r0 + j, :], tab_a, col[:, hf, 0, j:j + 1], ga_in[r0 + j])
                    gather(msg[:, r0 + j, 0:D], tab_a, col[:, hf, 1, j:j + 1], gb_in[r0 + j])

            def scatters(i, hf, first=False):
                pool.wait_ge(where, i * 2 + hf + 2)
                pool.wait_ge(summed, i * 2 + hf + 2)
                for j in range(H):
                    if not first:
                        pool.wait_ge(added[j], i * 32 + 16 * hf)
                    pool.sem_inc(passed, 1)
                    pool.indirect_dma_start(acc_d[j], bass.IndirectOffsetOnAxis(ap=where_i[:, hf, j:j + 1], axis=0),
                                            sums[:, hf * H + j, :], None, compute_op=ALU.add).then_inc(added[j], 16)

            def diffs_done(i, hf):
                pool.wait_ge(diff_s, i * 2 + hf)

            with pool.If(unfitting == 0):
                gather_half("sage", 0, 0, lambda i, hf: None)
                gather_half("sage", 0, 1, lambda i, hf: None)
                scatters(0, 0, True)
                with pool.Fori(1, ITERS) as i:
                    gather_half("sage", i, 0, diffs_done)
                    scatters(i - 1, 1)
                    gather_half("sage", i, 1, diffs_done)
                    scatters(i, 0)
                scatters(ITERS - 1, 1)
            with pool.Else():
                gathers(0, 0, True)
                gathers(0, 1, True)
                scatters(0, 0, True)
                with pool.Fori(1, ITERS) as i:
                    copies.enter(i, 4, 1)
                    gathers(i, 0, False)
                    scatters(i - 1, 1)
                    gathers(i, 1, False)
                    scatters(i, 0)
                copies.leave(ITERS - 1)
                scatters(ITERS - 1, 1)

            for p, ph, second in (("mlp", "sage", (tab_b, dst_i)), ("rel", "mlp", (rel_in, typ_i))):
                with pool.If(unfitting == 0):
                    gather_windows(p, ph)
                with pool.Else():
                    gather_pass(ph, second)

        @block.vector
        def _(dve):
            dve.sem_inc(hot, 1)
            dve.sem_inc(eq_s, 2)
            dve.sem_inc(dve_n, STEP0)
            dve.sem_inc(msg_s, 1)
            for n in ("oh_made", "win_added", "ohT_made", "mix_made", "typ_made"):
                dve.sem_inc(half_sem[n], 2)
            for q in (diff_s, where):
                dve.sem_inc(q, 1)
            chain = Count(start=0)

            def link(ins):
                ins.then_inc(dve_c, 1)
                dve.wait_ge(dve_c, chain.next())

            link(dve.memset(zeros[:, :], 0.0))
            link(dve.memset(w1[:, :, :], 0.0))
            link(dve.memset(ea_t[:, :], 0.0))
            link(dve.memset(msg[:, :, 2 * D:], 1.0))
            dve.wait_ge(in_small, 64)
            dve.wait_ge(consts, 10)
            link(dve.tensor_copy(grp_f, grp_i))
            link(dve.tensor_reduce(grp[0:HALVES, 0:1], grp_f, AX.X, ALU.min))
            link(dve.tensor_reduce(grp[0:HALVES, 1:2], grp_f, AX.X, ALU.max))
            link(dve.tensor_scalar(grp[0:HALVES, 2:3], grp[0:HALVES, 0:1], float(NP - WIN), None, ALU.min))
            link(dve.tensor_tensor(grp[0:HALVES, 4:5], grp[0:HALVES, 1:2], grp[0:HALVES, 2:3], ALU.subtract))
            link(dve.tensor_scalar(grp[0:HALVES, 3:4], grp[0:HALVES, 4:5], float(WIN - 1), None, ALU.is_gt))
            assert chain.n == GRP_CHAIN
            link(dve.tensor_copy(src_f[:, :], src_i[:, :]))
            link(dve.tensor_copy(dst_f[:, :], dst_i[:, :]))
            link(dve.tensor_copy(typ_f[:, :], typ_i[:, :]))
            link(dve.tensor_scalar(lo_i[:, :], dst_i[:, :], 127, None, ALU.bitwise_and))
            link(dve.tensor_scalar(hi_i[:, :], dst_i[:, :], 7, None, ALU.logical_shift_right))
            link(dve.tensor_copy(lo_f[:, :], lo_i[:, :]))
            link(dve.tensor_copy(hi_f[:, :], hi_i[:, :]))

            dve.wait_ge(grp_back, 16)
            link(dve.tensor_copy(base_row[:, :], grp_bc[0:1, :, 0]))
            link(dve.tensor_reduce(unfit[:, :], grp_bc[0:1, :, 1], AX.X, ALU.max))
            link(dve.tensor_copy(general[:, :], unfit[:, :]))
            link(dve.tensor_tensor(rel_dst[:, :].rearrange("p (g h) -> p g h", h=H),
                                   dst_f[:, :].rearrange("p (g h) -> p g h", h=H),
                                   grp_bc[:, :, 0:1].to_broadcast([128, HALVES, H]), ALU.subtract))
            link(dve.tensor_scalar(first_p[:, :], grp_bc[:, :, 0], iota_p[:, 0:1], None, ALU.add))
            dve.sem_inc(flag_made, 1)

            hots = Count()
            with dve.Fori(0, ITERS) as i:
                dve.wait_ge(deg_mm, i + 1)
                for hot_rows, part, width in ((oh_lo, lo_f, 128), (oh_hi, hi_f, NB)):
                    dve.tensor_tensor(hot_rows[:, :, :], iota[:, 0:width].unsqueeze(1).to_broadcast([128, U, width]),
                                      part[:, bass.ds(i * U, U)].unsqueeze(2).to_broadcast([128, U, width]),
                                      ALU.is_equal).then_inc(hot, 1)
            hots.n += 2 * ITERS
            dve.wait_ge(deg_mm, ITERS + 2)
            link(dve.tensor_copy(deg[:, :], ps[:, 0:NB]))
            link(dve.tensor_scalar(small[:, 0, :], deg[:, :], 1.0, None, ALU.max))
            chain_sq = chain.n
            dve.wait_ge(act_c, 1)
            link(dve.reciprocal(small[:, 2, :], small[:, 1, :]))
            link(dve.tensor_tensor(small[:, 3, :], small[:, 2, :], small[:, 2, :], ALU.mult))
            link(dve.tensor_tensor(small[:, 3, :], small[:, 3, :], small[:, 0, :], ALU.mult))
            link(dve.tensor_scalar(small[:, 3, :], small[:, 3, :], -0.5, 1.5, ALU.mult, ALU.add))
            link(dve.tensor_tensor(norm[:, :], small[:, 2, :], small[:, 3, :], ALU.mult))
            link(dve.tensor_scalar(small[:, 4, :], deg[:, :], 0.0, None, ALU.is_gt))
            link(dve.tensor_tensor(dis[:, :], norm[:, :], small[:, 4, :], ALU.mult))
            assert chain.n == DEG_CHAIN + 8 and chain_sq == DEG_CHAIN + 1, (chain.n, chain_sq)

            dve.wait_ge(in_x, 16)
            dve.wait_ge(in_w, 80)

            def step(ph, name, ins):
                tick("dve", ph, name, ins)

            def after(ph, c, name):
                dve.wait_ge(dve_n, at("dve", ph, c, name))

            def ln(ph, c, t, src):
                for k in range(CB):
                    last = dve.bn_stats(stats[:, k, :], src[:, k, :])
                step(ph, t + ".st", last)
                after(ph, c, t + ".st")
                dve.sem_inc(passed, 1)
                for k in range(CB):
                    last = dve.bn_aggr(mv[:, k, :], stats[:, k, :])
                step(ph, t + ".mv", last)
                after(ph, c, t + ".mv")
                step(ph, t + ".ve", dve.tensor_scalar(lns[:, 0, :], mv[:, :, 1], EPS, None, ALU.add))
                dve.wait_ge(act_n, at("act", ph, c, t + ".sd"))
                step(ph, t + ".r0", dve.reciprocal(lns[:, 2, :], lns[:, 1, :]))
                after(ph, c, t + ".r0")
                step(ph, t + ".r1", dve.tensor_tensor(lns[:, 3, :], lns[:, 2, :], lns[:, 2, :], ALU.mult))
                after(ph, c, t + ".r1")
                step(ph, t + ".r2", dve.tensor_tensor(lns[:, 3, :], lns[:, 3, :], lns[:, 0, :], ALU.mult))
                after(ph, c, t + ".r2")
                step(ph, t + ".r3", dve.tensor_scalar(lns[:, 3, :], lns[:, 3, :], -0.5, 1.5, ALU.mult, ALU.add))
                after(ph, c, t + ".r3")
                step(ph, t + ".r4", dve.tensor_tensor(lns[:, 4, :], lns[:, 2, :], lns[:, 3, :], ALU.mult))
                after(ph, c, t + ".r4")
                step(ph, t + ".co", dve.scalar_tensor_tensor(out=lns[:, 5, :], in0=mv[:, :, 0], scalar=-1.0,
                                                             in1=lns[:, 4, :], op0=ALU.mult, op1=ALU.mult))

            def per_node(v, c):
                return v[:, blk(c)].unsqueeze(2).to_broadcast([128, CB, D])

            def psv(p):
                return p.rearrange("p (b f) -> p b f", f=D)

            def affine(ph, c, w, b):
                dve.wait_ge(act_n, at("act", ph, c, "n.out"))
                step(ph, "w", dve.tensor_tensor(hh[:, :, :], hh[:, :, :], row(w), ALU.mult))
                after(ph, c, "w")
                step(ph, "b", dve.tensor_tensor(hh[:, :, :], hh[:, :, :], row(b), ALU.add))
                after(ph, c, "b")

            def add_to_x(ph, c, src):
                after(ph, c, "xn")
                step(ph, "xw", dve.tensor_scalar(x[:, blk(c), :], src[:, :, :], 1.0, None, ALU.mult))

            ph = "start"
            with dve.Fori(0, CH) as c:
                dve.wait_ge(act_n, at("act", ph, c, "m.out", back=1))
                step(ph, "xc", dve.tensor_scalar(ta[:, :, :], x[:, blk(c), :], 1.0, None, ALU.mult))
                after(ph, c, "xc")
                ln(ph, c, "m", ta)
                dve.wait_ge(act_n, at("act", ph, c, "m.out"))
                dve.wait_ge(pe_n, at("pe", ph, c, "tr", back=1))
                step(ph, "hd", dve.tensor_tensor(o[:, :, :], hh[:, :, :], per_node(dis, c), ALU.mult))
            phase_over("dve", ph)

            def one_hot_pass(mix=None):
                with dve.Fori(0, TILES) as t:
                    hots.enter(t, 1)
                    segs.enter(t, 1)
                    dve.wait_ge(seg, segs.next(back=1))
                    dve.tensor_scalar(big[:, :], iota[:, :], dst_f[:, bass.ds(t, 1)], None, ALU.is_equal).then_inc(hot, 1)
                    hots.next()
                    if mix is not None:
                        mixes.enter(t, 1)
                        loads.enter(t, 1)
                        dve.wait_ge(ga_in[0], loads.next())
                        dve.wait_ge(gb_in[0], 16 * t + 16 * mix[1])
                        dve.tensor_tensor(mix[0], g_a[:, 0, :], msg[:, 0, 0:D], ALU.add).then_inc(msg_s, 1)
                        mixes.next()
                hots.leave(TILES)
                segs.leave(TILES)
                if mix is not None:
                    mixes.leave(TILES)
                    loads.leave(TILES)

            segs, mixes, loads = Count(), Count(), Count(by=16, start=0)
            unfitting = is_general(dve)

            def bases(i, first, last):
                start, n = (0, 1) if first else (i * 2 - 1, 3 if last else 2)
                _, values = nc.values_load_multi_w_load_instructions(
                    base_row[0:1, bass.ds(start, n)], engines=[mybir.EngineType.DVE], min_val=0, max_val=NP - WIN)
                return ([None] if first else []) + list(values)

            def one_hot_half(p, i, hf):
                dve.wait_ge(half_sem["seg_made"], half("seg_made", p, i, hf, back=2))
                dve.tensor_tensor(oh[:, hf, :, :], iota[:, 0:WIN].unsqueeze(1).to_broadcast([128, H, WIN]),
                                  rel_dst[:, bass.ds(i * U + hf * H, H)].unsqueeze(2).to_broadcast([128, H, WIN]),
                                  ALU.is_equal).then_inc(half_sem["oh_made"], 1)

            def one_hot_T_half(p, i, hf):
                dve.wait_ge(drow_in[hf], dma_half(p, ["sage", "mlp"], i))
                dve.wait_ge(half_sem["z_made"], half("z_made", p, i, hf, back=2))
                dve.tensor_scalar(ohT[:, hf, :], drow[:, hf, :], first_p[:, bass.ds(i * 2 + hf, 1)], None, ALU.is_equal)\
                   .then_inc(half_sem["ohT_made"], 1)

            def add_window(p, i, hf, first, parts):
                dve.wait_ge(half_sem["seg_made"], half("seg_made", p, i, hf))
                dve.wait_ge(half_sem["win_added"], half("win_added", p, i, hf, back=1))
                there = acc[:, 0:parts, bass.ds(first, WIN)]
                dve.tensor_tensor(there, there, ps_w[hf][:, 0:parts, :], ALU.add).then_inc(half_sem["win_added"], 1)


            def nothing(*_):
                pass

            def window_pass(p, parts, readers=nothing, ahead=nothing, this=nothing, with_hot=nothing):
                readers()
                dve.memset(acc[:, 0:parts, :], 0.0).then_inc(acc_clear, 1)
                ahead(p, 0, 0)
                one_hot_half(p, 0, 0)
                with_hot(p, 0, 0)
                dve.wait_ge(acc_clear, PASSES_ADDING.index(p) + 1)

                def body(i, first, last):
                    start = bases(i, first, last)
                    for hf in range(2):
                        end_of_pass = last and hf
                        if not end_of_pass:
                            ahead(p, *after_half(i, hf))
                        this(p, i, hf)
                        if not (first and hf == 0):
                            add_window(p, *((i - 1, 1) if hf == 0 else (i, 0)), start[hf], parts)
                        if not end_of_pass:
                            one_hot_half(p, *after_half(i, hf))
                            with_hot(p, *after_half(i, hf))
                    if last:
                        add_window(p, i, 1, start[2], parts)
                three_parts(dve, body)

            def mix_half(p, i, hf):
                for j in range(H):
                    dve.wait_ge(fa_in[hf * H + j], dma_half(p, PASSES, i))
                dve.wait_ge(half_sem["z_made"], half("z_made", p, i, hf))
                dve.wait_ge(half_sem["relu_made"], half("relu_made", p, i, hf, back=2))
                dve.tensor_tensor(diff[:, hf, :, :], g_a[:, hf * H:hf * H + H, :],
                                  ps_zh[hf].rearrange("p (j f) -> p j f", j=H), ALU.add)\
                   .then_inc(half_sem["mix_made"], 1)

            def types_half(p, i, hf):
                dve.wait_ge(half_sem["cnt_made"], half("cnt_made", p, i, hf, back=2))
                dve.tensor_tensor(oh_typ[:, hf, :, :], iota[:, 0:NRELS].unsqueeze(1).to_broadcast([128, H, NRELS]),
                                  typ_f[:, bass.ds(i * U + hf * H, H)].unsqueeze(2).to_broadcast([128, H, NRELS]),
                                  ALU.is_equal)

            def narrow_half(p, i, hf):
                dve.wait_ge(half_sem["cnt_made"], half("cnt_made", p, i, hf, back=2))
                dve.wait_ge(half_sem["oh_made"], half("oh_made", p, i, hf))
                dve.tensor_copy(oh16[:, hf, :, :], oh[:, hf, :, :]).then_inc(half_sem["typ_made"], 1)

            for layer in range(LAYERS):
                ph = f"gcn{layer}"
                loads.n += TILES
                with dve.If(unfitting == 0):
                    window_pass(f"gcn{layer}", 2, nothing if layer == 0 else
                                lambda: dve.wait_ge(act_n, end("act", f"gcn{layer - 1}")))
                with dve.Else():
                    one_hot_pass()
                    one_hot_pass()
                with dve.Fori(0, CH) as c:
                    dve.wait_ge(pe_n, at("pe", ph, c, "ta"))
                    dve.wait_ge(pe_n, at("pe", ph, c, "tr", back=1))
                    step(ph, "c0", dve.tensor_tensor(o[:, :, :], psv(ps_t), per_node(dis, c), ALU.mult))
                    if layer == LAYERS - 1:
                        dve.wait_ge(stored, stored_at(ph, c, back=1))
                        dve.wait_ge(dve_n, at("dve", ph, c, "kp", back=1))
                    step(ph, "c1", dve.tensor_tensor(ta[:, :, :], row(f"eb{layer}"), per_node(deg, c), ALU.mult))
                    after(ph, c, "c1")
                    step(ph, "c2", dve.tensor_tensor(ta[:, :, :], ta[:, :, :], row(f"bias{layer}"), ALU.add))
                    after(ph, c, "c2")
                    step(ph, "c3", dve.tensor_tensor(o[:, :, :], o[:, :, :], ta[:, :, :], ALU.add))
                    after(ph, c, "c3")
                    dve.wait_ge(pe_n, at("pe", ph, c, "mb"))
                    step(ph, "c4", dve.tensor_tensor(o[:, :, :], o[:, :, :], psv(ps_m), ALU.add))
                    after(ph, c, "c4")
                    ln(ph, c, "n", o)
                    affine(ph, c, f"lnw{layer}", f"lnb{layer}")
                    if layer < LAYERS - 1:
                        step(ph, "hd", dve.scalar_tensor_tensor(out=o[:, :, :], in0=hh[:, :, :], scalar=0.0,
                                                                in1=per_node(dis, c), op0=ALU.max, op1=ALU.mult))
                    else:
                        step(ph, "xn", dve.scalar_tensor_tensor(out=ta[:, :, :], in0=hh[:, :, :], scalar=0.0,
                                                                in1=x[:, blk(c), :], op0=ALU.max, op1=ALU.add))
                        add_to_x(ph, c, ta)
                        ln(ph, c, "m", ta)
                        dve.wait_ge(act_n, at("act", ph, c, "m.out"))
                        dve.wait_ge(pe_n, at("pe", ph, c, "mm"))
                        step(ph, "hn", dve.tensor_tensor(ta[:, :, :], psv(ps_o), row("b_neigh"), ALU.add))
                        after(ph, c, "hn")
                        step(ph, "kp", dve.tensor_scalar(keep[:, blk(c), :], ta[:, :, :], 1.0, None, ALU.mult))
                        dve.wait_ge(pe_n, at("pe", ph, c, "mz"))
                        step(ph, "zs", dve.tensor_tensor(side[:, blk(c), :], psv(ps_m), row("b_lin"), ALU.add))
                phase_over("dve", ph)

            def edge_half(i, hf, prior, windows, last):
                r, tile = slice(hf * H, hf * H + H), i * U + hf * H
                if windows and not last:
                    one_hot_T_half("sage", *after_half(i, hf))
                here = src_f[:, bass.ds(tile, H)]
                dve.wait_ge(srow_in[hf], i * 16 + 16)
                dve.wait_ge(mrg, i * 2 + hf + 0 if prior else 1)
                dve.tensor_tensor(eq[:, hf, :, :], srow[:, hf, :].rearrange("p (j k) -> p j k", j=H),
                                  here.unsqueeze(2).to_broadcast([128, H, 128]), ALU.is_equal).then_inc(eq_s, 1)
                dve.wait_ge(eq_s, i * 2 + hf + 3)
                lchain(i, dve.tensor_tensor(junk[:, hf, :, :], eq[:, hf, :, :],
                                            lower[:, :].unsqueeze(1).to_broadcast([128, H, 128]), ALU.mult))
                lchain(i, dve.tensor_reduce(before[:, hf, :], junk[:, hf, :, :], AX.X, ALU.add))
                lchain(i, dve.tensor_scalar(bsel[:, hf, 0, :], before[:, hf, :], 0.0, None, ALU.is_gt))
                lchain(i, dve.tensor_tensor(bsel[:, hf, 1, :], dump[:, 0:1].to_broadcast([128, H]), here, ALU.subtract))
                lchain(i, dve.tensor_tensor(bsel[:, hf, 2, :], bsel[:, hf, 0, :], bsel[:, hf, 1, :], ALU.mult))
                for j in range(H if prior else 0):
                    dve.wait_ge(added[j], i * 32 + 16 * (hf - 1))
                dve.tensor_tensor(where_i[:, hf, :], bsel[:, hf, 2, :], here, ALU.add).then_inc(where, 1)
                dve.wait_ge(abs_s, i * 2 + hf + 0 if prior else 1)
                if windows:
                    for j in range(H):
                        dve.wait_ge(fa_in[hf * H + j], dma_half("sage", PASSES, i))
                    dve.wait_ge(half_sem["own_out"], half("own_out", "sage", i, hf))
                    other = ps_zh[hf].rearrange("p (j f) -> p j f", j=H)
                else:
                    for j in range(H):
                        dve.wait_ge(ga_in[hf * H + j], (LAYERS * TILES * 16 if hf * H + j == 0 else 0) + 16 + i * 16)
                        dve.wait_ge(gb_in[hf * H + j], i * 16 + 16)
                    other = msg[:, r, 0:D]
                dve.tensor_tensor(diff[:, hf, :, :], g_a[:, r, :], other, ALU.subtract).then_inc(diff_s, 1)

            def lchain(i, ins):
                ins.then_inc(dve_c, 1)
                dve.wait_ge(dve_c, chain.next())

            def sage_pass(windows):
                edge_half(0, 0, False, windows, False)
                edge_half(0, 1, False, windows, False)
                with dve.Fori(1, ITERS - 1) as i:
                    chain.enter(i, 10, 1)
                    edge_half(i, 0, True, windows, False)
                    edge_half(i, 1, True, windows, False)
                chain.leave(ITERS - 2)
                edge_half(ITERS - 1, 0, True, windows, False)
                edge_half(ITERS - 1, 1, True, windows, True)

            chain_now = chain.n
            with dve.If(unfitting == 0):
                one_hot_T_half("sage", 0, 0)
                sage_pass(True)
            chain.n = chain_now
            with dve.Else():
                sage_pass(False)

            ph = "sage"
            with dve.Fori(0, CH) as c:
                dve.wait_ge(sm_in, c * (16 * NACC) + 16 * NACC)
                step(ph, "s0", dve.tensor_tensor(sm[:, 0, :, :], sm[:, 0, :, :], sm[:, 1, :, :], ALU.add))
                step(ph, "s1", dve.tensor_tensor(sm[:, 2, :, :], sm[:, 2, :, :], sm[:, 3, :, :], ALU.add))
                after(ph, c, "s1")
                step(ph, "s2", dve.tensor_tensor(sm[:, 0, :, :], sm[:, 0, :, :], sm[:, 2, :, :], ALU.add))
                after(ph, c, "s2")
                step(ph, "cn", dve.tensor_scalar(rcnt[:, 0, :], sm[:, 0, :, 2 * D], 1.0, None, ALU.max))
                after(ph, c, "cn")
                step(ph, "rc", dve.reciprocal(rcnt[:, 1, :], rcnt[:, 0, :]))
                dve.wait_ge(stored, stored_at(ph, c, 1, back=1))
                step(ph, "c0", dve.tensor_tensor(ta[:, :, :], row("b_edge"),
                                                 sm[:, 0, :, 2 * D:].to_broadcast([128, CB, D]), ALU.mult))
                after(ph, c, "c0")
                dve.wait_ge(pe_n, at("pe", ph, c, "me"))
                step(ph, "c1", dve.tensor_tensor(ta[:, :, :], ta[:, :, :], psv(ps_o), ALU.add))
                after(ph, c, "c1")
                step(ph, "c2", dve.tensor_tensor(ta[:, :, :], ta[:, :, :], keep[:, blk(c), :], ALU.add))
                after(ph, c, "c2")
                dve.wait_ge(pe_n, at("pe", ph, c, "tr", back=1))
                step(ph, "c3", dve.tensor_tensor(o[:, :, :], ta[:, :, :],
                                                 rcnt[:, 1, :].unsqueeze(2).to_broadcast([128, CB, D]), ALU.mult))
                dve.wait_ge(pe_n, at("pe", ph, c, "mz"))
                dve.wait_ge(stored, stored_at(ph, c, 0, back=1))
                step(ph, "z0", dve.tensor_tensor(tb[:, :, :], side[:, blk(c), :], psv(ps_t), ALU.add))
                after(ph, c, "z0")
                step(ph, "xn", dve.tensor_tensor(ta[:, :, :], tb[:, :, :], x[:, blk(c), :], ALU.add))
                add_to_x(ph, c, ta)
                ln(ph, c, "m", ta)
                dve.wait_ge(act_n, at("act", ph, c, "m.out"))
                step(ph, "kp", dve.tensor_scalar(keep[:, blk(c), :], hh[:, :, :], 1.0, None, ALU.mult))
                dve.wait_ge(pe_n, at("pe", ph, c, "mq"))
                step(ph, "tq", dve.tensor_tensor(ta[:, :, :], psv(ps_m), row("b_m1"), ALU.add))
            phase_over("dve", ph)

            loads.n += ITERS
            gb0 = ITERS + 1
            with dve.If(unfitting == 0):
                window_pass("mlp", 1, ahead=one_hot_T_half, this=mix_half)
            with dve.Else():
                one_hot_pass((diff[:, 0, 0, :], gb0))
            ph = "mlp"
            with dve.Fori(0, CH) as c:
                dve.wait_ge(pe_n, at("pe", ph, c, "mu"))
                dve.wait_ge(pe_n, at("pe", ph, c, "ml", back=1))
                step(ph, "ua", dve.tensor_tensor(hT[:, :], side_fm[:, nodes(c)], ps_m, ALU.add))
                dve.wait_ge(pe_n, at("pe", ph, c, "my"))
                step(ph, "y", dve.tensor_tensor(o[:, :, :], row("b_u2"), psv(ps_o), ALU.add))
                after(ph, c, "y")
                ln(ph, c, "n", o)
                affine(ph, c, "gamma", "beta")
                step(ph, "hb", dve.tensor_tensor(ta[:, :, :], hh[:, :, :], keep[:, blk(c), :], ALU.add))
                after(ph, c, "hb")
                step(ph, "xn", dve.tensor_tensor(tb[:, :, :], ta[:, :, :], x[:, blk(c), :], ALU.add))
                add_to_x(ph, c, tb)
                ln(ph, c, "m", tb)
            phase_over("dve", ph)

            with dve.If(unfitting == 0):
                window_pass("rel", 1, lambda: dve.wait_ge(pe_n, end("pe", "mlp")), ahead=types_half,
                            with_hot=narrow_half)
            with dve.Else():
                one_hot_pass((zf[:, :], gb0 + TILES))
            ph = "rel"
            with dve.Fori(0, CH) as c:
                dve.wait_ge(pe_n, at("pe", ph, c, "mn"))
                step(ph, "c0", dve.tensor_tensor(o[:, :, :], psv(ps_o), per_node(norm, c), ALU.mult))
                after(ph, c, "c0")
                step(ph, "c1", dve.tensor_tensor(ta[:, :, :], o[:, :, :], side[:, blk(c), :], ALU.add))
                after(ph, c, "c1")
                dve.wait_ge(stored, stored_at(ph, c, back=1))
                step(ph, "c2", dve.scalar_tensor_tensor(out=tb[:, :, :], in0=ta[:, :, :], scalar=0.0,
                                                        in1=x[:, blk(c), :], op0=ALU.max, op1=ALU.add))
            phase_over("dve", ph)

        @block.scalar
        def _(act):
            for q in (abs_s, summed, relu, full):
                act.sem_inc(q, 1)
            act.sem_inc(act_n, STEP0)
            for n in ("relu_made", "own_out", "cnt_out"):
                act.sem_inc(half_sem[n], 2)

            def step(ph, name, ins):
                tick("act", ph, name, ins)

            def copy(ph, name, dst, src):
                step(ph, name, act.activation(dst, src, ACT.Copy))

            def ln(ph, c, t, src, func, again=None):
                act.wait_ge(dve_n, at("dve", ph, c, t + ".ve"))
                step(ph, t + ".sd", act.activation(lns[:, 1, :], lns[:, 0, :], ACT.Sqrt))
                act.wait_ge(dve_n, at("dve", ph, c, t + ".co"))
                if again is not None:
                    again(c)
                for k in range(CB):
                    last = act.activation(hh[:, k, :], src[:, k, :], func, scale=lns[:, 4, k:k + 1],
                                          bias=lns[:, 5, k:k + 1])
                step(ph, t + ".out", last)

            def turned(ph, c, name, pe_name, free):
                act.wait_ge(pe_n, at("pe", ph, c, pe_name))
                act.wait_ge(pe_n, free)
                copy(ph, name, hT[:, :], ps_h)

            act.wait_ge(dve_c, DEG_CHAIN + 1)
            act.activation(small[:, 1, :], small[:, 0, :], ACT.Sqrt).then_inc(act_c, 1)

            ph = "start"
            with act.Fori(0, CH) as c:
                ln(ph, c, "m", ta, ACT.Relu, lambda c: act.wait_ge(dve_n, at("dve", "start", c, "hd", back=1)))
                turned(ph, c, "hT", "tr", at("pe", ph, c, "mm", back=1))
                act.wait_ge(pe_n, at("pe", ph, c, "mm"))
                act.wait_ge(stored, stored_at(ph, c, back=1))
                copy(ph, "tab", tb[:, :, :].rearrange("p b f -> p (b f)"), ps_o)
            phase_over("act", ph)

            relus, mixes, fulls, zs = Count(), Count(), Count(start=0), Count()

            def sums_out(k):
                act.wait_ge(ps_full, fulls.next())
                act.activation(acc[:, k, 0:NP], ps[:, 0:NP], ACT.Copy).then_inc(full, 1)

            unfitting = is_general(act)

            def relu_halves(p):
                def body(i, last):
                    for hf in range(2):
                        if p == "mlp":
                            act.wait_ge(half_sem["mix_made"], half("mix_made", p, i, hf))
                            message = diff[:, hf, :, :]
                        else:
                            act.wait_ge(half_sem["z_made"], half("z_made", p, i, hf))
                            message = ps_zh[hf].rearrange("p (j f) -> p j f", j=H)
                        act.wait_ge(half_sem["seg_made"], half("seg_made", p, i, hf, back=2))
                        act.activation(zr[:, hf, :, :], message, ACT.Relu).then_inc(half_sem["relu_made"], 1)
                iterations(act, body)

            def sums_are_in(p, increments):
                act.wait_ge(half_sem["win_added"], half("win_added", p, ITERS - 1, 1))
                act.sem_inc(full, increments)

            for layer in range(LAYERS):
                ph = f"gcn{layer}"
                with act.If(unfitting == 0):
                    relu_halves(ph)
                    sums_are_in(ph, 2)
                with act.Else():
                    sums_out(0)
                    with act.Fori(0, TILES) as t:
                        relus.enter(t, 1)
                        zs.enter(t, 1)
                        act.wait_ge(seg, t + (1 + TILES * (2 * layer + 1)))
                        act.wait_ge(zmm, zs.next())
                        act.activation(zf[:, :], ps_z, ACT.Relu).then_inc(relu, 1)
                        relus.next()
                    relus.leave(TILES)
                    zs.leave(TILES)
                    sums_out(1)
                with act.Fori(0, CH) as c:
                    act.wait_ge(full, 1 + fulls.n)
                    act.wait_ge(pe_n, at("pe", ph, c, "ta", back=1))
                    copy(ph, "sa", s_a[:, :], acc[:, 0, nodes(c)])
                    act.wait_ge(pe_n, at("pe", ph, c, "mb", back=1))
                    copy(ph, "sb", s_b[:, :], acc[:, 1, nodes(c)])
                    if layer < LAYERS - 1:
                        ln(ph, c, "n", o, ACT.Identity, lambda c: act.wait_ge(dve_n, at("dve", ph, c, "hd", back=1)))
                        turned(ph, c, "hT", "tr", at("pe", ph, c, "mm", back=1))
                        act.wait_ge(pe_n, at("pe", ph, c, "mm"))
                        act.wait_ge(stored, stored_at(ph, c, back=1))
                        copy(ph, "tab", tb[:, :, :].rearrange("p b f -> p (b f)"), ps_o)
                    else:
                        ln(ph, c, "n", o, ACT.Identity, lambda c: act.wait_ge(pe_n, at("pe", ph, c, "tr", back=1)))
                        ln(ph, c, "m", ta, ACT.Relu)
                        turned(ph, c, "hT", "tr", at("pe", ph, c, "mz", back=1))
                phase_over("act", ph)

            def edge_half(i, hf, prior, windows):
                r = slice(hf * H, hf * H + H)
                if windows:
                    act.wait_ge(half_sem["z_made"], half("z_made", "sage", i, hf))
                    if prior:
                        act.wait_ge(mrg, i * 2 + hf)
                    act.activation(msg[:, r, 0:D], ps_zh[hf].rearrange("p (j f) -> p j f", j=H), ACT.Copy)\
                       .then_inc(half_sem["own_out"], 1)
                act.wait_ge(diff_s, i * 2 + hf + 2)
                act.sem_inc(passed, 1)
                act.activation(msg[:, r, D:2 * D], diff[:, hf, :, :], ACT.Abs).then_inc(abs_s, 1)
                act.wait_ge(mrg, i * 2 + hf + 2)
                for j in range(H if prior else 0):
                    act.wait_ge(added[j], i * 32 + 16 * (hf - 1))
                at_ps = 0 if windows else 2048 * hf
                act.activation(sums[:, r, :], ps[:, at_ps:at_ps + 2048].rearrange("p (j f) -> p j f", j=H)[:, :, 0:MS],
                               ACT.Copy).then_inc(summed, 1)

            def sage_pass(windows):
                edge_half(0, 0, False, windows)
                edge_half(0, 1, False, windows)
                with act.Fori(1, ITERS) as i:
                    edge_half(i, 0, True, windows)
                    edge_half(i, 1, True, windows)

            with act.If(unfitting == 0):
                sage_pass(True)
            with act.Else():
                sage_pass(False)

            ph = "sage"
            with act.Fori(0, CH) as c:
                act.wait_ge(pe_n, at("pe", ph, c, "ta"))
                act.wait_ge(pe_n, at("pe", ph, c, "me", back=1))
                copy(ph, "sa", s_a[:, :], ps_t)
                act.wait_ge(pe_n, at("pe", ph, c, "tb"))
                copy(ph, "sb", s_b[:, :], ps_m)
                turned(ph, c, "hT", "tr", at("pe", ph, c, "mu", back=1))
                ln(ph, c, "m", ta, ACT.Relu, lambda c: act.wait_ge(pe_n, at("pe", "sage", c, "tr2", back=1)))
                turned(ph, c, "hT2", "tr2", at("pe", ph, c, "mz"))
                act.wait_ge(pe_n, at("pe", ph, c, "mp"))
                act.wait_ge(dve_n, at("dve", ph, c, "xn"))
                copy(ph, "tp", tb[:, :, :].rearrange("p b f -> p (b f)"), ps_o)
                act.wait_ge(pe_n, at("pe", ph, c, "mu"))
                step(ph, "us", act.activation(side_fm[:, nodes(c)], ps_t, ACT.Identity, bias=bu1_col[:, 0:1]))
            phase_over("act", ph)

            with act.If(unfitting == 0):
                relu_halves("mlp")
                sums_are_in("mlp", 1)
            with act.Else():
                with act.Fori(0, TILES) as t:
                    relus.enter(t, 1)
                    mixes.enter(t, 1)
                    act.wait_ge(msg_s, mixes.next())
                    act.wait_ge(seg, t + (1 + TILES * 2 * LAYERS))
                    act.activation(zf[:, :], diff[:, 0, 0, :], ACT.Relu).then_inc(relu, 1)
                    relus.next()
                relus.leave(TILES)
                mixes.leave(TILES)
                sums_out(0)
            ph = "mlp"
            with act.Fori(0, CH) as c:
                act.wait_ge(pe_n, at("pe", ph, c, "ag"))
                act.wait_ge(pe_n, at("pe", ph, c, "mu", back=1))
                copy(ph, "sa", s_a[:, :], ps_t)
                act.wait_ge(dve_n, at("dve", ph, c, "ua"))
                act.wait_ge(pe_n, at("pe", ph, c, "my", back=1))
                step(ph, "ur", act.activation(s_b[:, :], hT[:, :], ACT.Relu))

                def hh_free(c):
                    act.wait_ge(stored, stored_at("mlp", c, back=1))
                    act.wait_ge(pe_n, at("pe", "mlp", c, "tr", back=1))

                ln(ph, c, "n", o, ACT.Identity, hh_free)
                ln(ph, c, "m", tb, ACT.Relu)
                act.wait_ge(act_n, at("act", ph, c, "ur"))
                turned(ph, c, "hT", "tr", at("pe", ph, c, "ml", back=1))
                act.wait_ge(pe_n, at("pe", ph, c, "ml"))
                act.wait_ge(dve_n, at("dve", ph, c, "ua"))
                step(ph, "zs", act.activation(side_fm[:, nodes(c)], ps_m, ACT.Copy))
            phase_over("act", ph)
            def counts_out(i, last):
                for hf in range(2):
                    act.wait_ge(half_sem["cnt_made"], half("cnt_made", "rel", i, hf))
                    act.wait_ge(half_sem["seg_made"], half("seg_made", "rel", i, hf, back=2))
                    act.activation(cnts[:, hf, :, :], ps_c[hf].rearrange("p (b k) -> p b k", b=TB), ACT.Copy)\
                       .then_inc(half_sem["cnt_out"], 1)

            with act.If(unfitting == 0):
                iterations(act, counts_out)
                sums_are_in("rel", 1)
            with act.Else():
                sums_out(0)
            ph = "rel"
            with act.Fori(0, CH) as c:
                act.wait_ge(full, 1 + fulls.n)
                act.wait_ge(pe_n, at("pe", ph, c, "mn", back=1))
                copy(ph, "sa", s_a[:, :], acc[:, 0, nodes(c)])
            phase_over("act", ph)

        @block.tensor
        def _(pe):
            for q in (deg_mm, seg, zmm, mrg):
                pe.sem_inc(q, 1)
            pe.sem_inc(pe_n, STEP0)
            for n in ("z_made", "seg_made", "cnt_made"):
                pe.sem_inc(half_sem[n], 2)

            def step(ph, name, ins):
                tick("pe", ph, name, ins)

            def open_sums(banks):
                for k, width in banks:
                    pe.matmul(ps[:, k:k + width], zeros[:, 0:128], zeros[:, 0:width], start=True, stop=False,
                              skip_group_check=True)

            def close_sums(banks):
                for k, width in banks:
                    last = pe.matmul(ps[:, k:k + width], zeros[:, 0:128], zeros[:, 0:width], start=False, stop=True,
                                     skip_group_check=True)
                return last

            pe.wait_ge(dve_c, 1)
            open_sums([(0, NB)])
            with pe.Fori(0, ITERS) as i:
                pe.wait_ge(hot, i * 2 + 3)
                for j in range(U):
                    last = pe.matmul(ps[:, 0:NB], oh_lo[:, j, :], oh_hi[:, j, :], start=False, stop=False,
                                     skip_group_check=True)
                last.then_inc(deg_mm, 1)
            close_sums([(0, NB)]).then_inc(deg_mm, 1)

            pe.wait_ge(consts, 10)
            pe.wait_ge(in_w, 80)
            pe.wait_ge(dve_c, 5)
            hots, segs, relus, mixes, loads, zin = Count(), Count(), Count(), Count(), Count(by=16, start=0), Count(by=16, start=0)
            hots.n += 2 * ITERS

            def turn(ph, c, name, dst, src):
                for k in range(CB):
                    last = pe.transpose(dst[:, k * 128:k * 128 + 128], src(k), ident[:, :])
                step(ph, name, last)

            def by_rows(ph, name, dst, parts):
                for k in range(CB):
                    for n, (lhs, w) in enumerate(parts):
                        last = pe.matmul(dst[:, k * 128:k * 128 + 128], lhs[:, k * 128:k * 128 + 128], W[w],
                                         start=(n == 0), stop=(n == len(parts) - 1))
                step(ph, name, last)

            def hh_blk(k):
                return hh[:, k, :]

            def o_blk(k):
                return o[:, k, :]

            def add_tile(message):
                for k, width in BANKS:
                    last = pe.matmul(ps[:, k:k + width], message, big[:, k:k + width], start=False, stop=False,
                                     skip_group_check=True)
                last.then_inc(seg, 1)

            def sum_pass(message, came):
                open_sums(BANKS)
                with pe.Fori(0, TILES) as t:
                    hots.enter(t, 1)
                    pe.wait_ge(hot, hots.next())
                    came(t)
                    add_tile(message)
                hots.leave(TILES)
                close_sums(BANKS).then_inc(ps_full, 1)

            ph = "start"
            with pe.Fori(0, CH) as c:
                pe.wait_ge(dve_n, at("dve", ph, c, "hd"))
                pe.wait_ge(act_n, at("act", ph, c, "hT", back=1))
                turn(ph, c, "tr", ps_h, o_blk)
                pe.wait_ge(act_n, at("act", ph, c, "hT"))
                pe.wait_ge(act_n, at("act", ph, c, "tab", back=1))
                by_rows(ph, "mm", ps_o, [(hT, "lin0")])
            phase_over("pe", ph)

            unfitting = is_general(pe)

            def mlp_half(p, i, hf):
                pe.wait_ge(ea_h[hf], dma_half(p, GCN, i))
                pe.wait_ge(half_sem["relu_made"], half("relu_made", p, i, hf, back=2))
                for j in range(H):
                    last = pe.matmul(ps_zh[hf][:, 128 * j:128 * j + 128], ea_r[:, hf, 128 * j:128 * j + 128],
                                     w1[:, GCN.index(p), :], start=True, stop=True)
                last.then_inc(half_sem["z_made"], 1)

            def own_half(p, i, hf):
                pe.wait_ge(win_in[hf], dma_half(p, ["sage", "mlp"], i))
                pe.wait_ge(half_sem["ohT_made"], half("ohT_made", p, i, hf))
                if p == "sage":
                    pe.wait_ge(half_sem["own_out"], half("own_out", p, i, hf, back=2))
                    pe.wait_ge(diff_s, i * 2 + hf) if not isinstance(i, int) or i else None
                else:
                    pe.wait_ge(half_sem["mix_made"], half("mix_made", p, i, hf, back=2))
                for j in range(H):
                    last = pe.matmul(ps_zh[hf][:, 128 * j:128 * j + 128], ohT[:, hf, 128 * j:128 * j + 128],
                                     win[:, hf, :], start=True, stop=True)
                last.then_inc(half_sem["z_made"], 1)

            def seg_half(p, i, hf):
                pe.wait_ge(half_sem["win_added"], half("win_added", p, i, hf, back=2))
                pe.wait_ge(half_sem["oh_made"], half("oh_made", p, i, hf))
                if p != "mlp":
                    for j in range(H):
                        pe.wait_ge(fa_in[hf * H + j], dma_half(p, PASSES, i))
                        last = pe.matmul(ps_w[hf][:, 0, :], g_a[:, hf * H + j, :], oh[:, hf, j, :],
                                         start=(j == 0), stop=(j == H - 1 and p != "rel"))
                if p == "rel":
                    pe.wait_ge(half_sem["cnt_out"], half("cnt_out", p, i, hf))
                    for b in range(TB):
                        last = pe.matmul(ps_w[hf][:, 0, :], rel_sb[:, b, :], cnts[:, hf, b, :], start=False,
                                         stop=(b == TB - 1))
                else:
                    pe.wait_ge(half_sem["relu_made"], half("relu_made", p, i, hf))
                    for j in range(H):
                        last = pe.matmul(ps_w[hf][:, 0 if p == "mlp" else 1, :], zr[:, hf, j, :], oh[:, hf, j, :],
                                         start=(j == 0), stop=(j == H - 1))
                last.then_inc(half_sem["seg_made"], 1)

            def count_half(p, i, hf):
                pe.wait_ge(half_sem["typ_made"], half("typ_made", p, i, hf))
                pe.wait_ge(half_sem["cnt_out"], half("cnt_out", p, i, hf, back=2))
                for b in range(TB):
                    for j in range(H):
                        last = pe.matmul(ps_c[hf][:, 128 * b:128 * b + 128], oh_typ[:, hf, j, TR * b:TR * b + TR],
                                         oh16[:, hf, j, :], start=(j == 0), stop=(j == H - 1))
                last.then_inc(half_sem["cnt_made"], 1)

            def window_pass(p, ahead, then):
                ahead(p, 0, 0)

                def body(i, last):
                    for hf in range(2):
                        if p == "rel":
                            then(p, i, hf)
                        if not (last and hf):
                            ahead(p, *after_half(i, hf))
                        if p != "rel":
                            then(p, i, hf)
                iterations(pe, body)

            full_n = 1
            for layer in range(LAYERS):
                pe.wait_ge(act_n, end("act", PHASES[layer]))
                pe.wait_ge(dve_n, end("dve", PHASES[layer]))
                if layer:
                    pe.wait_ge(full, full_n)

                def gathered(t):
                    loads.enter(t, 1)
                    pe.wait_ge(ga_in[0], loads.next())

                def through_mlp(t):
                    relus.enter(t, 1)
                    zin.enter(t, 1)
                    pe.wait_ge(ea_in_s, zin.next())
                    pe.matmul(ps_z, ea_t[:, :], w1[:, layer, :], start=True, stop=True).then_inc(zmm, 1)
                    pe.wait_ge(relu, relus.next())

                with pe.If(unfitting == 0):
                    window_pass(f"gcn{layer}", mlp_half, seg_half)
                with pe.Else():
                    sum_pass(g_a[:, 0, :], gathered)
                    loads.leave(TILES)
                    pe.wait_ge(full, full_n + 1)
                    sum_pass(zf[:, :], through_mlp)
                    relus.leave(TILES)
                    zin.leave(TILES)
                full_n += 2
                pe.wait_ge(full, full_n)
                ph = f"gcn{layer}"
                with pe.Fori(0, CH) as c:
                    pe.wait_ge(act_n, at("act", ph, c, "sa"))
                    pe.wait_ge(dve_n, at("dve", ph, c, "c0", back=1))
                    turn(ph, c, "ta", ps_t, lambda k: s_a[:, k * 128:k * 128 + 128])
                    pe.wait_ge(act_n, at("act", ph, c, "sb"))
                    pe.wait_ge(dve_n, at("dve", ph, c, "zs" if layer == LAYERS - 1 else "c4", back=1))
                    by_rows(ph, "mb", ps_m, [(s_b, f"ew{layer}")])
                    if layer < LAYERS - 1:
                        pe.wait_ge(dve_n, at("dve", ph, c, "hd"))
                        pe.wait_ge(act_n, at("act", ph, c, "hT", back=1))
                        turn(ph, c, "tr", ps_h, o_blk)
                        pe.wait_ge(act_n, at("act", ph, c, "hT"))
                        pe.wait_ge(act_n, at("act", ph, c, "tab", back=1))
                        by_rows(ph, "mm", ps_o, [(hT, f"lin{layer + 1}")])
                    else:
                        pe.wait_ge(act_n, at("act", ph, c, "m.out"))
                        turn(ph, c, "tr", ps_h, hh_blk)
                        pe.wait_ge(act_n, at("act", ph, c, "hT"))
                        pe.wait_ge(dve_n, at("dve", ph, c, "hn", back=1))
                        by_rows(ph, "mm", ps_o, [(hT, "neigh")])
                        pe.wait_ge(dve_n, at("dve", ph, c, "c4"))
                        by_rows(ph, "mz", ps_m, [(hT, "l1_a")])
                phase_over("pe", ph)

            pe.wait_ge(act_n, end("act", "gcn2"))
            pe.wait_ge(dve_n, end("dve", "gcn2"))

            def edge_half(i, hf, prior, windows=False):
                if windows:
                    pe.wait_ge(summed, i * 2 + (hf + 1))
                    pe.wait_ge(half_sem["own_out"], half("own_out", "sage", i, hf))
                elif prior:
                    pe.wait_ge(summed, i * 2 + hf)
                pe.wait_ge(eq_s, i * 2 + hf + 3)
                pe.wait_ge(abs_s, i * 2 + hf + 2)
                pe.sem_inc(passed, 1)
                for j in range(H):
                    k = (0 if windows else 2048 * hf) + 512 * j
                    last = pe.matmul(ps[:, k:k + MS], eq[:, hf, j, :], msg[:, hf * H + j, :], start=True, stop=True)
                last.then_inc(mrg, 1)

            with pe.If(unfitting == 0):
                window_pass("sage", own_half, lambda p, i, hf: edge_half(i, hf, True, True))
            with pe.Else():
                edge_half(0, 0, False)
                edge_half(0, 1, False)
                with pe.Fori(1, ITERS) as i:
                    edge_half(i, 0, True)
                    edge_half(i, 1, True)

            ph = "sage"
            pe.wait_ge(summed, ITERS * 2 + 1)
            with pe.Fori(0, CH) as c:
                pe.wait_ge(dve_n, at("dve", ph, c, "s2"))
                pe.wait_ge(act_n, at("act", ph, c, "us", back=1))
                turn(ph, c, "ta", ps_t, lambda k: sm[:, 0, k, 0:D])
                pe.wait_ge(dve_n, at("dve", ph, c, "tq", back=1))
                turn(ph, c, "tb", ps_m, lambda k: sm[:, 0, k, D:2 * D])
                pe.wait_ge(act_n, at("act", ph, c, "sb"))
                pe.wait_ge(act_n, at("act", ph, c, "tp", back=1))
                by_rows(ph, "me", ps_o, [(s_a, "edge_a"), (s_b, "edge_b")])
                pe.wait_ge(dve_n, at("dve", ph, c, "c3"))
                turn(ph, c, "tr", ps_h, o_blk)
                pe.wait_ge(act_n, at("act", ph, c, "hT"))
                by_rows(ph, "mz", ps_t, [(hT, "l1_b")])
                pe.wait_ge(act_n, at("act", ph, c, "m.out"))
                turn(ph, c, "tr2", ps_h, hh_blk)
                pe.wait_ge(act_n, at("act", ph, c, "hT2"))
                pe.wait_ge(dve_n, at("dve", ph, c, "c1"))
                by_rows(ph, "mp", ps_o, [(hT, "m1_a")])
                by_rows(ph, "mq", ps_m, [(hT, "m1_b")])
                pe.wait_ge(dve_n, at("dve", ph, c, "z0"))
                for lo, hi in ((0, 512), (512, CW)):
                    last = pe.matmul(ps_t[:, lo:hi], W["u1_a"], hT[:, lo:hi], start=True, stop=True)
                step(ph, "mu", last)
            phase_over("pe", ph)

            pe.wait_ge(act_n, end("act", "sage"))
            pe.wait_ge(dve_n, end("dve", "sage"))

            def through_relu(t):
                relus.enter(t, 1)
                pe.wait_ge(relu, relus.next())

            with pe.If(unfitting == 0):
                window_pass("mlp", own_half, seg_half)
            with pe.Else():
                sum_pass(zf[:, :], through_relu)
                relus.leave(TILES)
            full_n += 1
            pe.wait_ge(full, full_n)
            pe.wait_ge(deg_back, 16)
            ph = "mlp"
            eb = rows[0:1, ROWS.index("b_m2"), :]
            with pe.Fori(0, CH) as c:
                pe.wait_ge(act_n, at("act", ph, c, "sa", back=1))
                for lo, hi in ((0, 512), (512, CW)):
                    pe.matmul(ps_t[:, lo:hi], W["m2"], acc[:, 0, bass.ds(c * CW + lo, hi - lo)], start=True, stop=False)
                    last = pe.matmul(ps_t[:, lo:hi], eb, deg_row[0:1, bass.ds(c * CW + lo, hi - lo)], start=False, stop=True)
                step(ph, "ag", last)
                pe.wait_ge(act_n, at("act", ph, c, "sa"))
                pe.wait_ge(act_n, at("act", ph, c, "zs", back=1))
                for lo, hi in ((0, 512), (512, CW)):
                    last = pe.matmul(ps_m[:, lo:hi], W["u1_b"], s_a[:, lo:hi], start=True, stop=True)
                step(ph, "mu", last)
                pe.wait_ge(act_n, at("act", ph, c, "ur"))
                pe.wait_ge(dve_n, at("dve", ph, c, "y", back=1))
                by_rows(ph, "my", ps_o, [(s_b, "u2")])
                pe.wait_ge(act_n, at("act", ph, c, "m.out"))
                turn(ph, c, "tr", ps_h, hh_blk)
                pe.wait_ge(act_n, at("act", ph, c, "hT"))
                pe.wait_ge(dve_n, at("dve", ph, c, "ua"))
                by_rows(ph, "ml", ps_m, [(hT, "loop")])
            phase_over("pe", ph)

            pe.wait_ge(act_n, end("act", "mlp"))
            pe.wait_ge(dve_n, end("dve", "mlp"))

            def mixed(t):
                mixes.enter(t, 1)
                pe.wait_ge(msg_s, mixes.next())

            mixes.n += TILES
            with pe.If(unfitting == 0):
                window_pass("rel", count_half, seg_half)
            with pe.Else():
                sum_pass(zf[:, :], mixed)
                mixes.leave(TILES)
            full_n += 1
            pe.wait_ge(full, full_n)
            ph = "rel"
            with pe.Fori(0, CH) as c:
                pe.wait_ge(act_n, at("act", ph, c, "sa"))
                pe.wait_ge(dve_n, at("dve", ph, c, "c0", back=1))
                by_rows(ph, "mn", ps_o, [(s_a, "neighbor")])
            phase_over("pe", ph)


def kernel(**inputs):
    import concourse.bacc as bacc
    from concourse.bass_utils import run_bass_kernel_spmd

    g = {k: np.asarray(v) for k, v in inputs.items()}
    f32 = np.float32

    def edges(a):
        return np.concatenate([a, np.full(TILES * 128 - E, N, a.dtype)])

    x = np.concatenate([g["x"], np.zeros((NP - N, D), f32)]).reshape(NB, 128, D).transpose(1, 0, 2)
    src, dst = edges(g["src"]), edges(g["dst"])
    typ = np.concatenate([g["edge_type_500"], np.zeros(TILES * 128 - E, np.int32)])
    ea = np.concatenate([g["edge_attr_16"], np.zeros((TILES * 128 - E, DE), f32)]).T
    ea = np.concatenate([ea, np.ones((1, TILES * 128), f32)])
    n1, n2 = g["L1_gnn_W_edge"], g["L1_gnn_W_lin"]
    mats = {
        "lin0": g["L0_gnn_lin_w"][0], "lin1": g["L0_gnn_lin_w"][1], "lin2": g["L0_gnn_lin_w"][2],
        "ew0": g["L0_gnn_edge_w2"][0], "ew1": g["L0_gnn_edge_w2"][1], "ew2": g["L0_gnn_edge_w2"][2],
        "neigh": g["L1_gnn_W_neigh"].T, "edge_a": n1[:, :D].T, "edge_b": n1[:, D:].T,
        "l1_a": n2[:, :D].T, "l1_b": n2[:, D:].T,
        "m1_a": g["L2_gnn_w_m1"][:D], "m1_b": g["L2_gnn_w_m1"][D:], "m2": g["L2_gnn_w_m2"],
        "u1_a": g["L2_gnn_w_u1"][:D], "u1_b": g["L2_gnn_w_u1"][D:], "u2": g["L2_gnn_w_u2"],
        "neighbor": g["L3_gnn_W_neighbor"], "loop": g["L3_gnn_loop_weight"],
    }
    vecs = {"b_neigh": g["L1_gnn_b_neigh"], "b_edge": g["L1_gnn_b_edge"], "b_lin": g["L1_gnn_b_lin"],
            "b_m1": g["L2_gnn_b_m1"], "b_m2": g["L2_gnn_b_m2"], "b_u1": g["L2_gnn_b_u1"], "b_u2": g["L2_gnn_b_u2"],
            "gamma": g["L2_gnn_gamma"], "beta": g["L2_gnn_beta"]}
    for k in range(LAYERS):
        vecs |= {f"lnw{k}": g["L0_gnn_ln_w"][k], f"lnb{k}": g["L0_gnn_ln_b"][k], f"bias{k}": g["L0_gnn_bias"][k],
                 f"eb{k}": g["L0_gnn_edge_b2"][k]}
    w1 = np.concatenate([g["L0_gnn_edge_w1"], g["L0_gnn_edge_b1"][:, None, :]], axis=1).transpose(1, 0, 2)
    arrays = {
        "x_in": x, "src_in": src.reshape(TILES, 128).T, "dst_in": dst.reshape(TILES, 128).T,
        "typ_in": typ.reshape(TILES, 128).T, "srcrow_in": src.reshape(1, -1),
        "dstrow_in": dst.reshape(1, -1), "relblk_in": g["L3_gnn_rel_emb"].reshape(TB, TR, D).transpose(1, 0, 2),
        "dstgrp_in": dst.reshape(TILES // H, H * 128), "ea_in": ea,
        "w_in": np.stack([mats[n] for n in WEIGHTS], axis=1), "w1_in": w1,
        "rows_in": np.stack([vecs[n] for n in ROWS]), "cols_in": g["L2_gnn_b_u1"].reshape(D, 1),
        "rel_in": g["L3_gnn_rel_emb"],
    }
    arrays = {k: np.ascontiguousarray(v) for k, v in arrays.items()}
    nc = bacc.Bacc("TRN2", target_bir_lowering=False, num_devices=1)
    args = {k: nc.dram_tensor(k, v.shape, mybir.dt.from_np(v.dtype), kind="ExternalInput").ap() for k, v in arrays.items()}
    out = nc.dram_tensor("out", (NP, D), F32, kind="ExternalOutput").ap()
    build(nc, **args, out=out)
    r = run_bass_kernel_spmd(nc, [arrays], core_ids=[0])
    return r.results[0]["out"][:N]
```

```python
from contextlib import ExitStack

import numpy as np
import concourse.bass as bass
from concourse import mybir

F32 = mybir.dt.float32
I32 = mybir.dt.int32
BF16 = mybir.dt.bfloat16
ALU = mybir.AluOpType
ACT = mybir.ActivationFunctionType
AX = mybir.AxisListType

D = 128
N = 3125
E = 50000
DE = 16
NRELS = 500
LAYERS = 3
EPS = 1e-5

NB = -(-N // 128)
NP = NB * 128
CB = 5
CH = NB // CB
CW = CB * 128
U = 8
H = U // 2
ITERS = -(-E // (128 * U))
TILES = ITERS * U
HALVES = 2 * ITERS
WIN = 128
TB = 4
TR = NRELS // TB
MS = 2 * D + 1
NACC = 4
DUMP = NP

WEIGHTS = ["lin0", "lin1", "lin2", "ew0", "ew1", "ew2", "neigh", "edge_a", "edge_b", "l1_a", "l1_b",
           "m1_a", "m1_b", "m2", "u1_a", "u1_b", "u2", "neighbor", "loop"]
ROWS = ["lnw0", "lnw1", "lnw2", "lnb0", "lnb1", "lnb2", "bias0", "bias1", "bias2", "eb0", "eb1", "eb2",
        "b_neigh", "b_edge", "b_lin", "b_m1", "b_m2", "b_u1", "b_u2", "gamma", "beta"]


class Count:

    def __init__(self, by=1, start=1):
        self.by, self.start, self.n, self.var = by, start, 0, None

    def enter(self, var, per, first=0):
        self.var, self.per, self.first, self.n0 = var, per, first, self.n

    def leave(self, trips):
        assert self.n - self.n0 == self.per, (self.n, self.n0, self.per)
        self.n, self.var = self.n0 + self.per * trips, None

    def next(self, back=0):
        self.n += 1
        return self.now(back)

    def now(self, back=0):
        k = self.start + self.by * (self.n - back)
        if self.var is None:
            return k
        per = self.by * self.per
        return self.var * per + (k - self.first * per)


def build(nc, x_in, src_in, dst_in, typ_in, srcrow_in, dstrow_in, dstgrp_in, ea_in, w_in, w1_in, rows_in, cols_in,
          rel_in, relblk_in, out):
    ctx = ExitStack()
    with ctx:
        def sb(name, shape, dt=F32):
            return ctx.enter_context(nc.sbuf_tensor(name, shape, dt))

        def sem(name):
            return ctx.enter_context(nc.semaphore(name))

        def dram(name, shape, dt=F32):
            return nc.dram_tensor(name, shape, dt, kind="Internal").ap()

        tab_a, tab_b = dram("tab_a", (NP, D)), dram("tab_b", (NP, D))
        acc_d = [dram(f"acc_d{k}", (NP + 128, MS)) for k in range(NACC)]
        deg_d = dram("deg_d", (NB, 128))
        grp_d = dram("grp_d", (HALVES, 2))

        x = sb("x", [128, NB, D])
        keep = sb("keep", [128, NB, D])
        side = sb("side", [128, NB, D])
        acc = sb("acc", [128, 2, NP])
        wts = sb("wts", [128, len(WEIGHTS), D])
        w1 = sb("w1", [128, LAYERS, D])
        rows = sb("rows", [128, len(ROWS), D])
        bu1_col = sb("bu1_col", [128, 1])
        src_i, dst_i, typ_i = (sb(n, [128, TILES], I32) for n in ("src_i", "dst_i", "typ_i"))
        src_f, dst_f, typ_f = (sb(n, [128, TILES]) for n in ("src_f", "dst_f", "typ_f"))
        iota = sb("iota", [128, NP])
        ident = sb("ident", [128, 128])
        lower = sb("lower", [128, 128])
        dump = sb("dump", [128, 1])
        zeros = sb("zeros", [128, 512])
        deg, dis, norm = sb("deg", [128, NB]), sb("dis", [128, NB]), sb("norm", [128, NB])
        rcnt = sb("rcnt", [128, 2, CB])
        small = sb("small", [128, 6, NB])
        deg_row = sb("deg_row", [1, NP])
        s_a, s_b, hT = sb("s_a", [128, CW]), sb("s_b", [128, CW]), sb("hT", [128, CW])
        o, hh, ta, tb = (sb(n, [128, CB, D]) for n in ("o", "hh", "ta", "tb"))
        stats = {t: sb("stats_" + t, [128, CB, 6]) for t in ("n", "m")}
        mv = {t: sb("mv_" + t, [128, CB, 2]) for t in ("n", "m")}
        lns = {t: sb("lns_" + t, [128, 6, CB]) for t in ("n", "m")}
        sm = sb("sm", [128, NACC, CB, MS])
        col = sb("col", [128, 2, 2, H], I32)
        g_a = sb("g_a", [128, 2 * U, D])
        msg = sb("msg", [128, U, MS])
        sums = sb("sums", [128, U, MS])
        big = sb("big", [128, NP])
        iota_i = big[:, :].bitcast(I32)
        halves = big[:, 0:3072].rearrange("p (w h j k) -> p w h j k", w=3, h=2, j=H)
        eq = halves[:, 0]
        junk = halves[:, 1]
        srow = big[:, 2048:3072].bitcast(I32).rearrange("p (h k) -> p h k", h=2)
        diff = sb("diff", [128, 2, H, D])
        z_rows = diff[:, :, :, :].rearrange("p h j f -> p (h j) f")[:, 0:CB, :]
        where_i = sb("where_i", [128, 2, H], I32)
        before = sb("before", [128, 2, H])
        bsel = sb("bsel", [128, 2, 3, H])
        ea_t, zf = g_a[:, U, :], g_a[:, U + 1, :]
        grp = sb("grp", [128, 6])
        grp_bc = sb("grp_bc", [128, HALVES, 2])
        base_row, unfit = sb("base_row", [1, HALVES], I32), sb("unfit", [1, 1])
        general = sb("general", [1, 1], I32)
        rel_dst = sb("rel_dst", [128, TILES])
        iota_p = sb("iota_p", [128, 1])
        first_p = sb("first_p", [128, HALVES])
        win = sb("win", [128, 2, D])
        rel_sb = sb("rel_sb", [TR, TB, D])
        oh, zr = halves[:, 0], halves[:, 1]
        ea_r = big[:, 2048:3072].rearrange("p (h k) -> p h k", h=2)
        pair = big[:, 0:2 * CB * MS].rearrange("p (a b f) -> p a b f", a=2, b=CB)
        summ = sums[:, 0:CB, :]
        msgf = msg[:, :, :].rearrange("p a b -> p (a b)")
        m_a, m_b, m_c = (msgf[:, CW * k:CW * k + CW] for k in range(3))
        m_bb, m_cb = (m.rearrange("p (b f) -> p b f", f=D) for m in (m_b, m_c))
        m_ab = m_a.rearrange("p (b f) -> p b f", f=D)
        smf = sm[:, :, :, :].rearrange("p a b c -> p (a b c)")
        low = smf[:, 0:TILES].bitcast(BF16)
        lo_f, hi_f, iota_b = low[:, 0:TILES], low[:, TILES:2 * TILES], smf[:, TILES:TILES + 64].bitcast(BF16)
        lo_i, hi_i = smf[:, 2 * TILES:3 * TILES].bitcast(I32), smf[:, 3 * TILES:4 * TILES].bitcast(I32)
        oh_lo = smf[:, 1600:1600 + U * 64].bitcast(BF16).rearrange("p (u k) -> p u k", u=U)
        oh_hi = smf[:, 2112:2112 + U * NB // 2].bitcast(BF16).rearrange("p (u k) -> p u k", u=U)
        grp_i, grp_f = smf[0:HALVES, 2304:2816].bitcast(I32), smf[0:HALVES, 2816:3328]
        drow = smf[:, 0:1024].bitcast(I32).rearrange("p (h k) -> p h k", h=2)
        oh16 = smf[:, 0:H * WIN].bitcast(BF16).rearrange("p (h j k) -> p h j k", h=2, j=H)
        ohT = smf[:, 1024:2048].rearrange("p (h k) -> p h k", h=2)
        cnts = smf[0:TR, 2048:3072].rearrange("p (h b k) -> p h b k", h=2, b=TB)
        oh_typ = smf[:, 3072:3072 + H * NRELS].bitcast(BF16).rearrange("p (h j k) -> p h j k", h=2, j=H)

        ps = ctx.enter_context(nc.psum_tensor("ps", [128, 4096], F32))
        ps_t, ps_m, ps_h, ps_o = (ps[:, 1024 * k:1024 * k + CW] for k in range(4))

        in_small, in_x, in_w, zeroed = sem("in_small"), sem("in_x"), sem("in_w"), sem("zeroed")
        deg_out, deg_back = sem("deg_out"), sem("deg_back")
        store = sem("store")
        sm_in = [sem(f"sm_in{k}") for k in range(2)]
        ga_in = [sem(f"ga_in{r}") for r in range(U)]
        gb_in = [sem(f"gb_in{r}") for r in range(U)]
        added = [sem(f"added{k}") for k in range(NACC)]
        srow_in = [sem(f"srow_in{k}") for k in range(2)]
        ea_in_s = sem("ea_in_s")
        grp_out, grp_back = sem("grp_out"), sem("grp_back")
        fa_in = [sem(f"fa_in{r}") for r in range(2 * U)]
        ea_h = [sem(f"ea_h{k}") for k in range(2)]
        col_in = [sem(f"col_in{k}") for k in range(4)]
        drow_in = [sem(f"drow_in{k}") for k in range(2)]
        win_in = [sem(f"win_in{k}") for k in range(2)]
        flag_made = sem("flag_made")
        passed = sem("passed")
        stored = sem("stored")
        consts = sem("consts")
        dve_c = sem("dve_c")
        act_c = sem("act_c")
        acc_clear = sem("acc_clear")
        pool_c = sem("pool_c")
        hot = sem("hot")
        deg_mm = sem("deg_mm")
        seg = sem("seg")
        ps_full = sem("ps_full")
        zmm = sem("zmm")
        relu = sem("relu")
        msg_s = sem("msg_s")
        full = sem("full")
        pe_n = sem("pe_n")
        act_n = sem("act_n")
        dve_n = sem("dve_n")
        pool_n = sem("pool_n")
        eq_s, diff_s, abs_s, mrg, summed, where = (sem(n) for n in ("eq_s", "diff_s", "abs_s", "mrg", "summed", "where"))

        W = {n: wts[:, k, :] for k, n in enumerate(WEIGHTS)}

        def row(name, blocks=CB):
            k = ROWS.index(name)
            return rows[:, k:k + 1, :].to_broadcast([128, blocks, D])

        def blk(c):
            return bass.ds(c * CB, CB)

        def nodes(c):
            return bass.ds(c * CW, CW)

        def per_node(v, c):
            return v[:, blk(c)].unsqueeze(2).to_broadcast([128, CB, D])

        def acc_rows(k, c):
            return acc[:, k, nodes(c)].rearrange("p (b f) -> p b f", f=D)

        side_fm = side[:, :, :].rearrange("p b f -> p (b f)")
        tab_rows = {t: d.rearrange("(b p) f -> p b f", p=128) for t, d in (("a", tab_a), ("b", tab_b))}
        out_rows = out.rearrange("(b p) f -> p b f", p=128)
        ps_z = ps[:, 3584:3712]
        BANKS = [(k, min(512, NP - k)) for k in range(0, NP, 512)]

        def ln_dve(t):
            return [t + "." + k for k in ("st", "mv", "ve", "r0", "r1", "r2", "r3", "co")]

        def ln_act(t):
            return [t + ".sd", t + ".out"]

        def both(n_lag, m_lag):
            return [(lag, [step]) for pair in zip(ln_dve("n"), ln_dve("m")) for lag, step in zip((n_lag, m_lag), pair)]

        GCN_STEPS = {
            "pe": [(0, ["ta", "mb"]), (2, ["tr", "mm"])],
            "act": [(0, ["sa", "sb"]), (1, ["n.sd"]), (2, ["hT"]), (1, ["n.out"]), (2, ["tab"])],
            "dve": [(1, ["z0", "z1", "z2"]), (2, ["b", "hd"]), (1, ln_dve("n"))],
            "pool": [(2, ["w"]), (0, ["c1", "c2"]), (1, ["cl"])],
        }
        STEPS = {
            "start": {
                "pe": [(1, ["tr", "mm"])],
                "act": [(0, ["xc"] + ln_act("m")), (1, ["hT", "tab"])],
                "dve": [(0, ln_dve("m"))],
            },
            "scale": {"dve": [(0, ["hd"])]},
            "gcn0": GCN_STEPS, "gcn1": GCN_STEPS,
            "gcn2": {
                "pe": [(0, ["ta", "mb"]), (3, ["tr", "mm", "mz"])],
                "act": [(0, ["sa", "sb"]), (3, ["hT"]), (1, ["n.sd"]), (2, ["m.sd"]), (2, ["xw"]), (1, ["n.out"]),
                        (2, ["m.out"]), (3, ["kp"])],
                "dve": [(1, ["z0", "z1", "z2"]), (2, ["b", "xn"])] + both(1, 2) + [(3, ["hn", "zs"])],
                "pool": [(2, ["w"]), (0, ["c1", "c2"]), (1, ["cl"])],
            },
            "sage": {
                "pe": [(1, ["tr", "mz"]), (0, ["ta", "tb"]), (2, ["tr2"]), (0, ["me"]), (2, ["mp", "mq", "mu"])],
                "act": [(1, ["hT"]), (0, ["sa", "sb"]), (2, ["hT2"]), (1, ["xw", "m.sd"]), (2, ["tp"]),
                        (1, ["m.out", "kp"]), (2, ["us"])],
                "dve": [(1, ["c1", "c3"]), (0, ["s2", "cn", "rc"]), (1, ["z0", "xn"] + ln_dve("m")), (2, ["tq"])],
                "pool": [(1, ["c0", "c2"]), (0, ["s0", "s1"])],
            },
            "mlp": {
                "pe": [(0, ["ag"]), (1, ["my"]), (0, ["mu"]), (3, ["tr", "ml"])],
                "act": [(0, ["sa"]), (3, ["hT"]), (2, ["xw"]), (1, ["n.sd"]), (2, ["m.sd"]), (0, ["ur"]),
                        (1, ["n.out"]), (2, ["m.out"]), (3, ["zs"])],
                "dve": [(2, ["w", "b"]), (1, ["y"]), (2, ["hb", "xn"])] + both(1, 2)[:6] + [(0, ["ua"])] + both(1, 2)[6:],
                "pool": [(1, ["cl"])],
            },
            "rel": {"pe": [(0, ["mn"])], "act": [(0, ["sa"])], "dve": [(0, ["c0", "c1", "c2"])]},
        }
        PHASES = list(STEPS)
        LAST_LAG = {ph: max(lag for stages in STEPS[ph].values() for lag, _ in stages) for ph in PHASES}
        STEP0 = 32
        done_in = {e: [] for e in ("pe", "act", "dve", "pool")}

        def names_of(e, ph):
            return [n for _, names in STEPS[ph].get(e, []) for n in names]

        def start_of(e, ph):
            return STEP0 + sum((CH + LAST_LAG[p]) * len(names_of(e, p)) for p in PHASES[:PHASES.index(ph)])

        def at(e, ph, c, name, back=0):
            names = names_of(e, ph)
            lag = [lag for lag, stage in STEPS[ph][e] if name in stage][0]
            return c * len(names) + (start_of(e, ph) + names.index(name) + 1 + (lag - back) * len(names))

        def end(e, ph):
            return start_of(e, ph) + (CH + LAST_LAG[ph]) * len(names_of(e, ph))

        step_sem = {"pe": pe_n, "act": act_n, "dve": dve_n, "pool": pool_n}

        def tick(e, ph, name, ins):
            assert name == names_of(e, ph)[len(done_in[e])], (e, ph, name)
            done_in[e].append(name)
            ins.then_inc(step_sem[e], 1)

        def over_chunks(eng, e, ph, *stages):
            names = names_of(e, ph)

            def body(k):
                for (lag, steps), stage in zip(STEPS[ph][e], stages, strict=True):
                    if isinstance(k, int) and not 0 <= k - lag < CH:
                        eng.wait_ge(step_sem[e], start_of(e, ph) + k * len(names) + len(done_in[e]))
                        eng.sem_inc(step_sem[e], len(steps))
                        done_in[e].extend(steps)
                    else:
                        stage(k - lag if lag else k)
                assert done_in[e] == names, (e, ph)
                done_in[e].clear()

            last = LAST_LAG[ph]
            for k in range(last):
                body(k)
            with eng.Fori(last, CH) as k:
                body(k)
            for k in range(CH, CH + last):
                body(k)

        STORES = {"start": 0, "scale": 1, "gcn0": 1, "gcn1": 1, "gcn2": 1, "sage": 2, "mlp": 1, "rel": 1}

        def stored_at(ph, c, k=0, back=0):
            before = sum(CH * STORES[p] for p in PHASES[:PHASES.index(ph)])
            return c * STORES[ph] + (1 + before + k + 1 - back * STORES[ph])

        def all_stored(ph):
            return stored_at(ph, CH - 1, STORES[ph] - 1)

        GRP_CHAIN = 10
        DEG_CHAIN = 25

        PASSES = ["gcn0", "gcn1", "gcn2", "sage", "mlp", "rel"]
        GCN = PASSES[0:3]
        BEFORE = dict(gcn0="scale", gcn1="gcn0", gcn2="gcn1", mlp="gcn2", rel="mlp")
        USED_IN = {
            "oh_made": GCN + ["mlp", "rel"],
            "z_made": GCN + ["sage", "mlp"],
            "relu_made": GCN + ["mlp"],
            "seg_made": GCN + ["mlp", "rel"],
            "win_added": GCN + ["mlp", "rel"],
            "ohT_made": ["sage", "mlp"],
            "mix_made": ["mlp"],
            "own_out": ["sage"],
            "typ_made": ["rel"],
            "cnt_made": ["rel"],
            "cnt_out": ["rel"],
        }
        half_sem = {n: sem(n) for n in USED_IN}

        def half(name, p, i, hf, back=0):
            return i * 2 + (hf + HALVES * USED_IN[name].index(p) + 5 - back)

        def dma_half(p, passes, i):
            return i * 16 + 16 * (ITERS * passes.index(p) + 1)

        def after_half(i, hf):
            return (i, 1) if hf == 0 else (i + 1, 0)

        ps_w = [ps[:, 1024 * k:1024 * k + 1024].rearrange("p (a k) -> p a k", a=2)[:, :, 0:WIN] for k in range(2)]
        ps_zh = [ps[:, 2048 + 512 * k:2560 + 512 * k] for k in range(2)]
        ps_c = [ps[0:TR, 3072 + 512 * k:3584 + 512 * k] for k in range(2)]

        def is_general(eng):
            eng.wait_ge(flag_made, 1)
            return eng.value_load(general[0:1, 0:1], min_val=0, max_val=1)

        TURNS = (ITERS - ITERS // 2, ITERS // 2)

        def iterations(eng, body):
            assert ITERS % 2
            body(0, (0, 0), False)
            with eng.Fori(0, (ITERS - 3) // 2) as m:
                body(m * 2 + 1, (1, m), False)
                body(m * 2 + 2, (0, m + 1), False)
            body(ITERS - 2, (1, TURNS[1] - 1), False)
            body(ITERS - 1, (0, TURNS[0] - 1), True)

        def turn_done(p, turn, back=0):
            parity, k = turn
            return k * 16 + 16 * (TURNS[parity] * PASSES.index(p) + 1 - back)

        def slot(turn, hf, j=0):
            return turn[0] * U + hf * H + j

        SHARE = ITERS // CH

        def degree_share(eng, c, iteration):
            with eng.Fori(0, SHARE) as j:
                iteration(c * SHARE + j)

        def degree_rest(eng, iteration):
            with eng.Fori(SHARE * CH, ITERS) as i:
                iteration(i)

        block = ctx.enter_context(nc.Block())

        @block.sync
        def _(sp):
            sp.sem_inc(stored, 1)
            sp.dma_start(grp_i, dstgrp_in).then_inc(in_small, 16)
            for k, (dst, src) in enumerate(((src_i, src_in), (dst_i, dst_in), (typ_i, typ_in))):
                sp.dma_start(dst[:, :], src).then_inc(in_small, 16)
            sp.dma_start(x[:, :, :], x_in).then_inc(in_x, 16)
            sp.dma_start(wts[:, :, :], w_in).then_inc(in_w, 16)
            sp.wait_ge(dve_c, 2)
            sp.dma_start(w1[0:DE + 1, :, :], w1_in).then_inc(in_w, 16)
            sp.dma_start(rows[:, :, :], rows_in.unsqueeze(0).to_broadcast([128, len(ROWS), D])).then_inc(in_w, 16)
            sp.dma_start(bu1_col[:, :], cols_in).then_inc(in_w, 16)
            sp.dma_start(rel_sb[:, :, :], relblk_in).then_inc(in_w, 16)
            sp.wait_ge(dve_c, GRP_CHAIN)
            sp.dma_start(grp_d, grp[0:HALVES, 2:4]).then_inc(grp_out, 16)
            sp.wait_ge(grp_out, 16)
            sp.dma_start(grp_bc[:, :, :], grp_d.unsqueeze(0).to_broadcast([128, HALVES, 2])).then_inc(grp_back, 16)
            for k in range(NACC):
                flat = acc_d[k].rearrange("(b p) f -> p b f", p=128)
                for b in range(NB + 1):
                    sp.dma_start(flat[:, b, :], zeros[:, 0:MS]).then_inc(zeroed, 16)
            sp.wait_ge(dve_c, DEG_CHAIN)
            sp.dma_start(deg_d.rearrange("b p -> p b"), deg[:, :], allow_slow_non_contiguous=True).then_inc(deg_out, 16)
            sp.wait_ge(deg_out, 16)
            sp.dma_start(deg_row[:, :], deg_d.rearrange("(a b) p -> a (b p)", a=1)).then_inc(deg_back, 16)

            def store_table(ph, dst, src, e, name):
                with sp.Fori(0, CH) as c:
                    sp.wait_ge(step_sem[e], at(e, ph, c, name))
                    sp.dma_start(dst[:, blk(c), :], src[:, :, :]).then_inc(store, 16)
                    sp.wait_ge(store, (stored_at(ph, c) - 1) * 16)
                    sp.sem_inc(stored, 1)

            zc = Count()

            def load_ea(layer):
                with sp.Fori(0, TILES) as t:
                    zc.enter(t, 1)
                    sp.wait_ge(zmm, zc.next(back=1))
                    sp.dma_start(ea_t[0:DE + 1, :], ea_in[:, bass.ds(t * 128, 128)]).then_inc(ea_in_s, 16)
                zc.leave(TILES)

            def load_col(p, i, turn, hf):
                if not (p == PASSES[0] and isinstance(i, int) and i < 2):
                    for j in range(H):
                        sp.wait_ge(fa_in[slot(turn, hf, j)], turn_done(p, turn, back=1))
                sp.dma_start(col[:, hf, turn[0], :], src_in[:, bass.ds(i * U + hf * H, H)])\
                  .then_inc(col_in[turn[0] * 2 + hf], 16)

            def next_col(p, i, turn, hf):
                if not isinstance(i, int) or i:
                    load_col(p, i, turn, hf)

            def load_cols(p):
                def body(i, turn, last):
                    for hf in range(2):
                        next_col(p, i, turn, hf)
                iterations(sp, body)

            def load_ea_halves(p):
                def body(i, turn, last):
                    for hf in range(2):
                        next_col(p, i, turn, hf)
                        sp.wait_ge(half_sem["z_made"], half("z_made", p, i, hf, back=2))
                        sp.dma_start(ea_r[0:DE + 1, hf, :], ea_in[:, bass.ds((i * U + hf * H) * 128, H * 128)])\
                          .then_inc(ea_h[hf], 16)
                iterations(sp, body)

            def load_windows(p):
                table = tab_a if p == "sage" else tab_b

                def body(i, turn, last):
                    _, first = nc.values_load_multi_w_load_instructions(
                        base_row[0:1, bass.ds(i * 2, 2)], engines=[mybir.EngineType.SP], min_val=0, max_val=NP - WIN)
                    for hf in range(2):
                        tile = i * U + hf * H
                        next_col(p, i, turn, hf)
                        sp.wait_ge(half_sem["ohT_made"], half("ohT_made", p, i, hf, back=2))
                        sp.dma_start(drow[:, hf, :], dstrow_in[:, bass.ds(tile * 128, H * 128)]
                                     .to_broadcast([128, H * 128])).then_inc(drow_in[hf], 16)
                        sp.wait_ge(half_sem["z_made"], half("z_made", p, i, hf, back=2))
                        sp.dma_start(win[:, hf, :], table[bass.ds(first[hf], WIN), :]).then_inc(win_in[hf], 16)
                        if p == "sage":
                            load_srow(i, hf)
                iterations(sp, body)

            def load_srow(i, hf):
                tile = i * U + hf * H
                sp.wait_ge(eq_s, i * 2 + (hf + 1))
                sp.dma_start(srow[:, hf, :], srcrow_in[:, bass.ds(tile * 128, H * 128)]
                             .to_broadcast([128, H * 128])).then_inc(srow_in[hf], 16)

            def load_first_cols(p):
                with sp.If(unfitting == 0):
                    for hf in range(2):
                        load_col(p, 0, (0, 0), hf)
                with sp.Else():
                    sp.sem_inc(passed, 1)

            unfitting = is_general(sp)
            load_first_cols("gcn0")
            with sp.Fori(0, CH) as c:
                sp.wait_ge(dve_n, at("dve", "scale", c, "hd"))
                sp.dma_start(tab_rows["a"][:, blk(c), :], side[:, blk(c), :]).then_inc(store, 16)
            sp.wait_ge(store, 16 * CH)
            sp.sem_inc(stored, CH)
            for layer in range(LAYERS):
                with sp.If(unfitting == 0):
                    load_ea_halves(f"gcn{layer}")
                with sp.Else():
                    load_ea(layer)
                load_first_cols(PASSES[layer + 1])
                if layer < LAYERS - 1:
                    store_table(f"gcn{layer}", tab_rows["a"], tb, "act", "tab")
            store_table("gcn2", tab_rows["a"], tb, "dve", "hn")

            with sp.If(unfitting == 0):
                load_windows("sage")
            with sp.Else():
                with sp.Fori(0, ITERS) as i:
                    for hf in range(2):
                        load_srow(i, hf)

            load_first_cols("mlp")

            for k in range(NACC):
                sp.wait_ge(added[k], 32 * ITERS)

            def load_sums(c):
                for k in range(NACC):
                    if k % 2 == 0:
                        sp.wait_ge(pool_n, at("pool", "sage", c, f"s{k // 2}", back=1))
                    sp.dma_start(sm[:, k, :, :], acc_d[k].rearrange("(b p) f -> p b f", p=128)[:, blk(c), :])\
                      .then_inc(sm_in[k // 2], 16)

            def store_parts(c):
                for k, (e, name, dst, src) in enumerate((("act", "tp", "a", tb), ("dve", "tq", "b", m_bb))):
                    sp.wait_ge(step_sem[e], at(e, "sage", c, name))
                    sp.dma_start(tab_rows[dst][:, blk(c), :], src[:, :, :]).then_inc(store, 16)
                    sp.wait_ge(store, (stored_at("sage", c, k) - 1) * 16)
                    sp.sem_inc(stored, 1)

            for c in range(3):
                load_sums(c)
            with sp.Fori(0, CH - 3) as c:
                load_sums(c + 3)
                store_parts(c)
            for c in range(CH - 3, CH):
                store_parts(c)

            with sp.If(unfitting == 0):
                load_windows("mlp")
            with sp.Else():
                sp.sem_inc(passed, 1)
            load_first_cols("rel")
            store_table("mlp", tab_rows["a"], m_bb, "act", "m.out")
            with sp.If(unfitting == 0):
                load_cols("rel")
            with sp.Else():
                sp.sem_inc(passed, 1)
            store_table("rel", out_rows, tb, "dve", "c2")
            sp.wait_ge(store, (all_stored("rel") - 1) * 16)


        @block.gpsimd
        def _(pool):
            pool.sem_inc(pool_c, 1)
            pool.sem_inc(pool_n, STEP0)
            pool.iota(iota_i[:, :], pattern=[[1, NP]], base=0, channel_multiplier=0).then_inc(consts, 1)
            pool.memset(ident[:, :], 0.0).then_inc(consts, 1)
            pool.memset(lower[:, :], 1.0).then_inc(consts, 1)
            pool.wait_ge(consts, 3)
            pool.affine_select(out=ident[:, :], in_=ident[:, :], compare_op=ALU.not_equal, fill=1.0, base=0,
                               pattern=[[-1, 128]], channel_multiplier=1).then_inc(consts, 1)
            pool.affine_select(out=lower[:, :], in_=lower[:, :], compare_op=ALU.is_gt, fill=0.0, base=0,
                               pattern=[[-1, 128]], channel_multiplier=1).then_inc(consts, 1)
            pool.iota(col[:, 0, 0, 0:1], pattern=[[1, 1]], base=DUMP, channel_multiplier=1).then_inc(consts, 1)
            pool.iota(col[:, 0, 0, 1:2], pattern=[[1, 1]], base=0, channel_multiplier=1).then_inc(consts, 1)
            pool.wait_ge(consts, 7)
            pool.tensor_copy(dump[:, :], col[:, 0, 0, 0:1]).then_inc(consts, 1)
            pool.tensor_copy(iota_p[:, :], col[:, 0, 0, 1:2]).then_inc(consts, 1)
            pool.memset(acc[:, :, :], 0.0).then_inc(acc_clear, 1)
            pool.wait_ge(in_small, 64)

            copies, segs = Count(), Count()

            def gather(g, table, index, signal):
                pool.indirect_dma_start(g, None, table, bass.IndirectOffsetOnAxis(ap=index, axis=0)).then_inc(signal, 16)

            def gather_pass(ph, second):
                pool.wait_ge(stored, all_stored(ph))
                with pool.Fori(0, TILES) as t:
                    copies.enter(t, 2)
                    segs.enter(t, 1)
                    pool.wait_ge(seg, segs.next(back=1))
                    pool.tensor_copy(col[:, 0, 0, 0:1], src_i[:, bass.ds(t, 1)]).then_inc(pool_c, 1)
                    other = src_i if second is None else second[1]
                    copies.next()
                    pool.tensor_copy(col[:, 0, 1, 0:1], other[:, bass.ds(t, 1)]).then_inc(pool_c, 1)
                    pool.wait_ge(pool_c, copies.next())
                    pool.sem_inc(passed, 1)
                    gather(g_a[:, 0, :], tab_a, col[:, 0, 0, 0:1], ga_in[0])
                    if second is not None:
                        gather(msg[:, 0, 0:D], second[0], col[:, 0, 1, 0:1], gb_in[0])
                copies.leave(TILES)
                segs.leave(TILES)

            def gather_half(p, i, turn, hf, free):
                free(i, hf)
                pool.wait_ge(col_in[turn[0] * 2 + hf], turn_done(p, turn))
                pool.sem_inc(passed, 1)
                for j in range(H):
                    r = slot(turn, hf, j)
                    gather(g_a[:, r, :], tab_a, col[:, hf, turn[0], j:j + 1], fa_in[r])

            def gather_windows(p, ph):
                pool.wait_ge(stored, all_stored(ph))
                reader = {"mlp": "mix_made"}.get(p, "seg_made")

                def free(i, hf):
                    pool.wait_ge(half_sem[reader], half(reader, p, i, hf, back=4))

                def body(i, turn, last):
                    for hf in range(2):
                        gather_half(p, i, turn, hf, free)
                iterations(pool, body)

            def times_weight(ph, c, weight):
                pool.wait_ge(act_n, at("act", ph, c, "n.out"))
                pool.sem_inc(passed, 1)
                tick("pool", ph, "w", pool.tensor_tensor(hh[:, :, :], hh[:, :, :], row(weight), ALU.mult))

            def clear(ph, c, e, reader, parts):
                pool.wait_ge(step_sem[e], at(e, ph, c, reader))
                pool.sem_inc(passed, 1)
                none = zeros[:, 0:D].unsqueeze(1).to_broadcast([128, parts * CB, D])
                tick("pool", ph, "cl", pool.tensor_copy(
                    acc[:, 0:parts, nodes(c)].rearrange("p a (b f) -> p a b f", f=D),
                    none.rearrange("p (a b) f -> p a b f", a=parts)))

            unfitting = is_general(pool)
            for layer in range(LAYERS):
                ph = ("scale", "gcn0", "gcn1")[layer]
                with pool.If(unfitting == 0):
                    gather_windows(f"gcn{layer}", ph)
                with pool.Else():
                    gather_pass(ph, None)
                    segs.n += TILES
                ph = f"gcn{layer}"

                def bias_terms(c):
                    bt = acc_rows(1, c)
                    pool.wait_ge(act_n, at("act", ph, c, "sb"))
                    pool.sem_inc(passed, 1)
                    tick("pool", ph, "c1", pool.tensor_tensor(bt, row(f"eb{layer}"), per_node(deg, c), ALU.mult))
                    pool.wait_ge(pool_n, at("pool", ph, c, "c1"))
                    pool.sem_inc(passed, 1)
                    tick("pool", ph, "c2", pool.tensor_tensor(bt, bt, row(f"bias{layer}"), ALU.add))

                over_chunks(pool, "pool", ph, lambda c: times_weight(ph, c, f"lnw{layer}"), bias_terms,
                            lambda c: clear(ph, c, "dve", "z2", 2 if ph != "gcn2" else 1))

            pool.wait_ge(stored, all_stored("gcn2"))
            pool.wait_ge(zeroed, 16 * NACC * (NB + 1))

            def gathers(i, hf, first):
                r0, tile = hf * H, i * U + hf * H
                if not first:
                    pool.wait_ge(mrg, i * 2 + hf - 1 + 1)
                pool.tensor_copy(col[:, hf, 0, :], src_i[:, bass.ds(tile, H)]).then_inc(pool_c, 1)
                copies.next()
                pool.tensor_copy(col[:, hf, 1, :], dst_i[:, bass.ds(tile, H)]).then_inc(pool_c, 1)
                pool.wait_ge(pool_c, copies.next())
                pool.sem_inc(passed, 1)
                for j in range(H):
                    gather(g_a[:, r0 + j, :], tab_a, col[:, hf, 0, j:j + 1], ga_in[r0 + j])
                    gather(msg[:, r0 + j, 0:D], tab_a, col[:, hf, 1, j:j + 1], gb_in[r0 + j])

            def scatters(i, hf, first=False):
                pool.wait_ge(where, i * 2 + hf + 2)
                pool.wait_ge(summed, i * 2 + hf + 2)
                for j in range(H):
                    if not first:
                        pool.wait_ge(added[j], i * 32 + 16 * hf)
                    pool.sem_inc(passed, 1)
                    pool.indirect_dma_start(acc_d[j], bass.IndirectOffsetOnAxis(ap=where_i[:, hf, j:j + 1], axis=0),
                                            sums[:, hf * H + j, :], None, compute_op=ALU.add).then_inc(added[j], 16)

            def diffs_done(i, hf):
                pool.wait_ge(diff_s, i * 2 + hf)

            def sage_turn(i, turn, last):
                first = isinstance(i, int) and i == 0
                free = (lambda i, hf: None) if first else diffs_done
                gather_half("sage", i, turn, 0, free)
                if not first:
                    scatters(i - 1, 1)
                gather_half("sage", i, turn, 1, free)
                scatters(i, 0, first)
                if last:
                    scatters(i, 1)

            with pool.If(unfitting == 0):
                iterations(pool, sage_turn)
            with pool.Else():
                gathers(0, 0, True)
                gathers(0, 1, True)
                scatters(0, 0, True)
                with pool.Fori(1, ITERS) as i:
                    copies.enter(i, 4, 1)
                    gathers(i, 0, False)
                    scatters(i - 1, 1)
                    gathers(i, 1, False)
                    scatters(i, 0)
                copies.leave(ITERS - 1)
                scatters(ITERS - 1, 1)

            def half_sum(c):
                pool.wait_ge(dve_n, at("dve", "sage", c, "s2", back=1))
                for k in range(2):
                    pool.wait_ge(sm_in[k], c * 32 + 32)
                    pool.sem_inc(passed, 1)
                    tick("pool", "sage", f"s{k}",
                         pool.tensor_tensor(pair[:, k, :, :], sm[:, 2 * k, :, :], sm[:, 2 * k + 1, :, :], ALU.add))

            def bias_counted(c):
                pool.wait_ge(dve_n, at("dve", "sage", c, "s2"))
                pool.wait_ge(dve_n, at("dve", "sage", c, "c3", back=1))
                pool.sem_inc(passed, 1)
                tick("pool", "sage", "c0", pool.tensor_tensor(
                    m_ab, row("b_edge"), summ[:, :, 2 * D:].to_broadcast([128, CB, D]), ALU.mult))
                pool.wait_ge(pool_n, at("pool", "sage", c, "c0"))
                pool.sem_inc(passed, 1)
                tick("pool", "sage", "c2", pool.tensor_tensor(m_ab, m_ab, keep[:, blk(c), :], ALU.add))

            over_chunks(pool, "pool", "sage", bias_counted, half_sum)

            for p, ph, second in (("mlp", "sage", (tab_b, dst_i)), ("rel", "mlp", (rel_in, typ_i))):
                with pool.If(unfitting == 0):
                    gather_windows(p, ph)
                with pool.Else():
                    gather_pass(ph, second)
                if p == "mlp":
                    over_chunks(pool, "pool", "mlp", lambda c: clear("mlp", c, "pe", "ag", 1))

        @block.vector
        def _(dve):
            dve.sem_inc(hot, 1)
            dve.sem_inc(eq_s, 2)
            dve.sem_inc(dve_n, STEP0)
            dve.sem_inc(msg_s, 1)
            for n in ("oh_made", "win_added", "ohT_made", "mix_made", "typ_made"):
                dve.sem_inc(half_sem[n], 4)
            dve.sem_inc(diff_s, 3)
            dve.sem_inc(where, 1)
            chain = Count(start=0)

            def link(ins):
                ins.then_inc(dve_c, 1)
                dve.wait_ge(dve_c, chain.next())

            link(dve.memset(zeros[:, :], 0.0))
            link(dve.memset(w1[:, :, :], 0.0))
            link(dve.memset(ea_t[:, :], 0.0))
            link(dve.memset(msg[:, :, 2 * D:], 1.0))
            dve.wait_ge(in_small, 64)
            dve.wait_ge(consts, 9)
            link(dve.tensor_copy(grp_f, grp_i))
            link(dve.tensor_reduce(grp[0:HALVES, 0:1], grp_f, AX.X, ALU.min))
            link(dve.tensor_reduce(grp[0:HALVES, 1:2], grp_f, AX.X, ALU.max))
            link(dve.tensor_scalar(grp[0:HALVES, 2:3], grp[0:HALVES, 0:1], float(NP - WIN), None, ALU.min))
            link(dve.tensor_tensor(grp[0:HALVES, 4:5], grp[0:HALVES, 1:2], grp[0:HALVES, 2:3], ALU.subtract))
            link(dve.tensor_scalar(grp[0:HALVES, 3:4], grp[0:HALVES, 4:5], float(WIN - 1), None, ALU.is_gt))
            assert chain.n == GRP_CHAIN
            link(dve.tensor_copy(iota[:, :], iota_i[:, :]))
            link(dve.tensor_copy(src_f[:, :], src_i[:, :]))
            link(dve.tensor_copy(dst_f[:, :], dst_i[:, :]))
            link(dve.tensor_copy(typ_f[:, :], typ_i[:, :]))
            link(dve.tensor_scalar(lo_i[:, :], dst_i[:, :], 127, None, ALU.bitwise_and))
            link(dve.tensor_scalar(hi_i[:, :], dst_i[:, :], 7, None, ALU.logical_shift_right))
            link(dve.tensor_copy(lo_f[:, :], lo_i[:, :]))
            link(dve.tensor_copy(hi_f[:, :], hi_i[:, :]))
            link(dve.tensor_copy(iota_b[:, :], iota[:, 0:128]))

            dve.wait_ge(in_x, 16)
            dve.wait_ge(in_w, 80)

            def step(ph, name, ins):
                tick("dve", ph, name, ins)

            def after(ph, c, name):
                dve.wait_ge(dve_n, at("dve", ph, c, name))

            def ln_steps(ph, t, src, written):
                v, sd, y, part, inv, shift = (lns[t][:, k, :] for k in range(6))

                def make_stats(c):
                    if written:
                        after(ph, c, written)
                    for k in range(CB):
                        last = dve.bn_stats(stats[t][:, k, :], src[:, k, :])
                    return last

                def make_mean(c):
                    after(ph, c, t + ".st")
                    dve.sem_inc(passed, 1)
                    for k in range(CB):
                        last = dve.bn_aggr(mv[t][:, k, :], stats[t][:, k, :])
                    return last

                def add_eps(c):
                    after(ph, c, t + ".mv")
                    return dve.tensor_scalar(v, mv[t][:, :, 1], EPS, None, ALU.add)

                def invert(c):
                    dve.wait_ge(act_n, at("act", ph, c, t + ".sd"))
                    return dve.reciprocal(y, sd)

                def newton1(c):
                    after(ph, c, t + ".r0")
                    return dve.scalar_tensor_tensor(out=part, in0=y, scalar=-0.5, in1=y, op0=ALU.mult, op1=ALU.mult)

                def newton2(c):
                    after(ph, c, t + ".r1")
                    return dve.tensor_tensor(part, part, v, ALU.mult)

                def newton3(c):
                    after(ph, c, t + ".r2")
                    return dve.scalar_tensor_tensor(out=inv, in0=part, scalar=1.5, in1=y, op0=ALU.add, op1=ALU.mult)

                def make_shift(c):
                    after(ph, c, t + ".r3")
                    return dve.scalar_tensor_tensor(out=shift, in0=mv[t][:, :, 0], scalar=-1.0, in1=inv,
                                                    op0=ALU.mult, op1=ALU.mult)

                makers = (make_stats, make_mean, add_eps, invert, newton1, newton2, newton3, make_shift)
                return [lambda c, n=n, make=make: step(ph, n, make(c)) for n, make in zip(ln_dve(t), makers, strict=True)]

            def ln(ph, c, t, src, written=None):
                for run in ln_steps(ph, t, src, written):
                    run(c)

            def in_turn(n_steps, m_steps):
                return [run for pair in zip(n_steps, m_steps) for run in pair]

            def psv(p):
                return p.rearrange("p (b f) -> p b f", f=D)

            def add_bias(ph, c, b):
                dve.wait_ge(pool_n, at("pool", ph, c, "w"))
                step(ph, "b", dve.tensor_tensor(hh[:, :, :], hh[:, :, :], row(b), ALU.add))
                after(ph, c, "b")

            def hot_iteration(i):
                for hf in range(2):
                    dve.wait_ge(deg_mm, i * 2 + hf + 1)
                    for hot_rows, part, width in ((oh_lo, lo_f, 128), (oh_hi, hi_f, NB)):
                        dve.tensor_tensor(hot_rows[:, hf * H:hf * H + H, :],
                                          iota_b[:, 0:width].unsqueeze(1).to_broadcast([128, H, width]),
                                          part[:, bass.ds(i * U + hf * H, H)].unsqueeze(2).to_broadcast([128, H, width]),
                                          ALU.is_equal).then_inc(hot, 1)

            def start_norm(c):
                dve.wait_ge(act_n, at("act", "start", c, "xc"))
                ln("start", c, "m", ta)
                degree_share(dve, c, hot_iteration)

            over_chunks(dve, "dve", "start", start_norm)
            degree_rest(dve, hot_iteration)

            dve.wait_ge(grp_back, 16)
            link(dve.tensor_copy(base_row[:, :], grp_bc[0:1, :, 0]))
            link(dve.tensor_reduce(unfit[:, :], grp_bc[0:1, :, 1], AX.X, ALU.max))
            link(dve.tensor_copy(general[:, :], unfit[:, :]))
            link(dve.tensor_tensor(rel_dst[:, :].rearrange("p (g h) -> p g h", h=H),
                                   dst_f[:, :].rearrange("p (g h) -> p g h", h=H),
                                   grp_bc[:, :, 0:1].to_broadcast([128, HALVES, H]), ALU.subtract))
            link(dve.tensor_scalar(first_p[:, :], grp_bc[:, :, 0], iota_p[:, 0:1], None, ALU.add))
            dve.sem_inc(flag_made, 1)

            hots = Count()
            hots.n += 4 * ITERS
            dve.wait_ge(deg_mm, HALVES + 3)
            link(dve.tensor_copy(deg[:, :], ps[:, 0:NB]))
            link(dve.tensor_scalar(small[:, 0, :], deg[:, :], 1.0, None, ALU.max))
            chain_sq = chain.n
            dve.wait_ge(act_c, 1)
            link(dve.reciprocal(small[:, 2, :], small[:, 1, :]))
            link(dve.tensor_tensor(small[:, 3, :], small[:, 2, :], small[:, 2, :], ALU.mult))
            link(dve.tensor_tensor(small[:, 3, :], small[:, 3, :], small[:, 0, :], ALU.mult))
            link(dve.tensor_scalar(small[:, 3, :], small[:, 3, :], -0.5, 1.5, ALU.mult, ALU.add))
            link(dve.tensor_tensor(norm[:, :], small[:, 2, :], small[:, 3, :], ALU.mult))
            link(dve.tensor_scalar(small[:, 4, :], deg[:, :], 0.0, None, ALU.is_gt))
            link(dve.tensor_tensor(dis[:, :], norm[:, :], small[:, 4, :], ALU.mult))
            assert chain.n == DEG_CHAIN + 8 and chain_sq == DEG_CHAIN + 1, (chain.n, chain_sq)

            dve.wait_ge(act_n, end("act", "start"))
            over_chunks(dve, "dve", "scale", lambda c: step("scale", "hd", dve.tensor_tensor(
                side[:, blk(c), :], side[:, blk(c), :], per_node(dis, c), ALU.mult)))

            def one_hot_pass(mix=None):
                with dve.Fori(0, TILES) as t:
                    hots.enter(t, 1)
                    segs.enter(t, 1)
                    dve.wait_ge(seg, segs.next(back=1))
                    dve.tensor_scalar(big[:, :], iota[:, :], dst_f[:, bass.ds(t, 1)], None, ALU.is_equal).then_inc(hot, 1)
                    hots.next()
                    if mix is not None:
                        mixes.enter(t, 1)
                        loads.enter(t, 1)
                        dve.wait_ge(ga_in[0], loads.next())
                        dve.wait_ge(gb_in[0], 16 * t + 16 * mix[1])
                        dve.tensor_tensor(mix[0], g_a[:, 0, :], msg[:, 0, 0:D], ALU.add).then_inc(msg_s, 1)
                        mixes.next()
                hots.leave(TILES)
                segs.leave(TILES)
                if mix is not None:
                    mixes.leave(TILES)
                    loads.leave(TILES)

            segs, mixes, loads = Count(), Count(), Count(by=16, start=0)
            unfitting = is_general(dve)

            def bases(i, first, last):
                start, n = (0, 1) if first else (i * 2 - 1, 3 if last else 2)
                _, values = nc.values_load_multi_w_load_instructions(
                    base_row[0:1, bass.ds(start, n)], engines=[mybir.EngineType.DVE], min_val=0, max_val=NP - WIN)
                return ([None] if first else []) + list(values)

            def one_hot_half(p, i, hf):
                dve.wait_ge(half_sem["seg_made"], half("seg_made", p, i, hf, back=2))
                dve.tensor_tensor(oh[:, hf, :, :], iota[:, 0:WIN].unsqueeze(1).to_broadcast([128, H, WIN]),
                                  rel_dst[:, bass.ds(i * U + hf * H, H)].unsqueeze(2).to_broadcast([128, H, WIN]),
                                  ALU.is_equal).then_inc(half_sem["oh_made"], 1)

            def one_hot_T_half(p, i, hf):
                dve.wait_ge(drow_in[hf], dma_half(p, ["sage", "mlp"], i))
                dve.wait_ge(half_sem["z_made"], half("z_made", p, i, hf, back=2))
                dve.tensor_scalar(ohT[:, hf, :], drow[:, hf, :], first_p[:, bass.ds(i * 2 + hf, 1)], None, ALU.is_equal)\
                   .then_inc(half_sem["ohT_made"], 1)

            def add_window(p, i, hf, first, parts):
                dve.wait_ge(half_sem["seg_made"], half("seg_made", p, i, hf))
                dve.wait_ge(half_sem["win_added"], half("win_added", p, i, hf, back=1))
                there = acc[:, 0:parts, bass.ds(first, WIN)]
                dve.tensor_tensor(there, there, ps_w[hf][:, 0:parts, :], ALU.add).then_inc(half_sem["win_added"], 1)

            def nothing(*_):
                pass

            def window_pass(p, parts, ahead=nothing, this=nothing, with_hot=nothing):
                if p == "gcn0":
                    dve.wait_ge(acc_clear, 1)
                else:
                    dve.wait_ge(pool_n, end("pool", BEFORE[p]))
                ahead(p, 0, 0)
                one_hot_half(p, 0, 0)
                with_hot(p, 0, 0)

                def body(i, turn, last):
                    first = isinstance(i, int) and i == 0
                    start = bases(i, first, last)
                    for hf in range(2):
                        end_of_pass = last and hf
                        if not end_of_pass:
                            ahead(p, *after_half(i, hf))
                        this(p, i, turn, hf)
                        if not (first and hf == 0):
                            add_window(p, *((i - 1, 1) if hf == 0 else (i, 0)), start[hf], parts)
                        if not end_of_pass:
                            one_hot_half(p, *after_half(i, hf))
                            with_hot(p, *after_half(i, hf))
                    if last:
                        add_window(p, i, 1, start[2], parts)
                iterations(dve, body)

            def mix_half(p, i, turn, hf):
                for j in range(H):
                    dve.wait_ge(fa_in[slot(turn, hf, j)], turn_done(p, turn))
                dve.wait_ge(half_sem["z_made"], half("z_made", p, i, hf))
                dve.wait_ge(half_sem["relu_made"], half("relu_made", p, i, hf, back=2))
                dve.tensor_tensor(diff[:, hf, :, :], g_a[:, slot(turn, hf):slot(turn, hf) + H, :],
                                  ps_zh[hf].rearrange("p (j f) -> p j f", j=H), ALU.add)\
                   .then_inc(half_sem["mix_made"], 1)

            def types_half(p, i, hf):
                dve.wait_ge(half_sem["cnt_made"], half("cnt_made", p, i, hf, back=2))
                dve.tensor_tensor(oh_typ[:, hf, :, :], iota[:, 0:NRELS].unsqueeze(1).to_broadcast([128, H, NRELS]),
                                  typ_f[:, bass.ds(i * U + hf * H, H)].unsqueeze(2).to_broadcast([128, H, NRELS]),
                                  ALU.is_equal)

            def narrow_half(p, i, hf):
                dve.wait_ge(half_sem["cnt_made"], half("cnt_made", p, i, hf, back=2))
                dve.wait_ge(half_sem["oh_made"], half("oh_made", p, i, hf))
                dve.tensor_copy(oh16[:, hf, :, :], oh[:, hf, :, :]).then_inc(half_sem["typ_made"], 1)

            for layer in range(LAYERS):
                ph = f"gcn{layer}"
                loads.n += TILES
                with dve.If(unfitting == 0):
                    window_pass(f"gcn{layer}", 2)
                with dve.Else():
                    one_hot_pass()
                    one_hot_pass()

                def unite(c):
                    z = acc_rows(0, c)
                    dve.wait_ge(pe_n, at("pe", ph, c, "ta"))
                    dve.wait_ge(act_n, at("act", ph, c, "sa"))
                    step(ph, "z0", dve.tensor_tensor(z, psv(ps_t), per_node(dis, c), ALU.mult))
                    after(ph, c, "z0")
                    dve.wait_ge(pe_n, at("pe", ph, c, "mb"))
                    step(ph, "z1", dve.tensor_tensor(z, z, psv(ps_m), ALU.add))
                    after(ph, c, "z1")
                    dve.wait_ge(pool_n, at("pool", ph, c, "c2"))
                    dve.wait_ge(act_n, at("act", ph, c, "n.out", back=1))
                    step(ph, "z2", dve.tensor_tensor(rows_of_z[:, :, :], z, acc_rows(1, c), ALU.add))

                def scaled(c):
                    add_bias(ph, c, f"lnb{layer}")
                    dve.wait_ge(pe_n, at("pe", ph, c, "tr", back=1))
                    step(ph, "hd", dve.scalar_tensor_tensor(out=o[:, :, :], in0=hh[:, :, :], scalar=0.0,
                                                            in1=per_node(dis, c), op0=ALU.max, op1=ALU.mult))

                def onto_x(c):
                    add_bias(ph, c, f"lnb{layer}")
                    dve.wait_ge(act_n, at("act", ph, c, "m.out", back=1))
                    step(ph, "xn", dve.scalar_tensor_tensor(out=ta[:, :, :], in0=hh[:, :, :], scalar=0.0,
                                                            in1=x[:, blk(c), :], op0=ALU.max, op1=ALU.add))

                def layer1_parts(c):
                    dve.wait_ge(pe_n, at("pe", ph, c, "mm"))
                    dve.wait_ge(stored, stored_at(ph, c, back=1))
                    dve.wait_ge(act_n, at("act", ph, c, "kp", back=1))
                    step(ph, "hn", dve.tensor_tensor(tb[:, :, :], psv(ps_o), row("b_neigh"), ALU.add))
                    dve.wait_ge(pe_n, at("pe", ph, c, "mz"))
                    step(ph, "zs", dve.tensor_tensor(side[:, blk(c), :], psv(ps_h), row("b_lin"), ALU.add))

                if layer < LAYERS - 1:
                    rows_of_z = ta
                    over_chunks(dve, "dve", ph, unite, scaled, lambda c: ln(ph, c, "n", ta, "z2"))
                else:
                    rows_of_z = z_rows
                    over_chunks(dve, "dve", ph, unite, onto_x,
                                *in_turn(ln_steps(ph, "n", z_rows, "z2"), ln_steps(ph, "m", ta, "xn")), layer1_parts)

            def edge_half(i, turn, hf, prior, windows, last):
                tile = i * U + hf * H
                r = slice(hf * H, hf * H + H)
                mine = slice(slot(turn, hf), slot(turn, hf) + H) if windows else r
                if windows and not last:
                    one_hot_T_half("sage", *after_half(i, hf))
                here = src_f[:, bass.ds(tile, H)]
                dve.wait_ge(srow_in[hf], i * 16 + 16)
                dve.wait_ge(mrg, i * 2 + hf + 0 if prior else 1)
                dve.tensor_tensor(eq[:, hf, :, :], srow[:, hf, :].rearrange("p (j k) -> p j k", j=H),
                                  here.unsqueeze(2).to_broadcast([128, H, 128]), ALU.is_equal).then_inc(eq_s, 1)
                dve.wait_ge(eq_s, i * 2 + hf + 3)
                lchain(i, dve.tensor_tensor(junk[:, hf, :, :], eq[:, hf, :, :],
                                            lower[:, :].unsqueeze(1).to_broadcast([128, H, 128]), ALU.mult))
                lchain(i, dve.tensor_reduce(before[:, hf, :], junk[:, hf, :, :], AX.X, ALU.add))
                lchain(i, dve.tensor_scalar(bsel[:, hf, 0, :], before[:, hf, :], 0.0, None, ALU.is_gt))
                lchain(i, dve.tensor_tensor(bsel[:, hf, 1, :], dump[:, 0:1].to_broadcast([128, H]), here, ALU.subtract))
                lchain(i, dve.tensor_tensor(bsel[:, hf, 2, :], bsel[:, hf, 0, :], bsel[:, hf, 1, :], ALU.mult))
                for j in range(H if prior else 0):
                    dve.wait_ge(added[j], i * 32 + 16 * (hf - 1))
                dve.tensor_tensor(where_i[:, hf, :], bsel[:, hf, 2, :], here, ALU.add).then_inc(where, 1)
                dve.wait_ge(abs_s, i * 2 + hf + 0 if prior else 1)
                if windows:
                    for j in range(H):
                        dve.wait_ge(fa_in[slot(turn, hf, j)], turn_done("sage", turn))
                    dve.wait_ge(half_sem["own_out"], half("own_out", "sage", i, hf))
                    other = ps_zh[hf].rearrange("p (j f) -> p j f", j=H)
                else:
                    for j in range(H):
                        dve.wait_ge(ga_in[hf * H + j], (LAYERS * TILES * 16 if hf * H + j == 0 else 0) + 16 + i * 16)
                        dve.wait_ge(gb_in[hf * H + j], i * 16 + 16)
                    other = msg[:, r, 0:D]
                dve.tensor_tensor(diff[:, hf, :, :], g_a[:, mine, :], other, ALU.subtract).then_inc(diff_s, 1)

            def lchain(i, ins):
                ins.then_inc(dve_c, 1)
                dve.wait_ge(dve_c, chain.next())

            def sage_general():
                edge_half(0, None, 0, False, False, False)
                edge_half(0, None, 1, False, False, False)
                with dve.Fori(1, ITERS) as i:
                    chain.enter(i, 10, 1)
                    edge_half(i, None, 0, True, False, False)
                    edge_half(i, None, 1, True, False, False)
                chain.leave(ITERS - 1)

            def sage_windows():
                def both_halves(i, turn, prior=True, last=False):
                    edge_half(i, turn, 0, prior, True, False)
                    edge_half(i, turn, 1, prior, True, last)

                one_hot_T_half("sage", 0, 0)
                both_halves(0, (0, 0), prior=False)
                with dve.Fori(0, (ITERS - 3) // 2) as m:
                    chain.enter(m, 20)
                    both_halves(m * 2 + 1, (1, m))
                    both_halves(m * 2 + 2, (0, m + 1))
                chain.leave((ITERS - 3) // 2)
                both_halves(ITERS - 2, (1, TURNS[1] - 1))
                both_halves(ITERS - 1, (0, TURNS[0] - 1), last=True)

            chain_now = chain.n
            with dve.If(unfitting == 0):
                sage_windows()
            chain.n = chain_now
            with dve.Else():
                sage_general()

            ph = "sage"

            def near_and_far(c):
                dve.wait_ge(pe_n, at("pe", "sage", c, "me"))
                dve.wait_ge(pool_n, at("pool", "sage", c, "c2"))
                step("sage", "c1", dve.tensor_tensor(m_ab, m_ab, psv(ps_o), ALU.add))
                after("sage", c, "c1")
                dve.wait_ge(pe_n, at("pe", "sage", c, "tr", back=1))
                step("sage", "c3", dve.tensor_tensor(o[:, :, :], m_ab,
                                                     rcnt[:, 1, :].unsqueeze(2).to_broadcast([128, CB, D]), ALU.mult))

            def sum_up(c):
                dve.wait_ge(pool_n, at("pool", "sage", c, "s1"))
                dve.wait_ge(pe_n, at("pe", "sage", c, "tb", back=1))
                dve.wait_ge(pool_n, at("pool", "sage", c, "c0", back=1))
                step("sage", "s2", dve.tensor_tensor(summ, pair[:, 0, :, :], pair[:, 1, :, :], ALU.add))
                after("sage", c, "s2")
                step("sage", "cn", dve.tensor_scalar(rcnt[:, 0, :], summ[:, :, 2 * D], 1.0, None, ALU.max))
                after("sage", c, "cn")
                step("sage", "rc", dve.reciprocal(rcnt[:, 1, :], rcnt[:, 0, :]))

            def layer2_parts(c):
                dve.wait_ge(pe_n, at("pe", "sage", c, "mq"))
                dve.wait_ge(stored, stored_at("sage", c, 1, back=1))
                step("sage", "tq", dve.tensor_tensor(m_bb, psv(ps_m), row("b_m1"), ALU.add))

            def sage_out(c):
                dve.wait_ge(pe_n, at("pe", "sage", c, "mz"))
                step("sage", "z0", dve.tensor_tensor(m_cb, side[:, blk(c), :], psv(ps_t), ALU.add))
                after("sage", c, "z0")
                dve.wait_ge(act_n, at("act", "sage", c, "m.out", back=1))
                step("sage", "xn", dve.tensor_tensor(ta[:, :, :], m_cb, x[:, blk(c), :], ALU.add))
                ln("sage", c, "m", ta, "xn")

            over_chunks(dve, "dve", ph, near_and_far, sum_up, sage_out, layer2_parts)

            loads.n += ITERS
            gb_turns = ITERS + 1
            with dve.If(unfitting == 0):
                window_pass("mlp", 1, ahead=one_hot_T_half, this=mix_half)
            with dve.Else():
                one_hot_pass((diff[:, 0, 0, :], gb_turns))
            ph = "mlp"

            def mlp_affine(c):
                dve.wait_ge(act_n, at("act", "mlp", c, "n.out"))
                step("mlp", "w", dve.tensor_tensor(hh[:, :, :], hh[:, :, :], row("gamma"), ALU.mult))
                after("mlp", c, "w")
                step("mlp", "b", dve.tensor_tensor(hh[:, :, :], hh[:, :, :], row("beta"), ALU.add))

            def mlp_onto_x(c):
                after("mlp", c, "b")
                step("mlp", "hb", dve.tensor_tensor(m_cb, hh[:, :, :], keep[:, blk(c), :], ALU.add))
                after("mlp", c, "hb")
                dve.wait_ge(act_n, at("act", "mlp", c, "m.out", back=1))
                step("mlp", "xn", dve.tensor_tensor(tb[:, :, :], m_cb, x[:, blk(c), :], ALU.add))

            def mlp_rows(c):
                dve.wait_ge(pe_n, at("pe", "mlp", c, "my"))
                dve.wait_ge(act_n, at("act", "mlp", c, "n.out", back=1))
                step("mlp", "y", dve.tensor_tensor(o[:, :, :], row("b_u2"), psv(ps_o), ALU.add))

            def mlp_hidden(c):
                dve.wait_ge(pe_n, at("pe", "mlp", c, "mu"))
                dve.wait_ge(act_n, at("act", "mlp", c, "ur", back=1))
                step("mlp", "ua", dve.tensor_tensor(m_a, side_fm[:, nodes(c)], ps_m, ALU.add))

            norms = in_turn(ln_steps(ph, "n", o, "y"), ln_steps(ph, "m", tb, "xn"))
            over_chunks(dve, "dve", ph, mlp_affine, mlp_rows, mlp_onto_x, *norms[:6], mlp_hidden, *norms[6:])

            with dve.If(unfitting == 0):
                window_pass("rel", 1, ahead=types_half, with_hot=narrow_half)
            with dve.Else():
                one_hot_pass((zf[:, :], gb_turns + TILES))
            ph = "rel"

            def outputs(c):
                dve.wait_ge(pe_n, at("pe", ph, c, "mn"))
                step(ph, "c0", dve.tensor_tensor(o[:, :, :], psv(ps_o), per_node(norm, c), ALU.mult))
                after(ph, c, "c0")
                step(ph, "c1", dve.tensor_tensor(ta[:, :, :], o[:, :, :], side[:, blk(c), :], ALU.add))
                after(ph, c, "c1")
                dve.wait_ge(stored, stored_at(ph, c, back=1))
                step(ph, "c2", dve.scalar_tensor_tensor(out=tb[:, :, :], in0=ta[:, :, :], scalar=0.0,
                                                        in1=x[:, blk(c), :], op0=ALU.max, op1=ALU.add))

            over_chunks(dve, "dve", ph, outputs)

        @block.scalar
        def _(act):
            for q in (abs_s, summed, relu, full):
                act.sem_inc(q, 1)
            act.sem_inc(act_n, STEP0)
            for n in ("relu_made", "own_out", "cnt_out"):
                act.sem_inc(half_sem[n], 4)

            def step(ph, name, ins):
                tick("act", ph, name, ins)

            def copy(ph, name, dst, src):
                step(ph, name, act.activation(dst, src, ACT.Copy))

            def root(ph, c, t):
                act.wait_ge(dve_n, at("dve", ph, c, t + ".ve"))
                step(ph, t + ".sd", act.activation(lns[t][:, 1, :], lns[t][:, 0, :], ACT.Sqrt))

            def normed(ph, c, t, src, func, again=None, dst=hh):
                act.wait_ge(dve_n, at("dve", ph, c, t + ".co"))
                if again is not None:
                    again(c)
                for k in range(CB):
                    last = act.activation(dst[:, k, :], src[:, k, :], func, scale=lns[t][:, 4, k:k + 1],
                                          bias=lns[t][:, 5, k:k + 1])
                step(ph, t + ".out", last)

            def ln(ph, c, t, src, func, again=None):
                root(ph, c, t)
                normed(ph, c, t, src, func, again)

            def turned(ph, c, name, pe_name, free):
                act.wait_ge(pe_n, at("pe", ph, c, pe_name))
                act.wait_ge(pe_n, free)
                copy(ph, name, hT[:, :], ps_h)

            def new_x(ph, c, rows):
                act.wait_ge(dve_n, at("dve", ph, c, "xn"))
                copy(ph, "xw", x[:, blk(c), :], rows[:, :, :])

            def keep_rows(ph, c, rows):
                copy(ph, "kp", keep[:, blk(c), :], rows[:, :, :])

            def table_out(ph, c):
                act.wait_ge(pe_n, at("pe", ph, c, "mm"))
                act.wait_ge(stored, stored_at(ph, c, back=1))
                copy(ph, "tab", tb[:, :, :].rearrange("p b f -> p (b f)"), ps_o)

            def start_norm(c):
                act.wait_ge(act_n, at("act", "start", c, "m.out", back=1))
                copy("start", "xc", ta[:, :, :], x[:, blk(c), :])
                ln("start", c, "m", ta, ACT.Relu, lambda c: act.wait_ge(pe_n, at("pe", "start", c, "tr", back=1)))

            def first_table(c):
                turned("start", c, "hT", "tr", at("pe", "start", c, "mm", back=1))
                act.wait_ge(pe_n, at("pe", "start", c, "mm"))
                copy("start", "tab", side_fm[:, nodes(c)], ps_o)

            act.wait_ge(in_x, 16)
            over_chunks(act, "act", "start", start_norm, first_table)
            act.wait_ge(dve_c, DEG_CHAIN + 1)
            act.activation(small[:, 1, :], small[:, 0, :], ACT.Sqrt).then_inc(act_c, 1)

            relus, mixes, fulls, zs = Count(), Count(), Count(start=0), Count()

            def acc_cleared(p):
                if p == "gcn0":
                    act.wait_ge(acc_clear, 1)
                else:
                    act.wait_ge(pool_n, end("pool", BEFORE[p]))

            def sums_out(k):
                act.wait_ge(ps_full, fulls.next())
                act.activation(acc[:, k, 0:NP], ps[:, 0:NP], ACT.Copy).then_inc(full, 1)

            unfitting = is_general(act)

            def relu_halves(p):
                def body(i, turn, last):
                    for hf in range(2):
                        if p == "mlp":
                            act.wait_ge(half_sem["mix_made"], half("mix_made", p, i, hf))
                            message = diff[:, hf, :, :]
                        else:
                            act.wait_ge(half_sem["z_made"], half("z_made", p, i, hf))
                            message = ps_zh[hf].rearrange("p (j f) -> p j f", j=H)
                        act.wait_ge(half_sem["seg_made"], half("seg_made", p, i, hf, back=2))
                        act.activation(zr[:, hf, :, :], message, ACT.Relu).then_inc(half_sem["relu_made"], 1)
                iterations(act, body)

            def sums_are_in(p, increments):
                act.wait_ge(half_sem["win_added"], half("win_added", p, ITERS - 1, 1))
                act.sem_inc(full, increments)

            for layer in range(LAYERS):
                ph = f"gcn{layer}"
                with act.If(unfitting == 0):
                    relu_halves(ph)
                    sums_are_in(ph, 2)
                with act.Else():
                    acc_cleared(ph)
                    sums_out(0)
                    with act.Fori(0, TILES) as t:
                        relus.enter(t, 1)
                        zs.enter(t, 1)
                        act.wait_ge(seg, t + (1 + TILES * (2 * layer + 1)))
                        act.wait_ge(zmm, zs.next())
                        act.activation(zf[:, :], ps_z, ACT.Relu).then_inc(relu, 1)
                        relus.next()
                    relus.leave(TILES)
                    zs.leave(TILES)
                    sums_out(1)

                def h_kept(c):
                    act.wait_ge(dve_n, at("dve", ph, c, "hn"))
                    keep_rows(ph, c, tb)

                def sums_of(c):
                    act.wait_ge(full, 1 + fulls.n)
                    act.wait_ge(pe_n, at("pe", ph, c, "ta", back=1))
                    copy(ph, "sa", s_a[:, :], acc[:, 0, nodes(c)])
                    act.wait_ge(pe_n, at("pe", ph, c, "mb", back=1))
                    copy(ph, "sb", s_b[:, :], acc[:, 1, nodes(c)])

                if layer < LAYERS - 1:
                    over_chunks(act, "act", ph, sums_of,
                                lambda c: root(ph, c, "n"),
                                lambda c: turned(ph, c, "hT", "tr", at("pe", ph, c, "mm", back=1)),
                                lambda c: normed(ph, c, "n", ta, ACT.Identity,
                                             lambda c: act.wait_ge(dve_n, at("dve", ph, c, "hd", back=1))),
                                lambda c: table_out(ph, c))
                else:
                    over_chunks(act, "act", ph, sums_of,
                                lambda c: turned(ph, c, "hT", "tr", at("pe", ph, c, "mz", back=1)),
                                lambda c: root(ph, c, "n"), lambda c: root(ph, c, "m"), lambda c: new_x(ph, c, ta),
                                lambda c: normed(ph, c, "n", z_rows, ACT.Identity,
                                                 lambda c: act.wait_ge(dve_n, at("dve", ph, c, "xn", back=1))),
                                lambda c: normed(ph, c, "m", ta, ACT.Relu,
                                                 lambda c: act.wait_ge(pe_n, at("pe", ph, c, "tr", back=1)), dst=o),
                                h_kept)

            def edge_half(i, hf, prior, windows):
                r = slice(hf * H, hf * H + H)
                if windows:
                    act.wait_ge(half_sem["z_made"], half("z_made", "sage", i, hf))
                    if prior:
                        act.wait_ge(mrg, i * 2 + hf)
                    act.activation(msg[:, r, 0:D], ps_zh[hf].rearrange("p (j f) -> p j f", j=H), ACT.Copy)\
                       .then_inc(half_sem["own_out"], 1)
                act.wait_ge(diff_s, i * 2 + hf + 4)
                act.sem_inc(passed, 1)
                act.activation(msg[:, r, D:2 * D], diff[:, hf, :, :], ACT.Abs).then_inc(abs_s, 1)
                act.wait_ge(mrg, i * 2 + hf + 2)
                for j in range(H if prior else 0):
                    act.wait_ge(added[j], i * 32 + 16 * (hf - 1))
                at_ps = 0 if windows else 2048 * hf
                act.activation(sums[:, r, :], ps[:, at_ps:at_ps + 2048].rearrange("p (j f) -> p j f", j=H)[:, :, 0:MS],
                               ACT.Copy).then_inc(summed, 1)

            def sage_pass(windows):
                edge_half(0, 0, False, windows)
                edge_half(0, 1, False, windows)
                with act.Fori(1, ITERS) as i:
                    edge_half(i, 0, True, windows)
                    edge_half(i, 1, True, windows)

            with act.If(unfitting == 0):
                sage_pass(True)
            with act.Else():
                sage_pass(False)

            ph = "sage"

            def sage_table(c):
                act.wait_ge(pe_n, at("pe", "sage", c, "mp"))
                act.wait_ge(stored, stored_at("sage", c, 0, back=1))
                copy("sage", "tp", tb[:, :, :].rearrange("p b f -> p (b f)"), ps_h)

            def sage_side(c):
                act.wait_ge(pe_n, at("pe", "sage", c, "mu"))
                step("sage", "us", act.activation(side_fm[:, nodes(c)], ps_t, ACT.Identity, bias=bu1_col[:, 0:1]))

            def sage_sums(c):
                act.wait_ge(pe_n, at("pe", "sage", c, "ta"))
                act.wait_ge(pe_n, at("pe", "sage", c, "me", back=1))
                copy("sage", "sa", s_a[:, :], ps_t)
                act.wait_ge(pe_n, at("pe", "sage", c, "tb"))
                copy("sage", "sb", s_b[:, :], ps_m)

            def sage_root(c):
                new_x("sage", c, ta)
                root("sage", c, "m")

            def sage_applied(c):
                act.wait_ge(act_n, at("act", "sage", c, "kp", back=1))
                normed("sage", c, "m", ta, ACT.Relu, lambda c: act.wait_ge(pe_n, at("pe", "sage", c, "tr2", back=1)))
                act.wait_ge(act_n, at("act", "sage", c, "m.out"))
                keep_rows("sage", c, hh)

            over_chunks(act, "act", ph,
                        lambda c: turned("sage", c, "hT", "tr", at("pe", "sage", c, "mu", back=2)), sage_sums,
                        lambda c: turned("sage", c, "hT2", "tr2", at("pe", "sage", c, "mz", back=-1)),
                        sage_root, sage_table, sage_applied, sage_side)

            with act.If(unfitting == 0):
                relu_halves("mlp")
                sums_are_in("mlp", 1)
            with act.Else():
                acc_cleared("mlp")
                with act.Fori(0, TILES) as t:
                    relus.enter(t, 1)
                    mixes.enter(t, 1)
                    act.wait_ge(msg_s, mixes.next())
                    act.wait_ge(seg, t + (1 + TILES * 2 * LAYERS))
                    act.activation(zf[:, :], diff[:, 0, 0, :], ACT.Relu).then_inc(relu, 1)
                    relus.next()
                relus.leave(TILES)
                mixes.leave(TILES)
                sums_out(0)
            ph = "mlp"

            def mlp_agg(c):
                act.wait_ge(pe_n, at("pe", "mlp", c, "ag"))
                act.wait_ge(pe_n, at("pe", "mlp", c, "mu", back=1))
                copy("mlp", "sa", s_a[:, :], ps_t)

            def mlp_relu(c):
                act.wait_ge(dve_n, at("dve", "mlp", c, "ua"))
                act.wait_ge(pe_n, at("pe", "mlp", c, "my", back=1))
                step("mlp", "ur", act.activation(s_b[:, :], m_a, ACT.Relu))

            def mlp_side(c):
                act.wait_ge(pe_n, at("pe", "mlp", c, "ml"))
                act.wait_ge(dve_n, at("dve", "mlp", c, "ua"))
                step("mlp", "zs", act.activation(side_fm[:, nodes(c)], ps_m, ACT.Copy))

            def m_b_free(c):
                act.wait_ge(stored, stored_at("mlp", c, back=1))
                act.wait_ge(pe_n, at("pe", "mlp", c, "tr", back=1))

            over_chunks(act, "act", ph, mlp_agg,
                        lambda c: turned("mlp", c, "hT", "tr", at("pe", "mlp", c, "ml", back=1)),
                        lambda c: new_x("mlp", c, tb), lambda c: root("mlp", c, "n"),
                        lambda c: root("mlp", c, "m"), mlp_relu,
                        lambda c: normed("mlp", c, "n", o, ACT.Identity,
                                         lambda c: act.wait_ge(dve_n, at("dve", "mlp", c, "hb", back=1))),
                        lambda c: normed("mlp", c, "m", tb, ACT.Relu, m_b_free, dst=m_bb), mlp_side)

            def counts_out(i, turn, last):
                for hf in range(2):
                    act.wait_ge(half_sem["cnt_made"], half("cnt_made", "rel", i, hf))
                    act.wait_ge(half_sem["seg_made"], half("seg_made", "rel", i, hf, back=2))
                    act.activation(cnts[:, hf, :, :], ps_c[hf].rearrange("p (b k) -> p b k", b=TB), ACT.Copy)\
                       .then_inc(half_sem["cnt_out"], 1)

            with act.If(unfitting == 0):
                iterations(act, counts_out)
                sums_are_in("rel", 1)
            with act.Else():
                acc_cleared("rel")
                sums_out(0)
            ph = "rel"

            def rel_sums(c):
                act.wait_ge(full, 1 + fulls.n)
                act.wait_ge(pe_n, at("pe", "rel", c, "mn", back=1))
                copy("rel", "sa", s_a[:, :], acc[:, 0, nodes(c)])

            over_chunks(act, "act", ph, rel_sums)

        @block.tensor
        def _(pe):
            for q in (seg, zmm, mrg):
                pe.sem_inc(q, 1)
            pe.sem_inc(deg_mm, 2)
            pe.sem_inc(pe_n, STEP0)
            for n in ("z_made", "seg_made", "cnt_made"):
                pe.sem_inc(half_sem[n], 4)

            def step(ph, name, ins):
                tick("pe", ph, name, ins)

            def open_sums(banks):
                for k, width in banks:
                    pe.matmul(ps[:, k:k + width], zeros[:, 0:128], zeros[:, 0:width], start=True, stop=False,
                              skip_group_check=True)

            def close_sums(banks):
                for k, width in banks:
                    last = pe.matmul(ps[:, k:k + width], zeros[:, 0:128], zeros[:, 0:width], start=False, stop=True,
                                     skip_group_check=True)
                return last

            pe.wait_ge(consts, 9)
            pe.wait_ge(in_w, 80)
            pe.wait_ge(dve_c, 5)
            hots, segs, relus, mixes, loads, zin = Count(), Count(), Count(), Count(), Count(by=16, start=0), Count(by=16, start=0)
            hots.n += 4 * ITERS

            def turn(ph, c, name, dst, src):
                for k in range(CB):
                    last = pe.transpose(dst[:, k * 128:k * 128 + 128], src(k), ident[:, :])
                step(ph, name, last)

            def by_rows(ph, name, dst, parts):
                for k in range(CB):
                    for n, (lhs, w) in enumerate(parts):
                        last = pe.matmul(dst[:, k * 128:k * 128 + 128], lhs[:, k * 128:k * 128 + 128], W[w],
                                         start=(n == 0), stop=(n == len(parts) - 1))
                step(ph, name, last)

            def hh_blk(k):
                return hh[:, k, :]

            def o_blk(k):
                return o[:, k, :]

            def m_b_blk(k):
                return m_bb[:, k, :]

            def add_tile(message):
                for k, width in BANKS:
                    last = pe.matmul(ps[:, k:k + width], message, big[:, k:k + width], start=False, stop=False,
                                     skip_group_check=True)
                last.then_inc(seg, 1)

            def sum_pass(message, came):
                open_sums(BANKS)
                with pe.Fori(0, TILES) as t:
                    hots.enter(t, 1)
                    pe.wait_ge(hot, hots.next())
                    came(t)
                    add_tile(message)
                hots.leave(TILES)
                close_sums(BANKS).then_inc(ps_full, 1)

            def next_table(ph, c, mm_weight):
                pe.wait_ge(dve_n, at("dve", ph, c, "hd"))
                pe.wait_ge(act_n, at("act", ph, c, "hT", back=1))
                turn(ph, c, "tr", ps_h, o_blk)
                pe.wait_ge(act_n, at("act", ph, c, "hT"))
                pe.wait_ge(act_n, at("act", ph, c, "tab", back=1))
                by_rows(ph, "mm", ps_o, [(hT, mm_weight)])

            def first_table(c):
                pe.wait_ge(act_n, at("act", "start", c, "m.out"))
                pe.wait_ge(act_n, at("act", "start", c, "hT", back=1))
                turn("start", c, "tr", ps_h, hh_blk)
                pe.wait_ge(act_n, at("act", "start", c, "hT"))
                pe.wait_ge(act_n, at("act", "start", c, "tab", back=1))
                by_rows("start", "mm", ps_o, [(hT, "lin0")])
                if not isinstance(c, int):
                    degree_share(pe, c + 1, degree_iteration)

            def degree_iteration(i):
                for hf in range(2):
                    pe.wait_ge(hot, i * 4 + 2 * hf + 3)
                    for j in range(hf * H, hf * H + H):
                        last = pe.matmul(ps[:, 0:NB], oh_lo[:, j, :], oh_hi[:, j, :], start=False, stop=False,
                                         skip_group_check=True)
                    last.then_inc(deg_mm, 1)

            open_sums([(0, NB)])
            degree_share(pe, 0, degree_iteration)
            over_chunks(pe, "pe", "start", first_table)
            degree_rest(pe, degree_iteration)
            close_sums([(0, NB)]).then_inc(deg_mm, 1)

            unfitting = is_general(pe)

            def mlp_half(p, i, hf):
                pe.wait_ge(ea_h[hf], dma_half(p, GCN, i))
                pe.wait_ge(half_sem["relu_made"], half("relu_made", p, i, hf, back=2))
                for j in range(H):
                    last = pe.matmul(ps_zh[hf][:, 128 * j:128 * j + 128], ea_r[:, hf, 128 * j:128 * j + 128],
                                     w1[:, GCN.index(p), :], start=True, stop=True)
                last.then_inc(half_sem["z_made"], 1)

            def own_half(p, i, hf):
                pe.wait_ge(win_in[hf], dma_half(p, ["sage", "mlp"], i))
                pe.wait_ge(half_sem["ohT_made"], half("ohT_made", p, i, hf))
                if p == "sage":
                    pe.wait_ge(half_sem["own_out"], half("own_out", p, i, hf, back=2))
                    pe.wait_ge(diff_s, i * 2 + hf + 2)
                else:
                    pe.wait_ge(half_sem["mix_made"], half("mix_made", p, i, hf, back=2))
                for j in range(H):
                    last = pe.matmul(ps_zh[hf][:, 128 * j:128 * j + 128], ohT[:, hf, 128 * j:128 * j + 128],
                                     win[:, hf, :], start=True, stop=True)
                last.then_inc(half_sem["z_made"], 1)

            def seg_half(p, i, turn, hf):
                pe.wait_ge(half_sem["win_added"], half("win_added", p, i, hf, back=2))
                pe.wait_ge(half_sem["oh_made"], half("oh_made", p, i, hf))
                if p != "mlp":
                    for j in range(H):
                        pe.wait_ge(fa_in[slot(turn, hf, j)], turn_done(p, turn))
                        last = pe.matmul(ps_w[hf][:, 0, :], g_a[:, slot(turn, hf, j), :], oh[:, hf, j, :],
                                         start=(j == 0), stop=(j == H - 1 and p != "rel"))
                if p == "rel":
                    pe.wait_ge(half_sem["cnt_out"], half("cnt_out", p, i, hf))
                    for b in range(TB):
                        last = pe.matmul(ps_w[hf][:, 0, :], rel_sb[:, b, :], cnts[:, hf, b, :], start=False,
                                         stop=(b == TB - 1))
                else:
                    pe.wait_ge(half_sem["relu_made"], half("relu_made", p, i, hf))
                    for j in range(H):
                        last = pe.matmul(ps_w[hf][:, 0 if p == "mlp" else 1, :], zr[:, hf, j, :], oh[:, hf, j, :],
                                         start=(j == 0), stop=(j == H - 1))
                last.then_inc(half_sem["seg_made"], 1)

            def count_half(p, i, hf):
                pe.wait_ge(half_sem["typ_made"], half("typ_made", p, i, hf))
                pe.wait_ge(half_sem["cnt_out"], half("cnt_out", p, i, hf, back=2))
                for b in range(TB):
                    for j in range(H):
                        last = pe.matmul(ps_c[hf][:, 128 * b:128 * b + 128], oh_typ[:, hf, j, TR * b:TR * b + TR],
                                         oh16[:, hf, j, :], start=(j == 0), stop=(j == H - 1))
                last.then_inc(half_sem["cnt_made"], 1)

            def window_pass(p, ahead, then):
                ahead(p, 0, 0)

                def body(i, turn, last):
                    for hf in range(2):
                        if p == "rel":
                            then(p, i, turn, hf)
                        if not (last and hf):
                            ahead(p, *after_half(i, hf))
                        if p != "rel":
                            then(p, i, turn, hf)
                iterations(pe, body)

            full_n = 1
            for layer in range(LAYERS):
                pe.wait_ge(act_n, end("act", BEFORE[f"gcn{layer}"]))
                pe.wait_ge(dve_n, end("dve", BEFORE[f"gcn{layer}"]))
                if layer:
                    pe.wait_ge(full, full_n)

                def gathered(t):
                    loads.enter(t, 1)
                    pe.wait_ge(ga_in[0], loads.next())

                def through_mlp(t):
                    relus.enter(t, 1)
                    zin.enter(t, 1)
                    pe.wait_ge(ea_in_s, zin.next())
                    pe.matmul(ps_z, ea_t[:, :], w1[:, layer, :], start=True, stop=True).then_inc(zmm, 1)
                    pe.wait_ge(relu, relus.next())

                with pe.If(unfitting == 0):
                    window_pass(f"gcn{layer}", mlp_half, seg_half)
                with pe.Else():
                    sum_pass(g_a[:, 0, :], gathered)
                    loads.leave(TILES)
                    pe.wait_ge(full, full_n + 1)
                    sum_pass(zf[:, :], through_mlp)
                    relus.leave(TILES)
                    zin.leave(TILES)
                full_n += 2
                pe.wait_ge(full, full_n)
                ph = f"gcn{layer}"

                def gcn_sums(c):
                    pe.wait_ge(act_n, at("act", ph, c, "sa"))
                    pe.wait_ge(dve_n, at("dve", ph, c, "z0", back=1))
                    turn(ph, c, "ta", ps_t, lambda k: s_a[:, k * 128:k * 128 + 128])
                    pe.wait_ge(act_n, at("act", ph, c, "sb"))
                    pe.wait_ge(dve_n, at("dve", ph, c, "z1", back=1))
                    by_rows(ph, "mb", ps_m, [(s_b, f"ew{layer}")])

                def layer1_tables(c):
                    pe.wait_ge(act_n, at("act", ph, c, "m.out"))
                    pe.wait_ge(dve_n, at("dve", ph, c, "zs", back=1))
                    turn(ph, c, "tr", ps_h, o_blk)
                    pe.wait_ge(act_n, at("act", ph, c, "hT"))
                    pe.wait_ge(dve_n, at("dve", ph, c, "hn", back=1))
                    by_rows(ph, "mm", ps_o, [(hT, "neigh")])
                    by_rows(ph, "mz", ps_h, [(hT, "l1_a")])

                if layer < LAYERS - 1:
                    over_chunks(pe, "pe", ph, gcn_sums, lambda c: next_table(ph, c, f"lin{layer + 1}"))
                else:
                    over_chunks(pe, "pe", ph, gcn_sums, layer1_tables)

            pe.wait_ge(act_n, end("act", "gcn2"))
            pe.wait_ge(dve_n, end("dve", "gcn2"))

            def edge_half(i, hf, prior, windows=False):
                if windows:
                    pe.wait_ge(summed, i * 2 + (hf + 1))
                    pe.wait_ge(half_sem["own_out"], half("own_out", "sage", i, hf))
                elif prior:
                    pe.wait_ge(summed, i * 2 + hf)
                pe.wait_ge(eq_s, i * 2 + hf + 3)
                pe.wait_ge(abs_s, i * 2 + hf + 2)
                pe.sem_inc(passed, 1)
                for j in range(H):
                    k = (0 if windows else 2048 * hf) + 512 * j
                    last = pe.matmul(ps[:, k:k + MS], eq[:, hf, j, :], msg[:, hf * H + j, :], start=True, stop=True)
                last.then_inc(mrg, 1)

            with pe.If(unfitting == 0):
                window_pass("sage", own_half, lambda p, i, turn, hf: edge_half(i, hf, True, True))
            with pe.Else():
                edge_half(0, 0, False)
                edge_half(0, 1, False)
                with pe.Fori(1, ITERS) as i:
                    edge_half(i, 0, True)
                    edge_half(i, 1, True)

            ph = "sage"
            pe.wait_ge(summed, ITERS * 2 + 1)

            def far_sums(c):
                pe.wait_ge(act_n, at("act", "sage", c, "sb"))
                pe.wait_ge(dve_n, at("dve", "sage", c, "c1", back=1))
                by_rows("sage", "me", ps_o, [(s_a, "edge_a"), (s_b, "edge_b")])

            def sage_lin(c):
                pe.wait_ge(dve_n, at("dve", "sage", c, "c3"))
                pe.wait_ge(act_n, at("act", "sage", c, "tp", back=2))
                turn("sage", c, "tr", ps_h, o_blk)
                pe.wait_ge(act_n, at("act", "sage", c, "hT"))
                pe.wait_ge(act_n, at("act", "sage", c, "us", back=2))
                by_rows("sage", "mz", ps_t, [(hT, "l1_b")])

            def layer2_turned(c):
                pe.wait_ge(act_n, at("act", "sage", c, "m.out"))
                pe.wait_ge(act_n, at("act", "sage", c, "hT", back=-1))
                pe.wait_ge(act_n, at("act", "sage", c, "tp", back=1))
                turn("sage", c, "tr2", ps_h, hh_blk)

            def layer2_tables(c):
                pe.wait_ge(act_n, at("act", "sage", c, "hT2"))
                by_rows("sage", "mp", ps_h, [(hT, "m1_a")])
                pe.wait_ge(act_n, at("act", "sage", c, "sb", back=-2))
                pe.wait_ge(dve_n, at("dve", "sage", c, "tq", back=1))
                by_rows("sage", "mq", ps_m, [(hT, "m1_b")])
                pe.wait_ge(dve_n, at("dve", "sage", c, "z0", back=-1))
                for lo, hi in ((0, 512), (512, CW)):
                    last = pe.matmul(ps_t[:, lo:hi], W["u1_a"], hT[:, lo:hi], start=True, stop=True)
                tick("pe", "sage", "mu", last)

            def sums_turned(c):
                pe.wait_ge(dve_n, at("dve", "sage", c, "s2"))
                pe.wait_ge(act_n, at("act", "sage", c, "us", back=3))
                pe.wait_ge(dve_n, at("dve", "sage", c, "z0", back=1))
                turn("sage", c, "ta", ps_t, lambda k: summ[:, k, 0:D])
                pe.wait_ge(dve_n, at("dve", "sage", c, "tq", back=3))
                turn("sage", c, "tb", ps_m, lambda k: summ[:, k, D:2 * D])

            over_chunks(pe, "pe", ph, sage_lin, sums_turned, layer2_turned, far_sums, layer2_tables)

            pe.wait_ge(act_n, end("act", "sage"))
            pe.wait_ge(dve_n, end("dve", "sage"))

            def through_relu(t):
                relus.enter(t, 1)
                pe.wait_ge(relu, relus.next())

            with pe.If(unfitting == 0):
                window_pass("mlp", own_half, seg_half)
            with pe.Else():
                sum_pass(zf[:, :], through_relu)
                relus.leave(TILES)
            full_n += 1
            pe.wait_ge(full, full_n)
            pe.wait_ge(deg_back, 16)
            ph = "mlp"
            eb = rows[0:1, ROWS.index("b_m2"), :]

            def mlp_out(c):
                pe.wait_ge(act_n, at("act", "mlp", c, "ur"))
                pe.wait_ge(dve_n, at("dve", "mlp", c, "y", back=1))
                by_rows("mlp", "my", ps_o, [(s_b, "u2")])

            def mlp_agg(c):
                pe.wait_ge(act_n, at("act", "mlp", c, "sa", back=1))
                for lo, hi in ((0, 512), (512, CW)):
                    pe.matmul(ps_t[:, lo:hi], W["m2"], acc[:, 0, bass.ds(c * CW + lo, hi - lo)], start=True, stop=False)
                    last = pe.matmul(ps_t[:, lo:hi], eb, deg_row[0:1, bass.ds(c * CW + lo, hi - lo)], start=False, stop=True)
                tick("pe", "mlp", "ag", last)

            def mlp_update(c):
                pe.wait_ge(act_n, at("act", "mlp", c, "sa"))
                pe.wait_ge(act_n, at("act", "mlp", c, "zs", back=4))
                pe.wait_ge(dve_n, at("dve", "mlp", c, "ua", back=1))
                for lo, hi in ((0, 512), (512, CW)):
                    last = pe.matmul(ps_m[:, lo:hi], W["u1_b"], s_a[:, lo:hi], start=True, stop=True)
                tick("pe", "mlp", "mu", last)

            def mlp_loop(c):
                pe.wait_ge(act_n, at("act", "mlp", c, "m.out"))
                pe.wait_ge(act_n, at("act", "mlp", c, "hT", back=1))
                turn("mlp", c, "tr", ps_h, m_b_blk)
                pe.wait_ge(act_n, at("act", "mlp", c, "hT"))
                pe.wait_ge(dve_n, at("dve", "mlp", c, "ua", back=-3))
                by_rows("mlp", "ml", ps_m, [(hT, "loop")])

            over_chunks(pe, "pe", ph, mlp_agg, mlp_out, mlp_update, mlp_loop)

            pe.wait_ge(act_n, end("act", "mlp"))
            pe.wait_ge(dve_n, end("dve", "mlp"))

            def mixed(t):
                mixes.enter(t, 1)
                pe.wait_ge(msg_s, mixes.next())

            mixes.n += TILES
            with pe.If(unfitting == 0):
                window_pass("rel", count_half, seg_half)
            with pe.Else():
                sum_pass(zf[:, :], mixed)
                mixes.leave(TILES)
            full_n += 1
            pe.wait_ge(full, full_n)
            ph = "rel"

            def neighbors(c):
                pe.wait_ge(act_n, at("act", ph, c, "sa"))
                pe.wait_ge(dve_n, at("dve", ph, c, "c0", back=1))
                by_rows(ph, "mn", ps_o, [(s_a, "neighbor")])

            over_chunks(pe, "pe", ph, neighbors)


def kernel(**inputs):
    import concourse.bacc as bacc
    from concourse.bass_utils import run_bass_kernel_spmd

    g = {k: np.asarray(v) for k, v in inputs.items()}
    f32 = np.float32

    def edges(a):
        return np.concatenate([a, np.full(TILES * 128 - E, N, a.dtype)])

    x = np.concatenate([g["x"], np.zeros((NP - N, D), f32)]).reshape(NB, 128, D).transpose(1, 0, 2)
    src, dst = edges(g["src"]), edges(g["dst"])
    typ = np.concatenate([g["edge_type_500"], np.zeros(TILES * 128 - E, np.int32)])
    ea = np.concatenate([g["edge_attr_16"], np.zeros((TILES * 128 - E, DE), f32)]).T
    ea = np.concatenate([ea, np.ones((1, TILES * 128), f32)])
    n1, n2 = g["L1_gnn_W_edge"], g["L1_gnn_W_lin"]
    mats = {
        "lin0": g["L0_gnn_lin_w"][0], "lin1": g["L0_gnn_lin_w"][1], "lin2": g["L0_gnn_lin_w"][2],
        "ew0": g["L0_gnn_edge_w2"][0], "ew1": g["L0_gnn_edge_w2"][1], "ew2": g["L0_gnn_edge_w2"][2],
        "neigh": g["L1_gnn_W_neigh"].T, "edge_a": n1[:, :D].T, "edge_b": n1[:, D:].T,
        "l1_a": n2[:, :D].T, "l1_b": n2[:, D:].T,
        "m1_a": g["L2_gnn_w_m1"][:D], "m1_b": g["L2_gnn_w_m1"][D:], "m2": g["L2_gnn_w_m2"],
        "u1_a": g["L2_gnn_w_u1"][:D], "u1_b": g["L2_gnn_w_u1"][D:], "u2": g["L2_gnn_w_u2"],
        "neighbor": g["L3_gnn_W_neighbor"], "loop": g["L3_gnn_loop_weight"],
    }
    vecs = {"b_neigh": g["L1_gnn_b_neigh"], "b_edge": g["L1_gnn_b_edge"], "b_lin": g["L1_gnn_b_lin"],
            "b_m1": g["L2_gnn_b_m1"], "b_m2": g["L2_gnn_b_m2"], "b_u1": g["L2_gnn_b_u1"], "b_u2": g["L2_gnn_b_u2"],
            "gamma": g["L2_gnn_gamma"], "beta": g["L2_gnn_beta"]}
    for k in range(LAYERS):
        vecs |= {f"lnw{k}": g["L0_gnn_ln_w"][k], f"lnb{k}": g["L0_gnn_ln_b"][k], f"bias{k}": g["L0_gnn_bias"][k],
                 f"eb{k}": g["L0_gnn_edge_b2"][k]}
    w1 = np.concatenate([g["L0_gnn_edge_w1"], g["L0_gnn_edge_b1"][:, None, :]], axis=1).transpose(1, 0, 2)
    arrays = {
        "x_in": x, "src_in": src.reshape(TILES, 128).T, "dst_in": dst.reshape(TILES, 128).T,
        "typ_in": typ.reshape(TILES, 128).T, "srcrow_in": src.reshape(1, -1),
        "dstrow_in": dst.reshape(1, -1), "relblk_in": g["L3_gnn_rel_emb"].reshape(TB, TR, D).transpose(1, 0, 2),
        "dstgrp_in": dst.reshape(TILES // H, H * 128), "ea_in": ea,
        "w_in": np.stack([mats[n] for n in WEIGHTS], axis=1), "w1_in": w1,
        "rows_in": np.stack([vecs[n] for n in ROWS]), "cols_in": g["L2_gnn_b_u1"].reshape(D, 1),
        "rel_in": g["L3_gnn_rel_emb"],
    }
    arrays = {k: np.ascontiguousarray(v) for k, v in arrays.items()}
    nc = bacc.Bacc("TRN2", target_bir_lowering=False, num_devices=1)
    args = {k: nc.dram_tensor(k, v.shape, mybir.dt.from_np(v.dtype), kind="ExternalInput").ap() for k, v in arrays.items()}
    out = nc.dram_tensor("out", (NP, D), F32, kind="ExternalOutput").ap()
    build(nc, **args, out=out)
    r = run_bass_kernel_spmd(nc, [arrays], core_ids=[0])
    return r.results[0]["out"][:N]
```
